# Optimizing a Trainium2 kernel written in Bass

```python
import numpy as np
import jax
import jax.numpy as jnp

def _softmax(x, axis=-1):
    return jax.nn.softmax(x, axis=axis)

def _gelu(x):
    return jax.nn.gelu(x, approximate=True)

def _silu(x):
    return jax.nn.silu(x)

def _sigmoid(x):
    return jax.nn.sigmoid(x)

def _layernorm(x, axis=-1, eps=1e-05):
    m = jnp.mean(x, axis=axis, keepdims=True)
    v = jnp.var(x, axis=axis, keepdims=True)
    return (x - m) / jnp.sqrt(v + eps)

def _scatter_add(tgt, idx, src, axis=0):
    return tgt.at[idx].add(src)

def _segment_sum(src, seg, n):
    return jax.ops.segment_sum(src, seg, n)
kernel_name = 'mk_gnn_resnorm_d2_gnn_r32_fb8286'

def setup_inputs(seed: int=0):
    np.random.seed(seed)
    _w = jnp.asarray

    def _rec_inputs():
        import jax
        import jax.numpy as jnp
        _gk = jax.random.key(seed)
        x = -0.0007083 + 1.001 * jax.random.normal(jax.random.fold_in(_gk, 1), (50000, 48), jnp.float32)
        src = jax.random.randint(jax.random.fold_in(_gk, 2), (50000,), 0, 50000, jnp.int32)
        dst = jnp.minimum((50000 * jax.random.uniform(jax.random.fold_in(_gk, 3), (50000,)) ** 2.0).astype(jnp.int32), 49999)
        _o = jnp.argsort(dst, stable=True)
        src = src[_o]
        dst = dst[_o]
        edge_attr_40 = jax.random.uniform(jax.random.fold_in(_gk, 12), (50000, 40), jnp.float32, 0.0, 1)
        edge_weight = jax.random.uniform(jax.random.fold_in(_gk, 14), (50000,), jnp.float32, 0.0, 7.99999)
        node_type_119 = jax.random.randint(jax.random.fold_in(_gk, 15), (50000,), 0, 119, jnp.int32)
        node_vec = jax.random.uniform(jax.random.fold_in(_gk, 16), (50000,), jnp.float32, 0.0, 3.99996)
        return (x, src, dst, edge_attr_40, edge_weight, node_type_119, node_vec)
    x, src, dst, edge_attr_40, edge_weight, node_type_119, node_vec = _rec_inputs()

    def _L0_gnn_setup():
        import jax, jax.numpy as jnp
        import numpy as np
        N = 50000
        E = 37500
        H = 48
        RBF = 40
        L = 4
        NELEM = 119
        G = 32
        CUT = 6.0

        def _ln(x, g, b):
            m = x.mean(-1, keepdims=True)
            v = ((x - m) ** 2).mean(-1, keepdims=True)
            return (x - m) * jax.lax.rsqrt(v + 1e-05) * g + b
        key = jax.random.key(seed)
        k = jax.random.split(key, 16)
        s = 0.1
        return {'h': jax.random.normal(k[0], (N, H), jnp.float32), 'edge_index': jax.random.randint(k[1], (2, E), 0, N), 'edge_attr': jax.random.uniform(k[2], (E, RBF), dtype=jnp.float32), 'distances': jax.random.uniform(k[3], (E,), dtype=jnp.float32) * 8.0, 'atom_z': jax.random.randint(k[4], (N,), 0, NELEM), 'node_mult': jax.random.uniform(k[5], (N,), dtype=jnp.float32) * 3.0 + 1.0, 'batch': jnp.sort(jax.random.randint(k[6], (N,), 0, 64)), 'Wq': jax.random.normal(k[7], (L, H, H), jnp.float32) * s, 'gq': jnp.ones((L, H), jnp.float32), 'bq': jnp.zeros((L, H), jnp.float32), 'Wk': jax.random.normal(k[8], (L, H, H), jnp.float32) * s, 'gk': jnp.ones((L, H), jnp.float32), 'bk': jnp.zeros((L, H), jnp.float32), 'Wm': jax.random.normal(k[9], (L, H, H), jnp.float32) * s, 'Wu': jax.random.normal(k[10], (L, 2 * H, H), jnp.float32) * s, 'go': jnp.ones((L, H), jnp.float32), 'bo': jnp.zeros((L, H), jnp.float32), 'F1W': jax.random.normal(k[11], (RBF, H), jnp.float32) * s, 'F1b': jnp.zeros((H,), jnp.float32), 'F2W': jax.random.normal(k[12], (H, H), jnp.float32) * s, 'F2b': jnp.zeros((H,), jnp.float32), 'gn': jnp.ones((H,), jnp.float32), 'bn': jnp.zeros((H,), jnp.float32), 'emb': jax.random.normal(k[13], (NELEM, G), jnp.float32) * 0.01, 'adapt': jax.random.normal(k[14], (G, G), jnp.float32) * 0.01}
    _L0_gnn_all = _L0_gnn_setup()
    _L0_gnn_in = {k: v for k, v in _L0_gnn_all.items() if k in ('Wq', 'gq', 'bq', 'Wk', 'gk', 'bk', 'Wm', 'Wu', 'go', 'bo', 'F1W', 'F1b', 'F2W', 'F2b', 'gn', 'bn', 'emb', 'adapt')}
    del _L0_gnn_all

    def _L1_gnn_setup():
        import jax, jax.numpy as jnp
        import numpy as np
        N_NODES = 3125
        N_EDGES = 50000
        D_IN = 48
        D_H = 48
        D_OUT = 48

        def _graph_conv(x, src, dst, w_rel, w_root, b, num_nodes):
            agg = jax.ops.segment_sum(x[src], dst, num_segments=num_nodes)
            return agg @ w_rel + x @ w_root + b
        key = jax.random.key(seed)
        ks = jax.random.split(key, 8)
        s = 0.05
        x = jax.random.normal(ks[0], (N_NODES, D_IN), dtype=jnp.float32)
        edge_index = jax.random.randint(ks[1], (2, N_EDGES), 0, N_NODES, dtype=jnp.int64)
        w_rel1 = jax.random.normal(ks[2], (D_IN, D_H), dtype=jnp.float32) * s
        w_root1 = jax.random.normal(ks[3], (D_IN, D_H), dtype=jnp.float32) * s
        b1 = jax.random.normal(ks[4], (D_H,), dtype=jnp.float32) * s
        w_rel2 = jax.random.normal(ks[5], (D_H, D_OUT), dtype=jnp.float32) * s
        w_root2 = jax.random.normal(ks[6], (D_H, D_OUT), dtype=jnp.float32) * s
        b2 = jax.random.normal(ks[7], (D_OUT,), dtype=jnp.float32) * s
        return {'x': x, 'edge_index': edge_index, 'w_rel1': w_rel1, 'w_root1': w_root1, 'b1': b1, 'w_rel2': w_rel2, 'w_root2': w_root2, 'b2': b2}
    _L1_gnn_all = _L1_gnn_setup()
    _L1_gnn_in = {k: v for k, v in _L1_gnn_all.items() if k in ('w_rel1', 'w_root1', 'b1', 'w_rel2', 'w_root2', 'b2')}
    del _L1_gnn_all
    return {'x': x, 'src': src, 'dst': dst, 'edge_attr_40': edge_attr_40, 'edge_weight': edge_weight, 'node_type_119': node_type_119, 'node_vec': node_vec, 'L0_gnn_Wq': _L0_gnn_in['Wq'], 'L0_gnn_gq': _L0_gnn_in['gq'], 'L0_gnn_bq': _L0_gnn_in['bq'], 'L0_gnn_Wk': _L0_gnn_in['Wk'], 'L0_gnn_gk': _L0_gnn_in['gk'], 'L0_gnn_bk': _L0_gnn_in['bk'], 'L0_gnn_Wm': _L0_gnn_in['Wm'], 'L0_gnn_Wu': _L0_gnn_in['Wu'], 'L0_gnn_go': _L0_gnn_in['go'], 'L0_gnn_bo': _L0_gnn_in['bo'], 'L0_gnn_F1W': _L0_gnn_in['F1W'], 'L0_gnn_F1b': _L0_gnn_in['F1b'], 'L0_gnn_F2W': _L0_gnn_in['F2W'], 'L0_gnn_F2b': _L0_gnn_in['F2b'], 'L0_gnn_gn': _L0_gnn_in['gn'], 'L0_gnn_bn': _L0_gnn_in['bn'], 'L0_gnn_emb': _L0_gnn_in['emb'], 'L0_gnn_adapt': _L0_gnn_in['adapt'], 'L1_gnn_w_rel1': _L1_gnn_in['w_rel1'], 'L1_gnn_w_root1': _L1_gnn_in['w_root1'], 'L1_gnn_b1': _L1_gnn_in['b1'], 'L1_gnn_w_rel2': _L1_gnn_in['w_rel2'], 'L1_gnn_w_root2': _L1_gnn_in['w_root2'], 'L1_gnn_b2': _L1_gnn_in['b2']}

def reference(x, src, dst, edge_attr_40, edge_weight, node_type_119, node_vec, L0_gnn_Wq, L0_gnn_gq, L0_gnn_bq, L0_gnn_Wk, L0_gnn_gk, L0_gnn_bk, L0_gnn_Wm, L0_gnn_Wu, L0_gnn_go, L0_gnn_bo, L0_gnn_F1W, L0_gnn_F1b, L0_gnn_F2W, L0_gnn_F2b, L0_gnn_gn, L0_gnn_bn, L0_gnn_emb, L0_gnn_adapt, L1_gnn_w_rel1, L1_gnn_w_root1, L1_gnn_b1, L1_gnn_w_rel2, L1_gnn_w_root2, L1_gnn_b2):
    import jax
    import jax.numpy as jnp

    def _L0_gnn_ref(h, edge_index, edge_attr, distances, atom_z, node_mult, batch, Wq, gq, bq, Wk, gk, bk, Wm, Wu, go, bo, F1W, F1b, F2W, F2b, gn, bn, emb, adapt):
        import jax, jax.numpy as jnp
        import numpy as np
        N = 50000
        E = 37500
        H = 48
        RBF = 40
        L = 4
        NELEM = 119
        G = 32
        CUT = 6.0

        def _ln(x, g, b):
            m = x.mean(-1, keepdims=True)
            v = ((x - m) ** 2).mean(-1, keepdims=True)
            return (x - m) * jax.lax.rsqrt(v + 1e-05) * g + b
        src, dst = (edge_index[0], edge_index[1])
        gate = jax.nn.silu(edge_attr @ F1W + F1b) @ F2W + F2b
        ei = emb[atom_z[src]]
        ej = emb[atom_z[dst]]
        gate = gate + (ei * (ej @ adapt)).sum(-1, keepdims=True)
        cw = jnp.where(distances < CUT, 0.5 * (jnp.cos(jnp.pi * distances / CUT) + 1.0), 0.0)
        mj = node_mult[dst]
        msg = gate * h[dst] * (cw * mj)[:, None]
        agg = jax.ops.segment_sum(msg, src, num_segments=N)
        tot = jnp.clip(jax.ops.segment_sum(mj, src, num_segments=N), 1e-08, None)
        h = _ln(h + agg / tot[:, None], gn, bn)
        logm = jnp.log(jnp.clip(node_mult, 1.0, None))
        for i in range(L):
            Q = _ln(h @ Wq[i], gq[i], bq[i])
            K = _ln(h @ Wk[i], gk[i], bk[i])
            qi = Q[src]
            kj = K[dst]
            score = (qi * kj).sum(-1) + 0.1 * (edge_attr * qi[:, :RBF]).sum(-1) + logm[dst]
            smax = jax.ops.segment_max(score, src, num_segments=N)
            es = jnp.exp(jnp.minimum(score - smax[src], 20.0))
            denom = jax.ops.segment_sum(es, src, num_segments=N)
            alpha = es / (denom[src] + 1e-10)
            m = h[dst] @ Wm[i]
            aggi = jax.ops.segment_sum(alpha[:, None] * m, src, num_segments=N)
            z = jnp.concatenate([h, aggi], axis=-1) @ Wu[i]
            z = jnp.where(z > 0, z, 0.01 * z)
            h = _ln(h + z, go[i], bo[i])
        return h

    def _L1_gnn_ref(x, edge_index, w_rel1, w_root1, b1, w_rel2, w_root2, b2):
        import jax, jax.numpy as jnp
        import numpy as np
        N_NODES = 3125
        N_EDGES = 50000
        D_IN = 48
        D_H = 48
        D_OUT = 48

        def _graph_conv(x, src, dst, w_rel, w_root, b, num_nodes):
            agg = jax.ops.segment_sum(x[src], dst, num_segments=num_nodes)
            return agg @ w_rel + x @ w_root + b
        src, dst = (edge_index[0], edge_index[1])
        n = x.shape[0]
        h = jax.nn.relu(_graph_conv(x, src, dst, w_rel1, w_root1, b1, n))
        out = _graph_conv(h, src, dst, w_rel2, w_root2, b2, n)
        return out
    edge_index = jnp.stack([src, dst])
    batch0 = jnp.zeros((50000,), jnp.int32)
    x = _layernorm(x + _L0_gnn_ref(x, edge_index, edge_attr_40, edge_weight, node_type_119, node_vec, batch0, L0_gnn_Wq, L0_gnn_gq, L0_gnn_bq, L0_gnn_Wk, L0_gnn_gk, L0_gnn_bk, L0_gnn_Wm, L0_gnn_Wu, L0_gnn_go, L0_gnn_bo, L0_gnn_F1W, L0_gnn_F1b, L0_gnn_F2W, L0_gnn_F2b, L0_gnn_gn, L0_gnn_bn, L0_gnn_emb, L0_gnn_adapt), axis=-1)
    x = _layernorm(x + _L1_gnn_ref(x, edge_index, L1_gnn_w_rel1, L1_gnn_w_root1, L1_gnn_b1, L1_gnn_w_rel2, L1_gnn_w_root2, L1_gnn_b2), axis=-1)
    return x

_drawn_inputs = setup_inputs


def setup_inputs(seed=0):
    import zlib

    import numpy as np

    out = dict(_drawn_inputs(seed))
    spreads = {'L0_gnn_gq': (1.0, 0.2),
     'L0_gnn_bq': (0.0, 0.387),
     'L0_gnn_gk': (1.0, 0.2),
     'L0_gnn_bk': (0.0, 2.0),
     'L0_gnn_go': (1.0, 0.2),
     'L0_gnn_bo': (0.0, 0.1),
     'L0_gnn_F1b': (0.0, 0.8),
     'L0_gnn_F2b': (0.0, 0.295),
     'L0_gnn_gn': (1.0, 0.2),
     'L0_gnn_bn': (0.0, 0.1)}
    factors = {'edge_attr_40': 2.825,
     'node_vec': 2.707,
     'L0_gnn_emb': 64.0,
     'L0_gnn_adapt': 64.0,
     'L1_gnn_b1': 3.214}
    for name, (base, spread) in spreads.items():
        noise = np.random.default_rng([zlib.crc32(name.encode()), seed]).standard_normal(out[name].shape)
        drawn = base * np.exp(spread * noise) if base else spread * noise
        out[name] = jnp.asarray(drawn.astype(out[name].dtype))
    for name, factor in factors.items():
        out[name] = (out[name] * factor).astype(out[name].dtype)
    return out
```

```python
import concourse.bass as bass
from concourse import mybir
from contextlib import ExitStack
from itertools import count

P = 128
N = 50000
H = 48
RBF = 40
GE = 32
NELEM = 119
LAYERS = 4
NT = 392
NP = NT * P
CH = 14
NCH = NT // CH
IT = NCH // 2
HC = H + 1
W1 = 3 + RBF
NTW = H + GE + 1
CUT = 6.0
PI = 3.141592653589793
BIG = 1e30

F32 = mybir.dt.float32
I32 = mybir.dt.int32
BF16 = mybir.dt.bfloat16
ALU = mybir.AluOpType
ACT = mybir.ActivationFunctionType
AX = mybir.AxisListType


START = 16
PASSED = []
SERIAL = count()


class Chain:

    def __init__(self, eng, sem):
        self.eng, self.sem, self.n = eng, sem, 0

    def __call__(self, ins):
        self.n += 1
        ins.then_inc(self.sem, 1)
        self.eng.wait_ge(self.sem, self.n)

    def restart(self):
        self.eng.sem_clear(self.sem)
        self.n = 0


def wait_apart(eng, sem, value):
    eng.wait_ge(sem, value)
    eng.sem_inc(PASSED[0], 1)


def phase(nc, names, early=()):
    sems = {n: nc.alloc_semaphore(f"{n}_{next(SERIAL)}") for n in (*names, *early)}
    for n in early:
        nc.sync.sem_inc(sems[n], START)
    if early:
        nc.all_engine_barrier()
    return sems


def end_phase(nc, sems):
    nc.clear_and_free_semaphores(list(sems.values()))
    nc.all_engine_barrier()


def gnn_kernel(nc, a, out):
    ctx = ExitStack()
    with ctx:
        def sb(name, shape, dt=F32):
            return ctx.enter_context(nc.sbuf_tensor(name, shape, dt))

        def dram(name, shape, dt=F32):
            return nc.dram_tensor(name, shape, dt).ap()

        d_half = dram("half_sorted1", [NP, W1])
        d_edges = dram("edges_by_src", [NP, W1])
        d_half2 = dram("half_sorted2", [NP, 2])
        d_pairs = dram("edges_by_dst", [NP, 2])
        d_elem = dram("element_rows", [NELEM, 2 * GE])
        d_node = dram("node_rows", [NP, NTW])
        d_emb = dram("node_embeddings", [NP, GE])
        d_end = dram("last_edge", [65536], I32)
        d_has = dram("has_edges", [65536])
        d_seg = dram("scanned_rows", [NP, HC])
        d_h = dram("h_rows", [NP, H])
        d_q = dram("q_rows", [NP, H])
        d_kh = dram("k_h_rows", [NP, 2 * H])
        d_x1 = dram("x1_rows", [NP, H])
        d_y1 = dram("y1_rows", [NP, H])

        G = sb("G", [P, NT, HC])
        ident = sb("ident", [P, P])
        before = sb("before", [P, P])
        onesf = sb("onesf", [P, P])
        before_b = sb("before_b", [P, P], BF16)
        upto_b = sb("upto_b", [P, P], BF16)
        ones_b = sb("ones_b", [P, P], BF16)
        zeros_b = sb("zeros_b", [P, 512], BF16)
        iota_i = sb("iota_i", [P, 256], I32)
        iota_b = sb("iota_b", [P, 256], BF16)
        onesrow = sb("onesrow", [P, 256])
        base_lo = sb("base_lo", [P, 256])
        base_hi = sb("base_hi", [P, 256])
        seg_idx = sb("seg_idx", [P, NT], I32)
        far_idx = sb("far_idx", [P, NT], I32)
        end_idx = sb("end_idx", [P, NT], I32)
        has = sb("has", [P, NT])
        keyf = sb("keyf", [P, NT])
        farf = sb("farf", [P, NT])
        same_prev = sb("same_prev", [P, NT])
        same_next = sb("same_next", [P, NT])
        lead = sb("lead", [P, NT])
        trail = sb("trail", [P, NT])
        cut_prev = sb("cut_prev", [P, NT])
        cut_next = sb("cut_next", [P, NT])
        dist = sb("dist", [P, NT])
        cw = sb("cw", [P, NT])
        logm = sb("logm", [P, NT])
        score = sb("score", [P, NT])
        scanf = sb("scanf", [P, NT])
        scanb = sb("scanb", [P, NT])
        bufA = sb("bufA", [P, 2, CH, 2 * H])
        bufB = sb("bufB", [P, 2, CH, H])
        bufC = sb("bufC", [P, 2, CH, H])
        tmp = sb("tmp", [P, CH, 2 * H])
        tmp2 = sb("tmp2", [P, CH, 2 * H])
        xT = sb("xT", [2 * H, CH * P])
        col = sb("col", [P, 64])
        row = sb("row", [64, 4, P])
        rowc = sb("rowc", [1, 2, P])
        ez = sb("ez", [H, CH * P])
        bufD = sb("bufD", [P, 2, CH, H])
        chunk_i = sb("chunk_i", [P, 2, CH, 2], I32)
        idx = sb("idx", [P, 2, CH], I32)
        digi = sb("digi", [P, 2, CH], I32)
        digf = sb("digf", [P, 2, CH])
        rank = sb("rank", [P, 2, CH])
        primer = sb("primer", [16, 2])
        wqk = sb("wqk", [H, 2 * H])
        wz = sb("wz", [2 * H, H])
        wtmp = sb("wtmp", [H, 4, H])
        gb = sb("gb", [P, 8, H])
        f1w = sb("f1w", [RBF, H])
        f2w = sb("f2w", [H, H])
        f1b = sb("f1b", [H, 1])
        ps = [ctx.enter_context(nc.psum_tensor(f"ps{n}", [P, 512], F32)) for n in range(4)]
        psw = ctx.enter_context(nc.psum_tensor("psw", [P, 4, 512], F32))

        Gf = G[:, :, :].rearrange("p a b -> p (a b)")
        G_b = Gf.bitcast(BF16)
        oh = G_b[:, 0:2048].rearrange("p (b n) -> p b n", b=4)
        hist = Gf[:, 1024:1536]
        incl = Gf[:, 1536:2048]
        cnt = Gf[:, 2048:2560].rearrange("p (g n) -> p g n", g=2)
        cinc = Gf[:, 2560:3072].rearrange("p (g n) -> p g n", g=2)
        endf = Gf[:, 3072:3584].rearrange("p (g n) -> p g n", g=2)
        endi = Gf[:, 3584:4096].bitcast(I32).rearrange("p (g n) -> p g n", g=2)
        hasf = Gf[:, 4096:4608].rearrange("p (g n) -> p g n", g=2)
        key_i = Gf[:, 5000:5000 + NT].bitcast(I32)
        dg_i = Gf[:, 5400:5400 + NT].bitcast(I32)
        lof = Gf[:, 5800:5800 + NT]
        hif = Gf[:, 6200:6200 + NT]
        pay = Gf[:, 7000:7000 + 2 * CH * W1].rearrange("p (b t w) -> p b t w", b=2, w=W1)
        pay2 = Gf[:, 9000:9000 + 2 * CH * 2].rearrange("p (b t w) -> p b t w", b=2, w=2)

        def tiles(table):
            return table.rearrange("(p j) w -> p j w", p=P)

        def flat(v):
            return v.rearrange("(p j) -> p j", p=P)

        def bc(ap, n):
            return ap.unsqueeze(len(ap.shape)).to_broadcast(list(ap.shape) + [n])

        def bcm(ap, n=CH):
            return ap.unsqueeze(1).to_broadcast([ap.shape[0], n, ap.shape[1]])

        def prime(eng, sems):
            for n, sem in enumerate(sems):
                eng.dma_start(primer[:, n:n + 1], a["F1b"][0:16].rearrange("(p a) -> p a", a=1)).then_inc(sem, START)

        PASSED[:] = [nc.alloc_semaphore("waits_passed")]
        s = phase(nc, ["c_pool", "c_dve", "c_ld", "c_dma", "c_pe", "c_chain", "c_pchain"])
        with nc.Block() as block:
            @block.gpsimd
            def _(pool):
                link = Chain(pool, s["c_pchain"])
                link(pool.iota(iota_i[:], [[1, 256]], base=0, channel_multiplier=0))
                link(pool.memset(ones_b[:], 1.0))
                link(pool.memset(onesf[:], 1.0))
                link(pool.memset(onesrow[:], 1.0))
                link(pool.memset(zeros_b[:], 0.0))
                link(pool.memset(ident[:], 0.0))
                link(pool.affine_select(out=ident[:], in_=ident[:], compare_op=ALU.not_equal, fill=1.0,
                                        base=0, pattern=[[-1, P]], channel_multiplier=1))
                link(pool.affine_select(out=before[:], in_=onesf[:], compare_op=ALU.is_gt, fill=0.0,
                                        base=0, pattern=[[1, P]], channel_multiplier=-1))
                pool.sem_inc(s["c_pool"], 1)

            @block.vector
            def _(v):
                link = Chain(v, s["c_chain"])
                v.wait_ge(s["c_pool"], 1)
                link(v.tensor_copy(iota_b[:], iota_i[:]))
                link(v.tensor_copy(before_b[:], before[:]))
                link(v.tensor_scalar(upto_b[:], before[:], -1.0, 1.0, ALU.mult, ALU.add))
                v.sem_inc(s["c_dve"], 1)
                v.wait_ge(s["c_pe"], 1)
                v.tensor_copy(xT[0:GE, 0:NELEM], ps[0][0:GE, 0:NELEM]).then_inc(s["c_dve"], 1)
                v.wait_ge(s["c_pe"], 2)
                v.tensor_copy(bufA[0:NELEM, 0, 2, 0:GE], ps[1][0:NELEM, 0:GE]).then_inc(s["c_dve"], 1)

            @block.tensor
            def _(pe):
                pe.wait_ge(s["c_dve"], 1)
                pe.wait_ge(s["c_ld"], 32)
                pe.transpose(ps[0][0:GE, 0:NELEM], bufA[0:NELEM, 0, 0, 0:GE], ident[0:NELEM, 0:NELEM]).then_inc(s["c_pe"], 1)
                pe.wait_ge(s["c_dve"], 2)
                pe.matmul(ps[1][0:NELEM, 0:GE], xT[0:GE, 0:NELEM], bufA[0:GE, 0, 1, 0:GE],
                          start=True, stop=True).then_inc(s["c_pe"], 1)

            @block.sync
            def _(sp):
                sp.dma_start(bufA[0:NELEM, 0, 0, 0:GE], a["emb"]).then_inc(s["c_ld"], 16)
                sp.dma_start(bufA[0:GE, 0, 1, 0:GE], a["adapt"]).then_inc(s["c_ld"], 16)
                sp.dma_start(d_elem[:, 0:GE], a["emb"]).then_inc(s["c_dma"], 16)
                sp.dma_start(f1w[:], a["F1W"]).then_inc(s["c_dma"], 16)
                sp.dma_start(f2w[:], a["F2W"]).then_inc(s["c_dma"], 16)
                sp.dma_start(f1b[:], a["F1b"].rearrange("(p a) -> p a", a=1)).then_inc(s["c_dma"], 16)
                sp.wait_ge(s["c_dve"], 3)
                sp.dma_start(d_elem[:, GE:2 * GE], bufA[0:NELEM, 0, 2, 0:GE]).then_inc(s["c_dma"], 16)
                sp.wait_ge(s["c_dma"], 80)
        end_phase(nc, s)

        def node_rows():
            s = phase(nc, ["n_ld", "n_cp", "n_x0", "n_x1", "n_g0", "n_g1", "n_st0", "n_st1"])
            g, st, xs = [s["n_g0"], s["n_g1"]], [s["n_st0"], s["n_st1"]], [s["n_x0"], s["n_x1"]]
            with nc.Block() as block:
                @block.sync
                def _(sp):
                    sp.dma_start(seg_idx[:], flat(a["ntype"])).then_inc(s["n_ld"], 16)
                    sp.dma_start(score[:], flat(a["nvec"])).then_inc(s["n_ld"], 16)
                    prime(sp, st)
                    with sp.Fori(0, IT) as it:
                        for b in range(2):
                            at = (it * 2 + b) * CH
                            wait_apart(sp, st[b], it * 32 + START)
                            sp.dma_start(bufB[:, b], tiles(a["x"])[:, bass.ds(at, CH), :]).then_inc(xs[b], 16)
                            wait_apart(sp, s["n_cp"], it * 2 + b + 1)
                            sp.dma_start(tiles(d_node)[:, bass.ds(at, CH), :], bufC_row[b]).then_inc(st[b], 16)
                            sp.dma_start(tiles(d_emb)[:, bass.ds(at, CH), :], bufA[:, b, :, 0:GE]).then_inc(st[b], 16)
                    sp.wait_ge(st[0], IT * 32 + START)
                    sp.wait_ge(st[1], IT * 32 + START)

                @block.gpsimd
                def _(pool):
                    pool.wait_ge(s["n_ld"], 32)
                    with pool.Fori(0, IT) as it:
                        for b in range(2):
                            at = (it * 2 + b) * CH
                            pool.wait_ge(st[b], it * 32 + START)
                            pool.tensor_copy(idx[:, b], seg_idx[:, bass.ds(at, CH)]).then_inc(s_own[b], 1)
                            wait_apart(pool, s_own[b], it + 1)
                            for t in range(CH):
                                pool.indirect_dma_start(bufA[:, b, t, 0:2 * GE], None, d_elem[:, :],
                                                        bass.IndirectOffsetOnAxis(ap=idx[:, b, t:t + 1], axis=0)).then_inc(g[b], 16)

                @block.vector
                def _(v):
                    with v.Fori(0, IT) as it:
                        for b in range(2):
                            at = (it * 2 + b) * CH
                            v.wait_ge(st[b], it * 32 + START)
                            v.wait_ge(s["n_ld"], 32)
                            v.wait_ge(xs[b], it * 16 + 16)
                            v.tensor_copy(bufC_row[b][:, :, 0:H], bufB[:, b])
                            v.tensor_copy(bufC_row[b][:, :, H + GE:NTW], score[:, bass.ds(at, CH)].unsqueeze(2))
                            v.wait_ge(g[b], (it + 1) * (16 * CH))
                            v.tensor_copy(bufC_row[b][:, :, H:H + GE], bufA[:, b, :, GE:2 * GE]).then_inc(s["n_cp"], 1)
            end_phase(nc, s)

        bufC_row = [Gf[:, 12000 + n * CH * NTW:12000 + (n + 1) * CH * NTW].rearrange("p (t w) -> p t w", w=NTW) for n in range(2)]
        s_own = [nc.alloc_semaphore("own0"), nc.alloc_semaphore("own1")]
        node_rows()
        end_phase(nc, {"a": s_own[0], "b": s_own[1]})

        def histogram(key):
            s = phase(nc, ["h_ld", "h_oh", "h_mm", "h_chain", "h_pe", "h_dve", "h_st"])
            with nc.Block() as block:
                @block.sync
                def _(sp):
                    sp.dma_start(key_i[:], flat(key)).then_inc(s["h_ld"], 16)
                    sp.wait_ge(s["h_dve"], 2)
                    for g in range(2):
                        at = slice(g * 32768, (g + 1) * 32768)
                        sp.dma_start(d_end[at].rearrange("(p c) -> p c", p=P), endi[:, g]).then_inc(s["h_st"], 16)
                        sp.dma_start(d_has[at].rearrange("(p c) -> p c", p=P), hasf[:, g]).then_inc(s["h_st"], 16)
                    sp.wait_ge(s["h_st"], 64)
                    sp.dma_start(end_idx[:], flat(d_end[0:NP])).then_inc(s["h_st"], 16)
                    sp.dma_start(has[:], flat(d_has[0:NP])).then_inc(s["h_st"], 16)
                    sp.wait_ge(s["h_st"], 96)

                @block.vector
                def _(v):
                    link = Chain(v, s["h_chain"])
                    v.wait_ge(s["h_ld"], 16)
                    link(v.tensor_scalar(dg_i[:], key_i[:], 255, None, ALU.bitwise_and))
                    link(v.tensor_copy(lof[:], dg_i[:]))
                    link(v.tensor_scalar(dg_i[:], key_i[:], 8, None, ALU.logical_shift_right))
                    link(v.tensor_copy(hif[:], dg_i[:]))
                    with v.Fori(0, NT // 2) as it:
                        for b in range(2):
                            t = it * 2 + b
                            v.wait_ge(s["h_mm"], t + 1)
                            v.tensor_scalar(oh[:, b, 0:256], iota_b[:], lof[:, bass.ds(t, 1)], None, ALU.is_equal)
                            v.tensor_scalar(oh[:, b, 256:512], iota_b[:], hif[:, bass.ds(t, 1)], None,
                                            ALU.is_equal).then_inc(s["h_oh"], 1)
                    v.wait_ge(s["h_mm"], NT + 2)
                    link(v.tensor_copy(hist[:], ps[0][:]))
                    for at, base in ((0, base_lo), (256, base_hi)):
                        r = slice(at, at + 256)
                        link(v.tensor_tensor_scan(incl[:, r], onesrow[:, :], hist[:, r], 0.0, ALU.mult, ALU.add))
                        link(v.tensor_tensor(base[:], incl[:, r], hist[:, r], ALU.subtract))
                    for g in range(2):
                        link(v.tensor_copy(cnt[:, g], ps[1 + g][:, 0:256]))
                        link(v.tensor_tensor_scan(cinc[:, g], onesrow[:, :], cnt[:, g], 0.0, ALU.mult, ALU.add))
                        link(v.tensor_copy(col[:, g:g + 1], cinc[:, g, 255:256]))
                    v.sem_inc(s["h_dve"], 1)
                    v.wait_ge(s["h_pe"], 1)
                    link(v.tensor_copy(col[:, 2:4], ps[3][:, 0:2]))
                    link(v.tensor_tensor(col[:, 3:4], col[:, 3:4], ps[3][:, 2:3], ALU.add))
                    for g in range(2):
                        link(v.tensor_scalar(endf[:, g], cinc[:, g], col[:, 2 + g:3 + g], -1.0, ALU.add, ALU.add))
                        link(v.tensor_scalar(endi[:, g], endf[:, g], 0.0, None, ALU.max))
                        link(v.tensor_scalar(hasf[:, g], cnt[:, g], 1.0, None, ALU.min))
                    v.sem_inc(s["h_dve"], 1)

                @block.tensor
                def _(pe):
                    pe.matmul(ps[0][:], ones_b[:], zeros_b[:], start=True, stop=True)
                    pe.matmul(ps[1][:, 0:256], ones_b[:], zeros_b[:, 0:256], start=True, stop=True).then_inc(s["h_mm"], 1)
                    pe.matmul(ps[2][:, 0:256], ones_b[:], zeros_b[:, 0:256], start=True, stop=True).then_inc(s["h_mm"], 1)
                    with pe.Fori(0, NT // 2) as it:
                        for b in range(2):
                            pe.wait_ge(s["h_oh"], it * 2 + b + 1)
                            more = dict(start=False, stop=True, skip_group_check=True)
                            pe.matmul(ps[0][:], ones_b[:], oh[:, b, :], **more)
                            pe.matmul(ps[1][:, 0:256], oh[:, b, 256:384], oh[:, b, 0:256], **more)
                            pe.matmul(ps[2][:, 0:256], oh[:, b, 384:512], oh[:, b, 0:256], **more).then_inc(s["h_mm"], 1)
                    pe.wait_ge(s["h_dve"], 1)
                    pe.matmul(ps[3][:, 0:2], before[:], col[:, 0:2], start=True, stop=True)
                    pe.matmul(ps[3][:, 2:3], onesf[:], col[:, 0:1], start=True, stop=True).then_inc(s["h_pe"], 1)
            end_phase(nc, s)

        junk2 = [Gf[:, 4608:4864], Gf[:, 9200:9456]]

        def rank_pass(first, high, rows, table_in, table_out, key_col):
            s = phase(nc, ["r_ld0", "r_ld1", "r_oh", "r_mm1", "r_used", "r_chain", "r_sc0", "r_sc1"],
                      ["r_mm2", "r_idx"])
            ld, sc = [s["r_ld0"], s["r_ld1"]], [s["r_sc0"], s["r_sc1"]]
            base = base_hi if high else base_lo
            wide = rows.shape[3]
            n_ld = 16 * (2 if first and wide > 2 else 1)
            with nc.Block() as block:
                @block.sync
                def _(sp):
                    with sp.Fori(0, IT) as it:
                        for b in range(2):
                            at = (it * 2 + b) * CH
                            wait_apart(sp, sc[b], it * (16 * CH) + START)
                            wait_apart(sp, s["r_idx"], it * 2 + b - 1 + START)
                            if first:
                                sp.dma_start(chunk_i[:, b], tiles(a["pairs"])[:, bass.ds(at, CH), :]).then_inc(ld[b], 16)
                                if wide > 2:
                                    sp.dma_start(rows[:, b, :, 2:W1], tiles(a["efeat"])[:, bass.ds(at, CH), :]).then_inc(ld[b], 16)
                            else:
                                sp.dma_start(rows[:, b], table_in.rearrange("(j p) w -> p j w", p=P)[:, bass.ds(at, CH), :]).then_inc(ld[b], 16)

                @block.vector
                def _(v):
                    link = Chain(v, s["r_chain"])
                    with v.Fori(0, IT) as it:
                        link.restart()
                        for b in range(2):
                            v.wait_ge(ld[b], (it + 1) * n_ld)
                            v.wait_ge(sc[b], it * (16 * CH) + START)
                            if first:
                                link(v.tensor_copy(rows[:, b, :, 0:1], chunk_i[:, b, :, key_col:key_col + 1]))
                                link(v.tensor_copy(rows[:, b, :, 1:2], chunk_i[:, b, :, 1 - key_col:2 - key_col]))
                            link(v.tensor_copy(digi[:, b], rows[:, b, :, 0]))
                            if high:
                                link(v.tensor_scalar(idx[:, b], digi[:, b], 8, None, ALU.logical_shift_right))
                            else:
                                link(v.tensor_scalar(idx[:, b], digi[:, b], 255, None, ALU.bitwise_and))
                            link(v.tensor_copy(digf[:, b], idx[:, b]))
                            for t in range(CH):
                                n = (it * 2 + b) * CH + t
                                if t == 0:
                                    v.wait_ge(s["r_mm2"], n + START)
                                    v.tensor_scalar(oh[:, 0, 0:256], iota_b[:], digf[:, b, 0:1], None,
                                                    ALU.is_equal).then_inc(s["r_oh"], 1)
                                if t + 1 < CH:
                                    if t:
                                        v.wait_ge(s["r_mm2"], n + START)
                                    v.tensor_scalar(oh[:, (t + 1) % 2, 0:256], iota_b[:], digf[:, b, t + 1:t + 2], None,
                                                    ALU.is_equal).then_inc(s["r_oh"], 1)
                                v.wait_ge(s["r_mm1"], n + 1)
                                v.tensor_tensor_reduce(out=junk2[t % 2], in0=ps[0][:, 0:256], in1=oh[:, t % 2, 0:256],
                                                       scale=1.0, scalar=0.0, op0=ALU.mult, op1=ALU.add,
                                                       accum_out=rank[:, b, t:t + 1]).then_inc(s["r_used"], 1)
                            v.wait_ge(s["r_used"], (it * 2 + b + 1) * CH)
                            v.tensor_copy(idx[:, b], rank[:, b]).then_inc(s["r_idx"], 1)

                @block.tensor
                def _(pe):
                    pe.matmul(ps[0][:, 0:256], ident[:], base[:], start=True, stop=True)
                    with pe.Fori(0, IT) as it:
                        for t in range(2 * CH):
                            n = it * (2 * CH) + t
                            buf = oh[:, (t % CH) % 2, 0:256]
                            more = dict(start=False, stop=True, skip_group_check=True)
                            wait_apart(pe, s["r_oh"], n + 1)
                            pe.matmul(ps[0][:, 0:256], before_b[:], buf, **more).then_inc(s["r_mm1"], 1)
                            wait_apart(pe, s["r_used"], n + 1)
                            pe.matmul(ps[0][:, 0:256], upto_b[:], buf, **more).then_inc(s["r_mm2"], 1)

                @block.gpsimd
                def _(pool):
                    prime(pool, sc)
                    with pool.Fori(0, IT) as it:
                        for b in range(2):
                            wait_apart(pool, s["r_idx"], it * 2 + b + 1 + START)
                            for t in range(CH):
                                pool.indirect_dma_start(table_out[:, :], bass.IndirectOffsetOnAxis(ap=idx[:, b, t:t + 1], axis=0),
                                                        rows[:, b, t, :], None).then_inc(sc[b], 16)
                    pool.wait_ge(sc[0], IT * 16 * CH + START)
                    pool.wait_ge(sc[1], IT * 16 * CH + START)
            end_phase(nc, s)

        def take_order(table, width):
            s = phase(nc, ["t_ld0", "t_ld1", "t_edge", "t_dve", "t_chain"],
                      ["t_cp"])
            ld = [s["t_ld0"], s["t_ld1"]]
            rows = pay if width == W1 else pay2
            with nc.Block() as block:
                @block.sync
                def _(sp):
                    with sp.Fori(0, IT) as it:
                        for b in range(2):
                            wait_apart(sp, s["t_cp"], it * 2 + b - 1 + START)
                            sp.dma_start(rows[:, b], tiles(table)[:, bass.ds((it * 2 + b) * CH, CH), :]).then_inc(ld[b], 16)
                    sp.wait_ge(s["t_dve"], 1)
                    sp.dma_start(col[1:P, 0:1], keyf[0:P - 1, NT - 1:NT]).then_inc(s["t_edge"], 16)
                    sp.dma_start(col[0:P - 1, 1:2], keyf[1:P, 0:1]).then_inc(s["t_edge"], 16)

                @block.vector
                def _(v):
                    link = Chain(v, s["t_chain"])
                    with v.Fori(0, IT) as it:
                        for b in range(2):
                            at = bass.ds((it * 2 + b) * CH, CH)
                            v.wait_ge(ld[b], it * 16 + 16)
                            v.tensor_copy(keyf[:, at], rows[:, b, :, 0])
                            if width == W1:
                                v.tensor_copy(dist[:, at], rows[:, b, :, 2])
                            v.tensor_copy(farf[:, at], rows[:, b, :, 1]).then_inc(s["t_cp"], 1)
                    v.wait_ge(s["t_cp"], NCH + START)
                    link(v.memset(col[:, 0:2], -1.0))
                    link(v.tensor_copy(seg_idx[:], keyf[:]))
                    link(v.tensor_copy(far_idx[:], farf[:]))
                    v.sem_inc(s["t_dve"], 1)
                    v.wait_ge(s["t_edge"], 32)
                    link(v.tensor_tensor(same_prev[:, 1:NT], keyf[:, 1:NT], keyf[:, 0:NT - 1], ALU.is_equal))
                    link(v.tensor_tensor(same_prev[:, 0:1], keyf[:, 0:1], col[:, 0:1], ALU.is_equal))
                    link(v.tensor_copy(same_next[:, 0:NT - 1], same_prev[:, 1:NT]))
                    link(v.tensor_tensor(same_next[:, NT - 1:NT], keyf[:, NT - 1:NT], col[:, 1:2], ALU.is_equal))
                    link(v.tensor_tensor_scan(lead[:], same_prev[:], same_prev[:], 1.0, ALU.mult, ALU.min))
                    link(v.tensor_tensor_scan(trail[:, ::-1], same_next[:, ::-1], same_next[:, ::-1], 1.0, ALU.mult, ALU.min))
                    link(v.tensor_scalar(cut_prev[:], same_prev[:], -1.0, BIG, ALU.add, ALU.mult))
                    link(v.tensor_scalar(cut_next[:], same_next[:], -1.0, BIG, ALU.add, ALU.mult))
            end_phase(nc, s)

        def segment_sums():
            s = phase(nc, ["s_scan", "s_dve", "s_pe", "s_chain", "s_fix", "s_st"])
            with nc.Block() as block:
                @block.vector
                def _(v):
                    link = Chain(v, s["s_chain"])
                    with v.Fori(0, HC) as c:
                        g = G[:, :, bass.ds(c, 1)].rearrange("p j a -> p (j a)")
                        v.tensor_tensor_scan(g, same_prev[:], g, 0.0, ALU.mult, ALU.add).then_inc(s["s_scan"], 1)
                    v.wait_ge(s["s_scan"], HC)
                    link(v.tensor_copy(col[:, 0:HC], G[:, NT - 1, :]))
                    link(v.tensor_copy(tmp[:, 0, 0:HC], lead[:, NT - 1:NT].to_broadcast([P, HC])))
                    v.sem_inc(s["s_dve"], 1)
                    v.wait_ge(s["s_pe"], 1)
                    link(v.tensor_copy(row[0:HC, 0, :], ps[0][0:HC, 0:P]))
                    link(v.tensor_copy(row[0:HC, 1, :], ps[1][0:HC, 0:P]))
                    link(v.memset(row[0:HC, 2, 0:1], 0.0))
                    link(v.tensor_tensor_scan(row[0:HC, 2, 1:P], row[0:HC, 1, 0:P - 1], row[0:HC, 0, 0:P - 1],
                                              0.0, ALU.mult, ALU.add))
                    v.sem_inc(s["s_dve"], 1)
                    v.wait_ge(s["s_pe"], 2)
                    link(v.tensor_copy(col[:, 0:HC], ps[2][:, 0:HC]))
                    with v.Fori(0, HC) as c:
                        g = G[:, :, bass.ds(c, 1)].rearrange("p j a -> p (j a)")
                        v.scalar_tensor_tensor(g, lead[:], col[:, bass.ds(c, 1)], g, ALU.mult, ALU.add).then_inc(s["s_fix"], 1)

                @block.tensor
                def _(pe):
                    pe.wait_ge(s["s_dve"], 1)
                    pe.transpose(ps[0][0:HC, 0:P], col[:, 0:HC], ident[:])
                    pe.transpose(ps[1][0:HC, 0:P], tmp[:, 0, 0:HC], ident[:]).then_inc(s["s_pe"], 1)
                    pe.wait_ge(s["s_dve"], 2)
                    pe.transpose(ps[2][:, 0:HC], row[0:HC, 2, :], ident[0:HC, 0:HC]).then_inc(s["s_pe"], 1)

                @block.sync
                def _(sp):
                    sp.wait_ge(s["s_fix"], HC)
                    sp.dma_start(tiles(d_seg), G[:, :, :]).then_inc(s["s_st"], 16)
                    sp.wait_ge(s["s_st"], 16)
            end_phase(nc, s)

        def softmax_weights():
            s = phase(nc, ["m_dve", "m_pe", "m_act", "m_chain"])
            rev = slice(None, None, -1)
            with nc.Block() as block:
                @block.vector
                def _(v):
                    link = Chain(v, s["m_chain"])
                    link(v.tensor_tensor(score[:], score[:], logm[:], ALU.add))
                    link(v.tensor_tensor_scan(scanf[:], cut_prev[:], score[:], -BIG, ALU.add, ALU.max))
                    link(v.tensor_tensor_scan(scanb[:, rev], cut_next[:, rev], score[:, rev], -BIG, ALU.add, ALU.max))
                    link(v.tensor_copy(col[:, 0:1], scanf[:, NT - 1:NT]))
                    link(v.tensor_copy(col[:, 1:2], scanb[:, 0:1]))
                    link(v.tensor_scalar(col[:, 2:3], lead[:, NT - 1:NT], -1.0, BIG, ALU.add, ALU.mult))
                    link(v.tensor_scalar(col[:, 3:4], trail[:, 0:1], -1.0, BIG, ALU.add, ALU.mult))
                    v.sem_inc(s["m_dve"], 1)
                    v.wait_ge(s["m_pe"], 1)
                    for n in range(4):
                        link(v.tensor_copy(row[0:1, n, :], ps[n][0:1, 0:P]))
                    link(v.memset(rowc[0:1, :, :], -BIG))
                    link(v.tensor_tensor_scan(rowc[0:1, 0, 1:P], row[0:1, 2, 0:P - 1], row[0:1, 0, 0:P - 1], -BIG, ALU.add, ALU.max))
                    link(v.tensor_tensor_scan(rowc[0:1, 1, 0:P - 1][:, rev], row[0:1, 3, 1:P][:, rev], row[0:1, 1, 1:P][:, rev],
                                              -BIG, ALU.add, ALU.max))
                    v.sem_inc(s["m_dve"], 1)
                    v.wait_ge(s["m_pe"], 2)
                    link(v.tensor_copy(col[:, 4:5], ps[0][:, 0:1]))
                    link(v.tensor_copy(col[:, 5:6], ps[1][:, 0:1]))
                    link(v.tensor_tensor_scan(scanf[:], cut_prev[:], score[:], col[:, 4:5], ALU.add, ALU.max))
                    link(v.tensor_tensor_scan(scanb[:, rev], cut_next[:, rev], score[:, rev], col[:, 5:6], ALU.add, ALU.max))
                    link(v.tensor_tensor(scanf[:], scanf[:], scanb[:], ALU.max))
                    link(v.tensor_tensor(score[:], score[:], scanf[:], ALU.subtract))
                    link(v.tensor_scalar(score[:], score[:], 20.0, None, ALU.min))
                    v.sem_inc(s["m_dve"], 1)
                    v.wait_ge(s["m_act"], 1)
                    link(v.tensor_tensor(G[:, :, 0:H], G[:, :, 0:H], bc(scanb[:], H), ALU.mult))
                    link(v.tensor_copy(G[:, :, H:HC], scanb[:].unsqueeze(2)))

                @block.scalar
                def _(act):
                    act.wait_ge(s["m_dve"], 3)
                    act.activation(scanb[:], score[:], ACT.Exp).then_inc(s["m_act"], 1)
                    act.wait_ge(s["m_act"], 1)

                @block.tensor
                def _(pe):
                    pe.wait_ge(s["m_dve"], 1)
                    for n in range(4):
                        last = pe.transpose(ps[n][0:1, 0:P], col[:, n:n + 1], ident[:])
                    last.then_inc(s["m_pe"], 1)
                    pe.wait_ge(s["m_dve"], 2)
                    pe.transpose(ps[0][:, 0:1], rowc[0:1, 0, :], ident[0:1, 0:1])
                    pe.transpose(ps[1][:, 0:1], rowc[0:1, 1, :], ident[0:1, 0:1]).then_inc(s["m_pe"], 1)
            end_phase(nc, s)

        def first_messages():
            s = phase(nc, ["f_ld0", "f_ld1", "f_p0", "f_p1", "f_tr", "f_cp", "f_z", "f_silu", "f_gate", "f_act", "f_dve", "f_ix", "f_chain", "f_achain", "f_act2", "f_init", "f_g0", "f_g1"],
                      ["f_done"])
            ld, g, pk = [s["f_ld0"], s["f_ld1"]], [s["f_g0"], s["f_g1"]], [s["f_p0"], s["f_p1"]]
            W = CH * P
            with nc.Block() as block:
                @block.sync
                def _(sp):
                    sp.dma_start(gb[:, 0, :], a["F2b"].partition_broadcast(P)).then_inc(s["f_init"], 16)
                    with sp.Fori(0, IT) as it:
                        for b in range(2):
                            wait_apart(sp, s["f_done"], it * 2 + b - 1 + START)
                            sp.dma_start(bufB[:, b, :, 0:RBF], tiles(d_edges)[:, bass.ds((it * 2 + b) * CH, CH), 3:W1]).then_inc(ld[b], 16)

                @block.gpsimd
                def _(pool):
                    with pool.Fori(0, IT) as it:
                        for b in range(2):
                            at = bass.ds((it * 2 + b) * CH, CH)
                            pool.wait_ge(s["f_done"], it * 2 + b - 1 + START)
                            pool.tensor_copy(chunk_i[:, b, :, 0:1], far_idx[:, at].unsqueeze(2)).then_inc(pk[b], 1)
                            pool.tensor_copy(chunk_i[:, b, :, 1:2], seg_idx[:, at].unsqueeze(2)).then_inc(pk[b], 1)
                            wait_apart(pool, pk[b], it * 2 + 2)
                            for t in range(CH):
                                pool.indirect_dma_start(bufA[:, b, t, 0:NTW], None, d_node[:, :],
                                                        bass.IndirectOffsetOnAxis(ap=chunk_i[:, b, t, 0:1], axis=0)).then_inc(g[b], 16)
                                pool.indirect_dma_start(bufC[:, b, t, 0:GE], None, d_emb[:, :],
                                                        bass.IndirectOffsetOnAxis(ap=chunk_i[:, b, t, 1:2], axis=0)).then_inc(g[b], 16)

                @block.tensor
                def _(pe):
                    with pe.Fori(0, IT) as it:
                        for b in range(2):
                            n = it * 2 + b
                            wait_apart(pe, ld[b], it * 16 + 16)
                            for q in range(4):
                                k = min(4, CH - 4 * q)
                                for t in range(4 * q, 4 * q + k):
                                    last = pe.transpose(psw[0:RBF, q, (t % 4) * P:(t % 4 + 1) * P], bufB[:, b, t, 0:RBF], ident[:])
                            last.then_inc(s["f_tr"], 1)
                            wait_apart(pe, s["f_cp"], n + 1)
                            for q in range(4):
                                k = min(4, CH - 4 * q) * P
                                last = pe.matmul(psw[0:H, q, 0:k], f1w[:], xT[0:RBF, q * 512:q * 512 + k], start=True, stop=True)
                            last.then_inc(s["f_z"], 1)
                            wait_apart(pe, s["f_silu"], n + 1)
                            for t in range(CH):
                                last = pe.matmul(psw[:, t // 8, (t % 8) * 64:(t % 8) * 64 + H], xT[0:H, t * P:(t + 1) * P], f2w[:],
                                                 start=True, stop=True)
                            last.then_inc(s["f_gate"], 1)
                            wait_apart(pe, s["f_dve"], n + 1)

                @block.scalar
                def _(act):
                    link = Chain(act, s["f_achain"])
                    act.wait_ge(s["f_ix"], 1)
                    act.activation(cw[:], cw[:], ACT.Sin).then_inc(s["f_act2"], 1)
                    with act.Fori(0, IT) as it:
                        link.restart()
                        for b in range(2):
                            n = it * 2 + b
                            act.wait_ge(s["f_tr"], n + 1)
                            for q in range(4):
                                k = min(4, CH - 4 * q) * P
                                link(act.copy(xT[0:RBF, q * 512:q * 512 + k], psw[0:RBF, q, 0:k]))
                            act.sem_inc(s["f_cp"], 1)
                            act.wait_ge(s["f_z"], n + 1)
                            for q in range(4):
                                k = min(4, CH - 4 * q) * P
                                link(act.activation(xT[0:H, q * 512:q * 512 + k], psw[0:H, q, 0:k], ACT.Identity, bias=f1b[:]))
                                link(act.activation(ez[0:H, q * 512:q * 512 + k], xT[0:H, q * 512:q * 512 + k], ACT.Exp, scale=-1.0))
                            act.sem_inc(s["f_act"], 1)
                    act.wait_ge(s["f_ix"], 2)
                    act.activation(logm[:], logm[:], ACT.Ln).then_inc(s["f_act2"], 1)

                @block.vector
                def _(v):
                    link = Chain(v, s["f_chain"])
                    v.wait_ge(s["f_init"], 16)
                    link(v.tensor_scalar(cw[:], dist[:], CUT, -PI / (2 * CUT), ALU.min, ALU.mult))
                    link(v.tensor_scalar(cw[:], cw[:], PI / 2, None, ALU.add))
                    v.sem_inc(s["f_ix"], 1)
                    v.wait_ge(s["f_act2"], 1)
                    link(v.tensor_tensor(cw[:], cw[:], cw[:], ALU.mult))
                    link(v.tensor_scalar(dist[:], dist[:], CUT, None, ALU.is_lt))
                    link(v.tensor_tensor(cw[:], cw[:], dist[:], ALU.mult))
                    with v.Fori(0, IT) as it:
                        link.restart()
                        for b in range(2):
                            n = it * 2 + b
                            at = bass.ds(n * CH, CH)
                            v.wait_ge(s["f_act"], n + 1)
                            link(v.tensor_scalar(ez[0:H, 0:W], ez[0:H, 0:W], 1.0, None, ALU.add))
                            link(v.reciprocal(ez[0:H, 0:W], ez[0:H, 0:W]))
                            link(v.tensor_tensor(xT[0:H, 0:W], xT[0:H, 0:W], ez[0:H, 0:W], ALU.mult))
                            v.sem_inc(s["f_silu"], 1)
                            v.wait_ge(g[b], (it + 1) * (32 * CH))
                            link(v.tensor_tensor(tmp[:, :, 0:GE], bufA[:, b, :, H:H + GE], bufC[:, b, :, 0:GE], ALU.mult))
                            link(v.tensor_reduce(col[:, 0:CH], tmp[:, :, 0:GE], AX.X, ALU.add))
                            link(v.tensor_copy(col[:, CH:2 * CH], bufA[:, b, :, NTW - 1]))
                            link(v.tensor_copy(G[:, at, H:HC], col[:, CH:2 * CH].unsqueeze(2)))
                            link(v.tensor_tensor(col[:, CH:2 * CH], col[:, CH:2 * CH], cw[:, at], ALU.mult))
                            v.wait_ge(s["f_gate"], n + 1)
                            for q, k in ((0, 8), (1, CH - 8)):
                                link(v.tensor_tensor(tmp[:, 8 * q:8 * q + k, 0:H],
                                                     psw[:, q, 0:64 * k].rearrange("p (t c) -> p t c", c=64)[:, :, 0:H],
                                                     bcm(gb[:, 0, :], k), ALU.add))
                            v.sem_inc(s["f_dve"], 1)
                            link(v.tensor_tensor(tmp[:, :, 0:H], tmp[:, :, 0:H], bc(col[:, 0:CH], H), ALU.add))
                            link(v.tensor_tensor(tmp[:, :, 0:H], tmp[:, :, 0:H], bufA[:, b, :, 0:H], ALU.mult))
                            link(v.tensor_tensor(G[:, at, 0:H], tmp[:, :, 0:H], bc(col[:, CH:2 * CH], H), ALU.mult))
                            v.sem_inc(s["f_done"], 1)
                    link(v.tensor_scalar(logm[:].unsqueeze(2), G[:, :, H:HC], 1.0, None, ALU.max))
                    v.sem_inc(s["f_ix"], 1)
                    v.wait_ge(s["f_act2"], 2)

            end_phase(nc, s)

        def layer_norm(v, link, y, mean, sems, n, gain=None, bias=None, dst=None):
            if mean:
                link(v.tensor_reduce(col[:, 0:CH], y, AX.X, ALU.add))
                link(v.tensor_scalar(col[:, 0:CH], col[:, 0:CH], -1.0 / H, None, ALU.mult))
                link(v.tensor_tensor(y, y, bc(col[:, 0:CH], H), ALU.add))
            link(v.tensor_tensor(tmp2[:, :, 0:H], y, y, ALU.mult))
            link(v.tensor_reduce(col[:, 0:CH], tmp2[:, :, 0:H], AX.X, ALU.add))
            link(v.tensor_scalar(col[:, 0:CH], col[:, 0:CH], 1.0 / H, 1e-5, ALU.mult, ALU.add))
            v.sem_inc(sems[0], 1)
            v.wait_ge(sems[1], n + 1)
            link(v.reciprocal(col[:, CH:2 * CH], col[:, CH:2 * CH]))
            if gain is None:
                link(v.tensor_tensor(dst, y, bc(col[:, CH:2 * CH], H), ALU.mult))
            else:
                link(v.tensor_tensor(y, y, bc(col[:, CH:2 * CH], H), ALU.mult))
                link(v.tensor_tensor(y, y, bcm(gain), ALU.mult))
                link(v.tensor_tensor(dst, y, bcm(bias), ALU.add))

        def node_step(mode, table_in, table_out, table_add=None, gain=None):
            s = phase(nc, ["u_ld0", "u_ld1", "u_ix0", "u_ix1", "u_hz", "u_tr", "u_cp", "u_z", "u_leak", "u_var", "u_root", "u_chain", "u_achain", "u_w", "u_g0", "u_g1", "u_st0", "u_st1"],
                      ["u_done"])
            ld, g, st, ix = [[s[k + "0"], s[k + "1"]] for k in ("u_ld", "u_g", "u_st", "u_ix")]
            product = mode in ("layer", "conv", "last")
            sums = mode != "join"
            n_ld = 16 * (1 + (table_add is not None))
            with nc.Block() as block:
                @block.sync
                def _(sp):
                    with sp.Fori(0, IT) as it:
                        for b in range(2):
                            n = it * 2 + b
                            at = bass.ds(n * CH, CH)
                            wait_apart(sp, s["u_done"], n - 1 + START)
                            sp.dma_start(bufB[:, b], tiles(table_in)[:, at, :]).then_inc(ld[b], 16)
                            if table_add is not None:
                                sp.dma_start(bufD[:, b], tiles(table_add)[:, at, :]).then_inc(ld[b], 16)

                @block.gpsimd
                def _(pool):
                    def fetch(n, b, w):
                        pool.tensor_copy(idx[:, b], end_idx[:, bass.ds(n * CH, CH)]).then_inc(ix[b], 1)
                        wait_apart(pool, ix[b], w)
                        for t in range(CH):
                            pool.indirect_dma_start(bufA[:, b, t, 0:HC], None, d_seg[:, :],
                                                    bass.IndirectOffsetOnAxis(ap=idx[:, b, t:t + 1], axis=0)).then_inc(g[b], 16)
                    if sums:
                        with pool.Fori(0, IT) as it:
                            for b in range(2):
                                pool.wait_ge(s["u_done"], it * 2 + b - 1 + START)
                                fetch(it * 2 + b, b, it + 1)

                @block.vector
                def _(v):
                    link = Chain(v, s["u_chain"])
                    with v.Fori(0, IT) as it:
                        link.restart()
                        for b in range(2):
                            n = it * 2 + b
                            at = bass.ds(n * CH, CH)
                            v.wait_ge(ld[b], (it + 1) * n_ld)
                            v.wait_ge(st[b], it * 16 + START)
                            if sums:
                                v.wait_ge(g[b], (it + 1) * (16 * CH))
                                if mode in ("first", "layer"):
                                    link(v.tensor_tensor(col[:, 0:CH], bufA[:, b, :, H], has[:, at], ALU.mult))
                                    if mode == "first":
                                        link(v.tensor_scalar(col[:, 0:CH], col[:, 0:CH], 1e-8, None, ALU.max))
                                    else:
                                        link(v.tensor_scalar(col[:, 0:CH], col[:, 0:CH], 1e-10, None, ALU.add))
                                    link(v.reciprocal(col[:, 0:CH], col[:, 0:CH]))
                                    link(v.tensor_tensor(col[:, 0:CH], col[:, 0:CH], has[:, at], ALU.mult))
                                else:
                                    link(v.tensor_copy(col[:, 0:CH], has[:, at]))
                                link(v.tensor_tensor(tmp[:, :, H:2 * H], bufA[:, b, :, 0:H], bc(col[:, 0:CH], H), ALU.mult))
                            if product:
                                link(v.tensor_copy(tmp[:, :, 0:H], bufB[:, b]))
                                v.sem_inc(s["u_hz"], 1)
                            if mode == "layer":
                                v.wait_ge(s["u_leak"], n + 1)
                                for q, k in ((0, 8), (1, CH - 8)):
                                    r = slice(8 * q, 8 * q + k)
                                    link(v.tensor_tensor(tmp2[:, r, 0:H], z_part(q, k), tmp2[:, r, 0:H], ALU.max))
                                link(v.tensor_tensor(tmp[:, :, 0:H], tmp2[:, :, 0:H], bufB[:, b], ALU.add))
                            elif product:
                                v.wait_ge(s["u_z"], n + 1)
                                for q, k in ((0, 8), (1, CH - 8)):
                                    link(v.tensor_tensor(tmp[:, 8 * q:8 * q + k, 0:H], z_part(q, k), bcm(gb[:, 7, :], k), ALU.add))
                                if mode == "last":
                                    link(v.tensor_tensor(tmp[:, :, 0:H], tmp[:, :, 0:H], bufD[:, b], ALU.add))
                            elif mode == "first":
                                link(v.tensor_tensor(tmp[:, :, 0:H], tmp[:, :, H:2 * H], bufB[:, b], ALU.add))
                            else:
                                link(v.tensor_tensor(tmp[:, :, 0:H], bufB[:, b], bufD[:, b], ALU.add))
                            if mode == "conv":
                                link(v.tensor_scalar(bufC[:, b], tmp[:, :, 0:H], 0.0, None, ALU.max))
                            else:
                                affine = gain is not None
                                layer_norm(v, link, tmp[:, :, 0:H], True, (s["u_var"], s["u_root"]), n,
                                           gb[:, gain, :] if affine else None, gb[:, gain + 1, :] if affine else None, bufC[:, b])
                            v.sem_inc(s["u_done"], 1)

                @block.scalar
                def _(act):
                    link = Chain(act, s["u_achain"])
                    prime(act, st)
                    with act.Fori(0, IT) as it:
                        link.restart()
                        for b in range(2):
                            n = it * 2 + b
                            if product:
                                act.wait_ge(s["u_tr"], n + 1)
                                for q in range(4):
                                    k = min(4, CH - 4 * q) * P
                                    link(act.copy(xT[:, q * 512:q * 512 + k], psw[0:2 * H, q, 0:k]))
                                act.sem_inc(s["u_cp"], 1)
                            if mode == "layer":
                                act.wait_ge(s["u_z"], n + 1)
                                for q, k in ((0, 8), (1, CH - 8)):
                                    link(act.mul(tmp2[:, 8 * q:8 * q + k, 0:H], z_part(q, k), 0.01))
                                act.sem_inc(s["u_leak"], 1)
                            if mode != "conv":
                                act.wait_ge(s["u_var"], n + 1)
                                link(act.activation(col[:, CH:2 * CH], col[:, 0:CH], ACT.Sqrt))
                                act.sem_inc(s["u_root"], 1)
                            act.wait_ge(s["u_done"], n + 1 + START)
                            act.dma_start(tiles(table_out)[:, bass.ds(n * CH, CH), :], bufC[:, b]).then_inc(st[b], 16)
                    act.wait_ge(st[0], IT * 16 + START)
                    act.wait_ge(st[1], IT * 16 + START)

                if product:
                    @block.tensor
                    def _(pe):
                        with pe.Fori(0, IT) as it:
                            for b in range(2):
                                n = it * 2 + b
                                wait_apart(pe, s["u_done"], n + START)
                                wait_apart(pe, s["u_hz"], n + 1)
                                for t in range(CH):
                                    last = pe.transpose(psw[0:2 * H, t // 4, (t % 4) * P:(t % 4 + 1) * P], tmp[:, t, :], ident[:])
                                last.then_inc(s["u_tr"], 1)
                                wait_apart(pe, s["u_cp"], n + 1)
                                for t in range(CH):
                                    last = pe.matmul(psw[:, t // 8, (t % 8) * 64:(t % 8) * 64 + H], xT[:, t * P:(t + 1) * P], wz[:],
                                                     start=True, stop=True)
                                last.then_inc(s["u_z"], 1)
            end_phase(nc, s)

        def z_part(q, k):
            return psw[:, q, 0:64 * k].rearrange("p (t c) -> p t c", c=64)[:, :, 0:H]

        def qk_step():
            s = phase(nc, ["q_ld0", "q_ld1", "q_tr", "q_cp", "q_mm", "q_sq", "q_var", "q_root", "q_chain", "q_achain", "q_st0", "q_st1"],
                      ["q_done"])
            ld, st = [s["q_ld0"], s["q_ld1"]], [s["q_st0"], s["q_st1"]]

            def prod(q, k):
                return psw[:, q, 0:P * k].rearrange("p (t c) -> p t c", c=P)[:, :, 0:2 * H]
            PARTS = [(q, min(4, CH - 4 * q)) for q in range(4)]
            with nc.Block() as block:
                @block.sync
                def _(sp):
                    with sp.Fori(0, IT) as it:
                        for b in range(2):
                            n = it * 2 + b
                            wait_apart(sp, s["q_done"], n - 1 + START)
                            sp.dma_start(bufB[:, b], tiles(d_h)[:, bass.ds(n * CH, CH), :]).then_inc(ld[b], 16)

                @block.tensor
                def _(pe):
                    with pe.Fori(0, IT) as it:
                        for b in range(2):
                            n = it * 2 + b
                            wait_apart(pe, ld[b], it * 16 + 16)
                            wait_apart(pe, s["q_done"], n + START)
                            for t in range(CH):
                                last = pe.transpose(psw[0:H, t // 4, (t % 4) * P:(t % 4 + 1) * P], bufB[:, b, t, :], ident[:])
                            last.then_inc(s["q_tr"], 1)
                            wait_apart(pe, s["q_cp"], n + 1)
                            for t in range(CH):
                                last = pe.matmul(psw[:, t // 4, (t % 4) * P:(t % 4) * P + 2 * H], xT[0:H, t * P:(t + 1) * P], wqk[:],
                                                 start=True, stop=True)
                            last.then_inc(s["q_mm"], 1)

                @block.scalar
                def _(act):
                    link = Chain(act, s["q_achain"])
                    prime(act, st)
                    with act.Fori(0, IT) as it:
                        link.restart()
                        for b in range(2):
                            n = it * 2 + b
                            at = bass.ds(n * CH, CH)
                            act.wait_ge(s["q_tr"], n + 1)
                            for q, k in PARTS:
                                link(act.copy(xT[0:H, q * 512:q * 512 + k * P], psw[0:H, q, 0:k * P]))
                            act.sem_inc(s["q_cp"], 1)
                            act.wait_ge(s["q_mm"], n + 1)
                            for q, k in PARTS:
                                link(act.activation(tmp2[:, 4 * q:4 * q + k, :], prod(q, k), ACT.Square))
                            act.sem_inc(s["q_sq"], 1)
                            act.wait_ge(s["q_var"], n + 1)
                            link(act.activation(col[:, 2 * CH:4 * CH], col[:, 0:2 * CH], ACT.Sqrt))
                            act.sem_inc(s["q_root"], 1)
                            act.wait_ge(s["q_done"], n + 1 + START)
                            act.dma_start(tiles(d_q)[:, at, :], bufC[:, b]).then_inc(st[b], 16)
                            act.dma_start(tiles(d_kh)[:, at, :], bufA[:, b]).then_inc(st[b], 16)
                    act.wait_ge(st[0], IT * 32 + START)
                    act.wait_ge(st[1], IT * 32 + START)

                @block.vector
                def _(v):
                    link = Chain(v, s["q_chain"])
                    with v.Fori(0, IT) as it:
                        link.restart()
                        for b in range(2):
                            n = it * 2 + b
                            v.wait_ge(s["q_sq"], n + 1)
                            two = tmp2[:, :, :].rearrange("p t (a c) -> p (t a) c", a=2)
                            link(v.tensor_reduce(col[:, 0:2 * CH], two, AX.X, ALU.add))
                            link(v.tensor_scalar(col[:, 0:2 * CH], col[:, 0:2 * CH], 1.0 / H, 1e-5, ALU.mult, ALU.add))
                            v.sem_inc(s["q_var"], 1)
                            v.wait_ge(s["q_root"], n + 1)
                            v.wait_ge(st[b], it * 32 + START)
                            link(v.reciprocal(col[:, 0:2 * CH], col[:, 2 * CH:4 * CH]))
                            rstd = col[:, 0:2 * CH].rearrange("p (t a) -> p t a", a=2)
                            for q, k in PARTS:
                                r = slice(4 * q, 4 * q + k)
                                link(v.tensor_tensor(tmp[:, r, 0:H], prod(q, k)[:, :, 0:H], bc(rstd[:, r, 0], H), ALU.mult))
                                link(v.tensor_tensor(tmp[:, r, H:2 * H], prod(q, k)[:, :, H:2 * H], bc(rstd[:, r, 1], H), ALU.mult))
                            link(v.tensor_tensor(tmp[:, :, 0:H], tmp[:, :, 0:H], bcm(gb[:, 0, :]), ALU.mult))
                            link(v.tensor_tensor(bufC[:, b], tmp[:, :, 0:H], bcm(gb[:, 1, :]), ALU.add))
                            link(v.tensor_tensor(tmp[:, :, H:2 * H], tmp[:, :, H:2 * H], bcm(gb[:, 2, :]), ALU.mult))
                            link(v.tensor_tensor(bufA[:, b, :, 0:H], tmp[:, :, H:2 * H], bcm(gb[:, 3, :]), ALU.add))
                            link(v.tensor_copy(bufA[:, b, :, H:2 * H], bufB[:, b]))
                            v.sem_inc(s["q_done"], 1)
            end_phase(nc, s)

        def edge_step(table=None):
            s = phase(nc, ["e_ld0", "e_ld1", "e_ix0", "e_ix1", "e_chain", "e_g0", "e_g1"],
                      ["e_done", "e_cp"])
            ld, g, ix = [s["e_ld0"], s["e_ld1"]], [s["e_g0"], s["e_g1"]], [s["e_ix0"], s["e_ix1"]]
            scored = table is None
            per = 32 if scored else 16
            with nc.Block() as block:
                if scored:
                    @block.sync
                    def _(sp):
                        with sp.Fori(0, IT) as it:
                            for b in range(2):
                                n = it * 2 + b
                                wait_apart(sp, s["e_done"], n - 1 + START)
                                sp.dma_start(bufB[:, b, :, 0:RBF], tiles(d_edges)[:, bass.ds(n * CH, CH), 3:W1]).then_inc(ld[b], 16)

                @block.gpsimd
                def _(pool):
                    with pool.Fori(0, IT) as it:
                        for b in range(2):
                            n = it * 2 + b
                            at = bass.ds(n * CH, CH)
                            if scored:
                                pool.wait_ge(s["e_done"], n - 1 + START)
                            pool.wait_ge(s["e_cp"], n - 1 + START)
                            pool.tensor_copy(chunk_i[:, b, :, 0:1], far_idx[:, at].unsqueeze(2)).then_inc(ix[b], 1)
                            pool.tensor_copy(chunk_i[:, b, :, 1:2], seg_idx[:, at].unsqueeze(2)).then_inc(ix[b], 1)
                            wait_apart(pool, ix[b], it * 2 + 2)
                            for t in range(CH):
                                far = bass.IndirectOffsetOnAxis(ap=chunk_i[:, b, t, 0:1], axis=0)
                                near = bass.IndirectOffsetOnAxis(ap=chunk_i[:, b, t, 1:2], axis=0)
                                if scored:
                                    pool.indirect_dma_start(bufA[:, b, t, :], None, d_kh[:, :], far).then_inc(g[b], 16)
                                    pool.indirect_dma_start(bufC[:, b, t, :], None, d_q[:, :], near).then_inc(g[b], 16)
                                else:
                                    pool.indirect_dma_start(bufC[:, b, t, :], None, table[:, :], far).then_inc(g[b], 16)

                @block.scalar
                def _(act):
                    with act.Fori(0, IT) as it:
                        for b in range(2):
                            n = it * 2 + b
                            act.wait_ge(g[b], (it + 1) * (per * CH))
                            rows = bufA[:, b, :, H:2 * H] if scored else bufC[:, b]
                            act.copy(G[:, bass.ds(n * CH, CH), 0:H], rows).then_inc(s["e_cp"], 1)

                @block.vector
                def _(v):
                    link = Chain(v, s["e_chain"])
                    if not scored:
                        link(v.memset(G[:, :, H:HC], 0.0))
                        return
                    with v.Fori(0, IT) as it:
                        link.restart()
                        for b in range(2):
                            n = it * 2 + b
                            v.wait_ge(g[b], (it + 1) * (per * CH))
                            v.wait_ge(ld[b], it * 16 + 16)
                            link(v.scalar_tensor_tensor(bufA[:, b, :, 0:RBF], bufB[:, b, :, 0:RBF], 0.1, bufA[:, b, :, 0:RBF], ALU.mult, ALU.add))
                            link(v.tensor_tensor(tmp[:, :, 0:H], bufA[:, b, :, 0:H], bufC[:, b], ALU.mult))
                            link(v.tensor_reduce(score[:, bass.ds(n * CH, CH)], tmp[:, :, 0:H], AX.X, ALU.add))
                            v.sem_inc(s["e_done"], 1)
            end_phase(nc, s)

        def load_rows(pairs, zrows=None):
            s = phase(nc, ["w_ld"])
            with nc.Block() as block:
                @block.sync
                def _(sp):
                    for n, src in pairs:
                        sp.dma_start(gb[:, n, :], src.partition_broadcast(P)).then_inc(s["w_ld"], 16)
                    for n, src in enumerate(zrows or []):
                        sp.dma_start(wz[n * H:(n + 1) * H, :], src).then_inc(s["w_ld"], 16)
                    sp.wait_ge(s["w_ld"], 16 * (len(pairs) + len(zrows or [])))
            end_phase(nc, s)

        def layer_weights(i):
            s = phase(nc, ["l_ld", "l_ch", "l_pe", "l_dve", "l_z"])

            def of(name):
                return a[name][bass.ds(i, 1)].rearrange("a k n -> (a k) n")

            def vec(name):
                return a[name][bass.ds(i, 1), :].rearrange("a n -> (a n)")
            with nc.Block() as block:
                @block.sync
                def _(sp):
                    sp.dma_start(wtmp[:, 0, :], of("Wq")).then_inc(s["l_ld"], 16)
                    sp.dma_start(wtmp[:, 1, :], of("Wk")).then_inc(s["l_ld"], 16)
                    sp.dma_start(wtmp[:, 2, :], of("Wm")).then_inc(s["l_ld"], 16)
                    sp.dma_start(wz[0:H, :], of("Wu")[0:H, :]).then_inc(s["l_ld"], 16)
                    sp.dma_start(wtmp[:, 3, :], of("Wu")[H:2 * H, :]).then_inc(s["l_ld"], 16)
                    for n, name in enumerate(("gq", "bq", "gk", "bk", "go", "bo")):
                        sp.dma_start(gb[:, n, :], vec(name).partition_broadcast(P)).then_inc(s["l_ld"], 16)
                    sp.wait_ge(s["l_dve"], 2)
                    sp.dma_start(wz[H:2 * H, :], xT[0:H, H:2 * H]).then_inc(s["l_z"], 16)
                    sp.wait_ge(s["l_z"], 16)

                @block.vector
                def _(v):
                    link = Chain(v, s["l_ch"])
                    v.wait_ge(s["l_ld"], 11 * 16)
                    link(v.tensor_reduce(col[0:H, 0:2], wtmp[:, 0:2, :], AX.X, ALU.add))
                    link(v.tensor_scalar(col[0:H, 0:2], col[0:H, 0:2], -1.0 / H, None, ALU.mult))
                    for n in range(2):
                        link(v.tensor_scalar(wqk[:, n * H:(n + 1) * H], wtmp[:, n, :], col[0:H, n:n + 1], None, ALU.add))
                    v.wait_ge(s["l_pe"], 1)
                    v.tensor_copy(xT[0:H, 0:H], ps[0][0:H, 0:H]).then_inc(s["l_dve"], 1)
                    v.wait_ge(s["l_pe"], 2)
                    v.tensor_copy(xT[0:H, H:2 * H], ps[1][0:H, 0:H]).then_inc(s["l_dve"], 1)

                @block.tensor
                def _(pe):
                    pe.wait_ge(s["l_ld"], 11 * 16)
                    pe.transpose(ps[0][0:H, 0:H], wtmp[:, 2, :], ident[0:H, 0:H]).then_inc(s["l_pe"], 1)
                    pe.wait_ge(s["l_dve"], 1)
                    pe.matmul(ps[1][0:H, 0:H], xT[0:H, 0:H], wtmp[:, 3, :], start=True, stop=True).then_inc(s["l_pe"], 1)
            end_phase(nc, s)

        histogram(a["src"])
        rank_pass(True, False, pay, None, d_half, 0)
        rank_pass(False, True, pay, d_half, d_edges, 0)
        take_order(d_edges, W1)
        first_messages()
        segment_sums()
        load_rows([(0, a["gn"]), (1, a["bn"])])
        node_step("first", a["x"], d_h, gain=0)
        with nc.Fori(0, LAYERS) as layer:
            layer_weights(layer)
            qk_step()
            edge_step()
            softmax_weights()
            segment_sums()
            node_step("layer", d_h, d_h, gain=4)
        node_step("join", a["x"], d_x1, table_add=d_h)
        histogram(a["dst"])
        rank_pass(True, False, pay2, None, d_half2, 1)
        rank_pass(False, True, pay2, d_half2, d_pairs, 1)
        take_order(d_pairs, 2)
        edge_step(d_x1)
        segment_sums()
        load_rows([(7, a["b1"])], [a["w_root1"], a["w_rel1"]])
        node_step("conv", d_x1, d_y1)
        edge_step(d_y1)
        segment_sums()
        load_rows([(7, a["b2"])], [a["w_root2"], a["w_rel2"]])
        node_step("last", d_y1, out, table_add=d_x1)


def kernel(**inputs):
    import numpy as np
    import concourse.bacc as bacc
    from concourse.bass_utils import run_bass_kernel_spmd

    def arr(name):
        return np.ascontiguousarray(inputs[name])

    def padded(v):
        return np.pad(v, [(0, NP - N)] + [(0, 0)] * (v.ndim - 1))
    ends = np.arange(N, NP, dtype=np.int32)
    src = np.concatenate([arr("src"), ends])
    dst = np.concatenate([arr("dst"), ends])
    arrays = {
        "x": padded(arr("x")), "src": src, "dst": dst, "pairs": np.stack([src, dst], 1),
        "efeat": np.concatenate([padded(arr("edge_weight"))[:, None], padded(arr("edge_attr_40"))], 1),
        "ntype": padded(arr("node_type_119")), "nvec": padded(arr("node_vec")),
    }
    for n in ("Wq", "gq", "bq", "Wk", "gk", "bk", "Wm", "Wu", "go", "bo", "F1W", "F1b", "F2W", "F2b", "gn", "bn", "emb", "adapt"):
        arrays[n] = arr("L0_gnn_" + n)
    for n in ("w_rel1", "w_root1", "b1", "w_rel2", "w_root2", "b2"):
        arrays[n] = arr("L1_gnn_" + n)
    nc = bacc.Bacc("TRN2", target_bir_lowering=False, num_devices=1)
    a = {n: nc.dram_tensor(f"in_{n}", v.shape, mybir.dt.from_np(v.dtype), kind="ExternalInput").ap() for n, v in arrays.items()}
    out = nc.dram_tensor("out", (NP, H), F32, kind="ExternalOutput").ap()
    gnn_kernel(nc, a, out)
    r = run_bass_kernel_spmd(nc, [{f"in_{n}": v for n, v in arrays.items()}], core_ids=[0])
    return r.results[0]["out"][:N]
```

```python
import concourse.bass as bass
from concourse import mybir
from contextlib import ExitStack
from itertools import count

P = 128
N = 50000
H = 48
RBF = 40
GE = 32
NELEM = 119
LAYERS = 4
NT = 392
NP = NT * P
CH = 14
NCH = NT // CH
IT = NCH // 2
RING = 4
ST = NCH // RING
HC = H + 1
W1 = 3 + RBF
NTW = H + GE + 2
SLW = H + GE + 1
CUT = 6.0
PI = 3.141592653589793
BIG = 1e30

F32 = mybir.dt.float32
I32 = mybir.dt.int32
BF16 = mybir.dt.bfloat16
ALU = mybir.AluOpType
ACT = mybir.ActivationFunctionType
AX = mybir.AxisListType


START = 16
PASSED = []
SERIAL = count()


class Chain:

    def __init__(self, eng, sem):
        self.eng, self.sem, self.n = eng, sem, 0

    def __call__(self, ins):
        self.n += 1
        ins.then_inc(self.sem, 1)
        self.eng.wait_ge(self.sem, self.n)

    def restart(self):
        self.eng.sem_clear(self.sem)
        self.n = 0


class Halves:

    def __init__(self, eng, sem):
        self.eng, self.sem, self.n, self.at = eng, sem, 0, [0, 0]

    def __call__(self, op):
        for q in range(2):
            if self.at[q]:
                self.eng.wait_ge(self.sem, self.at[q])
            self.n += 1
            op(q).then_inc(self.sem, 1)
            self.at[q] = self.n

    def join(self):
        self.eng.wait_ge(self.sem, self.n)

    def restart(self):
        self.eng.sem_clear(self.sem)
        self.n, self.at = 0, [0, 0]


def wait_apart(eng, sem, value):
    eng.wait_ge(sem, value)
    eng.sem_inc(PASSED[0], 1)


def phase(nc, names, early=()):
    sems = {n: nc.alloc_semaphore(f"{n}_{next(SERIAL)}") for n in (*names, *early)}
    for n in early:
        nc.sync.sem_inc(sems[n], START)
    if early:
        nc.all_engine_barrier()
    return sems


def end_phase(nc, sems):
    nc.clear_and_free_semaphores(list(sems.values()))
    nc.all_engine_barrier()


def gnn_kernel(nc, a, out):
    ctx = ExitStack()
    with ctx:
        def sb(name, shape, dt=F32):
            return ctx.enter_context(nc.sbuf_tensor(name, shape, dt))

        def dram(name, shape, dt=F32):
            return nc.dram_tensor(name, shape, dt).ap()

        d_half = dram("half_sorted1", [NP, W1])
        d_edges = dram("edges_by_src", [NP, W1])
        d_half2 = dram("half_sorted2", [NP, 2])
        d_pairs = dram("edges_by_dst", [NP, 2])
        d_elem = dram("element_rows", [NELEM, 2 * GE])
        d_node = dram("node_rows", [NP, NTW])
        d_slot = dram("slot_rows", [NP, SLW])
        d_place = dram("slot_places", [2 * NP, 1], I32)
        d_end = dram("last_edge", [65536], I32)
        d_has = dram("has_edges", [65536])
        d_seg = dram("scanned_rows", [NP, HC])
        d_kh = dram("k_h_rows", [NP, 2 * H])
        d_h = d_kh[:, H:2 * H]
        d_x1 = dram("x1_rows", [NP, H])
        d_y1 = dram("y1_rows", [NP, H])

        G = sb("G", [P, NT, HC])
        ident = sb("ident", [P, P])
        before = sb("before", [P, P])
        onesf = sb("onesf", [P, P])
        before_b = sb("before_b", [P, P], BF16)
        upto_b = sb("upto_b", [P, P], BF16)
        ones_b = sb("ones_b", [P, P], BF16)
        zeros_b = sb("zeros_b", [P, 512], BF16)
        iota_i = sb("iota_i", [P, 256], I32)
        iota_b = sb("iota_b", [P, 256], BF16)
        onesrow = sb("onesrow", [P, NT])
        base_lo = sb("base_lo", [P, 256])
        base_hi = sb("base_hi", [P, 256])
        seg_idx = sb("seg_idx", [P, NT], I32)
        far_idx = sb("far_idx", [P, NT], I32)
        end_idx = sb("end_idx", [P, NT], I32)
        has = sb("has", [P, NT])
        keyf = sb("keyf", [P, NT])
        farf = sb("farf", [P, NT])
        same_prev = sb("same_prev", [P, NT])
        same_next = sb("same_next", [P, NT])
        lead = sb("lead", [P, NT])
        trail = sb("trail", [P, NT])
        cut_prev = sb("cut_prev", [P, NT])
        cut_next = sb("cut_next", [P, NT])
        is_end = sb("is_end", [P, NT])
        pos_i = sb("pos_i", [P, NT], I32)
        slot_i = sb("slot_i", [P, NT], I32)
        node_i = sb("node_i", [P, NT], I32)
        dist = sb("dist", [P, NT])
        cw = sb("cw", [P, NT])
        logm = sb("logm", [P, NT])
        score = sb("score", [P, NT])
        scanf = sb("scanf", [P, NT])
        scanb = sb("scanb", [P, NT])
        bufA = sb("bufA", [P, 2, CH, 2 * H])
        hz = sb("hz", [P, RING, CH, 2 * H])
        bufD = sb("bufD", [P, RING, CH, H])
        bufB = bufD[:, 0:2]
        bufC = sb("bufC", [P, 2, CH, H])
        tmps = sb("tmps", [P, 2, CH, 2 * H])
        tmp = tmps[:, 0]
        weight = sb("weight", [P, NT])
        eps = sb("eps", [P, 1])
        tmp2 = sb("tmp2", [P, CH, 2 * H])
        sT = sb("sT", [H, CH * P])
        xT = sb("xT", [2 * H, CH * P])
        col = sb("col", [P, 64])
        row = sb("row", [64, 4, P])
        rowc = sb("rowc", [1, 2, P])
        chunk_i = sb("chunk_i", [P, 2, CH, 2], I32)
        idx = sb("idx", [P, 2, CH], I32)
        digi = sb("digi", [P, 2, CH], I32)
        digf = sb("digf", [P, 2, CH])
        rank = sb("rank", [P, 2, CH])
        primer = sb("primer", [16, 4])
        wqk = sb("wqk", [H, 2 * H])
        wz = sb("wz", [2 * H, H])
        wtmp = sb("wtmp", [H, 4, H])
        gb = sb("gb", [P, 8, H])
        f1w = sb("f1w", [RBF, H])
        f2w = sb("f2w", [H, H])
        f1b = sb("f1b", [H, 1])
        psm = ctx.enter_context(nc.psum_tensor("psm", [P, 4, 512], F32))
        ps = [psm[:, n] for n in range(4)]
        psw = ctx.enter_context(nc.psum_tensor("psw", [P, 4, 512], F32))

        Gf = G[:, :, :].rearrange("p a b -> p (a b)")
        G_b = Gf.bitcast(BF16)
        oh = G_b[:, 0:2048].rearrange("p (b n) -> p b n", b=4)
        hist = Gf[:, 1024:1536]
        incl = Gf[:, 1536:2048]
        cnt = Gf[:, 2048:2560].rearrange("p (g n) -> p g n", g=2)
        cinc = Gf[:, 2560:3072].rearrange("p (g n) -> p g n", g=2)
        endf = Gf[:, 3072:3584].rearrange("p (g n) -> p g n", g=2)
        endi = Gf[:, 3584:4096].bitcast(I32).rearrange("p (g n) -> p g n", g=2)
        hasf = Gf[:, 4096:4608].rearrange("p (g n) -> p g n", g=2)
        key_i = Gf[:, 5000:5000 + NT].bitcast(I32)
        dg_i = Gf[:, 5400:5400 + NT].bitcast(I32)
        lof = Gf[:, 5800:5800 + NT]
        hif = Gf[:, 6200:6200 + NT]
        pay = Gf[:, 7000:7000 + 2 * CH * W1].rearrange("p (b t w) -> p b t w", b=2, w=W1)
        pay2 = Gf[:, 9000:9000 + 2 * CH * 2].rearrange("p (b t w) -> p b t w", b=2, w=2)

        def tiles(table):
            return table.rearrange("(p j) w -> p j w", p=P)

        def flat(v):
            return v.rearrange("(p j) -> p j", p=P)

        def bc(ap, n):
            return ap.unsqueeze(len(ap.shape)).to_broadcast(list(ap.shape) + [n])

        def bcm(ap, n=CH):
            return ap.unsqueeze(1).to_broadcast([ap.shape[0], n, ap.shape[1]])

        def prime(eng, sems):
            for n, sem in enumerate(sems):
                eng.dma_start(primer[:, n:n + 1], a["F1b"][0:16].rearrange("(p a) -> p a", a=1)).then_inc(sem, START)

        def prime2(eng, sems):
            for n, sem in enumerate(sems):
                eng.dma_start(primer[:, 2 + n:3 + n], a["F1b"][0:16].rearrange("(p a) -> p a", a=1)).then_inc(sem, START)

        PASSED[:] = [nc.alloc_semaphore("waits_passed")]
        s = phase(nc, ["c_pool", "c_dve", "c_ld", "c_dma", "c_pe", "c_chain", "c_pchain"])
        with nc.Block() as block:
            @block.gpsimd
            def _(pool):
                link = Chain(pool, s["c_pchain"])
                link(pool.iota(iota_i[:], [[1, 256]], base=0, channel_multiplier=0))
                link(pool.iota(pos_i[:], [[1, NT]], base=0, channel_multiplier=NT))
                link(pool.memset(ones_b[:], 1.0))
                link(pool.memset(onesf[:], 1.0))
                link(pool.memset(onesrow[:], 1.0))
                link(pool.memset(zeros_b[:], 0.0))
                link(pool.memset(eps[:], 1e-5))
                link(pool.memset(ident[:], 0.0))
                link(pool.affine_select(out=ident[:], in_=ident[:], compare_op=ALU.not_equal, fill=1.0,
                                        base=0, pattern=[[-1, P]], channel_multiplier=1))
                link(pool.affine_select(out=before[:], in_=onesf[:], compare_op=ALU.is_gt, fill=0.0,
                                        base=0, pattern=[[1, P]], channel_multiplier=-1))
                pool.sem_inc(s["c_pool"], 1)

            @block.vector
            def _(v):
                link = Chain(v, s["c_chain"])
                v.wait_ge(s["c_pool"], 1)
                link(v.tensor_copy(iota_b[:], iota_i[:]))
                link(v.tensor_copy(before_b[:], before[:]))
                link(v.tensor_scalar(upto_b[:], before[:], -1.0, 1.0, ALU.mult, ALU.add))
                v.sem_inc(s["c_dve"], 1)
                v.wait_ge(s["c_pe"], 1)
                v.tensor_copy(xT[0:GE, 0:NELEM], ps[0][0:GE, 0:NELEM]).then_inc(s["c_dve"], 1)
                v.wait_ge(s["c_pe"], 2)
                v.tensor_copy(bufA[0:NELEM, 0, 2, 0:GE], ps[1][0:NELEM, 0:GE]).then_inc(s["c_dve"], 1)

            @block.tensor
            def _(pe):
                pe.wait_ge(s["c_dve"], 1)
                pe.wait_ge(s["c_ld"], 32)
                pe.transpose(ps[0][0:GE, 0:NELEM], bufA[0:NELEM, 0, 0, 0:GE], ident[0:NELEM, 0:NELEM]).then_inc(s["c_pe"], 1)
                pe.wait_ge(s["c_dve"], 2)
                pe.matmul(ps[1][0:NELEM, 0:GE], xT[0:GE, 0:NELEM], bufA[0:GE, 0, 1, 0:GE],
                          start=True, stop=True).then_inc(s["c_pe"], 1)

            @block.sync
            def _(sp):
                sp.dma_start(bufA[0:NELEM, 0, 0, 0:GE], a["emb"]).then_inc(s["c_ld"], 16)
                sp.dma_start(bufA[0:GE, 0, 1, 0:GE], a["adapt"]).then_inc(s["c_ld"], 16)
                sp.dma_start(d_elem[:, 0:GE], a["emb"]).then_inc(s["c_dma"], 16)
                sp.dma_start(f1w[:], a["F1W"]).then_inc(s["c_dma"], 16)
                sp.dma_start(f2w[:], a["F2W"]).then_inc(s["c_dma"], 16)
                sp.dma_start(f1b[:], a["F1b"].rearrange("(p a) -> p a", a=1)).then_inc(s["c_dma"], 16)
                sp.wait_ge(s["c_dve"], 3)
                sp.dma_start(d_elem[:, GE:2 * GE], bufA[0:NELEM, 0, 2, 0:GE]).then_inc(s["c_dma"], 16)
                sp.wait_ge(s["c_dma"], 80)
        end_phase(nc, s)

        def steps(eng, body, count=IT):
            with eng.Fori(0, count - 1) as it:
                body(it, False)
            body(count - 1, True)

        def make_slots():
            s = phase(nc, ["p_dve", "p_pe", "p_chain"])
            with nc.Block() as block:
                @block.vector
                def _(v):
                    link = Chain(v, s["p_chain"])
                    link(v.tensor_scalar(is_end[:], same_next[:], -1.0, 1.0, ALU.mult, ALU.add))
                    link(v.tensor_scalar(cw[:], has[:], -1.0, 1.0, ALU.mult, ALU.add))
                    link(v.tensor_tensor_scan(scanf[:], onesrow[:], same_next[:], 0.0, ALU.mult, ALU.add))
                    link(v.tensor_tensor_scan(scanb[:], onesrow[:], cw[:], 0.0, ALU.mult, ALU.add))
                    link(v.tensor_copy(col[:, 0:1], scanf[:, NT - 1:NT]))
                    link(v.tensor_copy(col[:, 1:2], scanb[:, NT - 1:NT]))
                    v.sem_inc(s["p_dve"], 1)
                    v.wait_ge(s["p_pe"], 1)
                    link(v.tensor_copy(col[:, 2:4], ps[0][:, 0:2]))
                    for c, (scan, own) in enumerate(((scanf, same_next), (scanb, cw))):
                        link(v.scalar_tensor_tensor(scan[:], scan[:], col[:, 2 + c:3 + c], own[:], ALU.add, ALU.subtract))
                        link(v.tensor_tensor(scan[:], scan[:], own[:], ALU.mult))
                    link(v.tensor_copy(logm[:], pos_i[:]))
                    link(v.scalar_tensor_tensor(logm[:], logm[:], float(NP), is_end[:], ALU.add, ALU.mult))
                    link(v.tensor_tensor(seg_idx[:], scanf[:], logm[:], ALU.add))
                    link(v.tensor_copy(logm[:], end_idx[:]))
                    link(v.scalar_tensor_tensor(logm[:], logm[:], float(NP), has[:], ALU.add, ALU.mult))
                    link(v.tensor_tensor(node_i[:], scanb[:], logm[:], ALU.add))

                @block.tensor
                def _(pe):
                    pe.wait_ge(s["p_dve"], 1)
                    pe.matmul(ps[0][:, 0:2], before[:], col[:, 0:2], start=True, stop=True).then_inc(s["p_pe"], 1)
            end_phase(nc, s)

            s = phase(nc, ["p_sc0", "p_sc1", "p_g0", "p_g1", "p_ix"], ["p_cp"])
            sc, g = [s["p_sc0"], s["p_sc1"]], [s["p_g0"], s["p_g1"]]
            with nc.Block() as block:
                @block.gpsimd
                def _(pool):
                    prime(pool, sc)
                    with pool.Fori(0, IT) as it:
                        for b in range(2):
                            at = bass.ds((it * 2 + b) * CH, CH)
                            pool.wait_ge(sc[b], it * (16 * CH) + START)
                            pool.tensor_copy(chunk_i[:, b, :, 0:1], pos_i[:, at].unsqueeze(2)).then_inc(s["p_ix"], 1)
                            pool.tensor_copy(idx[:, b], seg_idx[:, at]).then_inc(s["p_ix"], 1)
                            wait_apart(pool, s["p_ix"], it * 4 + 2 * b + 2)
                            for t in range(CH):
                                pool.indirect_dma_start(d_place[:, :], bass.IndirectOffsetOnAxis(ap=idx[:, b, t:t + 1], axis=0),
                                                        chunk_i[:, b, t, 0:1], None).then_inc(sc[b], 16)
                    pool.wait_ge(sc[0], IT * 16 * CH + START)
                    pool.wait_ge(sc[1], IT * 16 * CH + START)
                    with pool.Fori(0, IT) as it:
                        for b in range(2):
                            at = bass.ds((it * 2 + b) * CH, CH)
                            pool.wait_ge(s["p_cp"], it * 2 + b - 1 + START)
                            pool.tensor_copy(idx[:, b], node_i[:, at]).then_inc(s["p_ix"], 1)
                            wait_apart(pool, s["p_ix"], it * 2 + b + (4 * IT + 1))
                            for t in range(CH):
                                pool.indirect_dma_start(chunk_i[:, b, t, 1:2], None, d_place[:, :],
                                                        bass.IndirectOffsetOnAxis(ap=idx[:, b, t:t + 1], axis=0)).then_inc(g[b], 16)

                @block.vector
                def _(v):
                    with v.Fori(0, IT) as it:
                        for b in range(2):
                            v.wait_ge(g[b], (it + 1) * (16 * CH))
                            v.tensor_copy(slot_i[:, bass.ds((it * 2 + b) * CH, CH)].unsqueeze(2),
                                          chunk_i[:, b, :, 1:2]).then_inc(s["p_cp"], 1)
            end_phase(nc, s)

        def node_rows():
            s = phase(nc, ["n_ld", "n_g0", "n_g1", "n_st0", "n_st1", "n_sc0", "n_sc1", "n_ix", "n_x0", "n_x1", "n_chain"], ["n_cp"])
            g, st, sc, xs = [[s[k + "0"], s[k + "1"]] for k in ("n_g", "n_st", "n_sc", "n_x")]
            with nc.Block() as block:
                @block.sync
                def _(sp):
                    sp.dma_start(seg_idx[:], flat(a["ntype"])).then_inc(s["n_ld"], 16)
                    sp.dma_start(score[:], flat(a["nvec"])).then_inc(s["n_ld"], 16)
                    prime(sp, st)
                    with sp.Fori(0, IT) as it:
                        for b in range(2):
                            at = (it * 2 + b) * CH
                            wait_apart(sp, s["n_cp"], it * 2 + b - 1 + START)
                            sp.dma_start(bufB[:, b], tiles(a["x"])[:, bass.ds(at, CH), :]).then_inc(xs[b], 16)
                            sp.wait_ge(s["n_cp"], it * 2 + b + 1 + START)
                            sp.dma_start(tiles(d_node)[:, bass.ds(at, CH), :], node_row[b]).then_inc(st[b], 16)
                    sp.wait_ge(st[0], IT * 16 + START)
                    sp.wait_ge(st[1], IT * 16 + START)

                @block.gpsimd
                def _(pool):
                    prime2(pool, sc)
                    pool.wait_ge(s["n_ld"], 32)

                    def fetch(n, b, first):
                        pool.tensor_copy(idx[:, b], seg_idx[:, bass.ds(n * CH, CH)]).then_inc(s["n_ix"], 1)
                        wait_apart(pool, s["n_ix"], first)
                        for t in range(CH):
                            pool.indirect_dma_start(bufA[:, b, t, 0:2 * GE], None, d_elem[:, :],
                                                    bass.IndirectOffsetOnAxis(ap=idx[:, b, t:t + 1], axis=0)).then_inc(g[b], 16)

                    fetch(0, 0, 1)

                    def step(it, last):
                        for b in range(2):
                            n = it * 2 + b
                            if not (last and b):
                                pool.wait_ge(s["n_cp"], n + START)
                                fetch(n + 1, 1 - b, n * 2 + 2)
                            pool.wait_ge(s["n_cp"], n + 1 + START)
                            pool.tensor_copy(chunk_i[:, b, :, 0:1], slot_i[:, bass.ds(n * CH, CH)].unsqueeze(2)).then_inc(s["n_ix"], 1)
                            wait_apart(pool, s["n_ix"], n * 2 + 3 - (1 if last and b else 0))
                            for t in range(CH):
                                pool.indirect_dma_start(d_slot[:, :], bass.IndirectOffsetOnAxis(ap=chunk_i[:, b, t, 0:1], axis=0),
                                                        slot_row[b][:, t, :], None).then_inc(sc[b], 16)
                    steps(pool, step)
                    pool.wait_ge(sc[0], IT * 16 * CH + START)
                    pool.wait_ge(sc[1], IT * 16 * CH + START)

                @block.vector
                def _(v):
                    v.wait_ge(s["n_ld"], 32)
                    with v.Fori(0, IT) as it:
                        for b in range(2):
                            at = bass.ds((it * 2 + b) * CH, CH)
                            v.wait_ge(st[b], it * 16 + START)
                            v.wait_ge(sc[b], it * (16 * CH) + START)
                            v.tensor_copy(node_row[b][:, :, H + GE:H + GE + 1], score[:, at].unsqueeze(2))
                            v.tensor_copy(node_row[b][:, :, H + GE + 1:NTW], slot_i[:, at].unsqueeze(2))
                            v.tensor_copy(slot_row[b][:, :, H + GE:SLW], pos_i[:, at].unsqueeze(2))
                            v.wait_ge(xs[b], it * 16 + 16)
                            v.tensor_copy(node_row[b][:, :, 0:H], bufB[:, b])
                            v.tensor_copy(slot_row[b][:, :, 0:H], bufB[:, b])
                            v.wait_ge(g[b], (it + 1) * (16 * CH))
                            v.tensor_copy(slot_row[b][:, :, H:H + GE], bufA[:, b, :, 0:GE])
                            v.tensor_copy(node_row[b][:, :, H:H + GE], bufA[:, b, :, GE:2 * GE]).then_inc(s["n_cp"], 1)
            end_phase(nc, s)

        node_row = [Gf[:, 10000 + n * CH * NTW:10000 + (n + 1) * CH * NTW].rearrange("p (t w) -> p t w", w=NTW) for n in range(2)]
        slot_row = [Gf[:, 13000 + n * CH * SLW:13000 + (n + 1) * CH * SLW].rearrange("p (t w) -> p t w", w=SLW) for n in range(2)]

        def histogram(key):
            s = phase(nc, ["h_ld", "h_oh", "h_mm", "h_chain", "h_pe", "h_dve", "h_st"])
            with nc.Block() as block:
                @block.sync
                def _(sp):
                    sp.dma_start(key_i[:], flat(key)).then_inc(s["h_ld"], 16)
                    sp.wait_ge(s["h_dve"], 2)
                    for g in range(2):
                        at = slice(g * 32768, (g + 1) * 32768)
                        sp.dma_start(d_end[at].rearrange("(p c) -> p c", p=P), endi[:, g]).then_inc(s["h_st"], 16)
                        sp.dma_start(d_has[at].rearrange("(p c) -> p c", p=P), hasf[:, g]).then_inc(s["h_st"], 16)
                    sp.wait_ge(s["h_st"], 64)
                    sp.dma_start(end_idx[:], flat(d_end[0:NP])).then_inc(s["h_st"], 16)
                    sp.dma_start(has[:], flat(d_has[0:NP])).then_inc(s["h_st"], 16)
                    sp.wait_ge(s["h_st"], 96)

                @block.vector
                def _(v):
                    link = Chain(v, s["h_chain"])
                    v.wait_ge(s["h_ld"], 16)
                    link(v.tensor_scalar(dg_i[:], key_i[:], 255, None, ALU.bitwise_and))
                    link(v.tensor_copy(lof[:], dg_i[:]))
                    link(v.tensor_scalar(dg_i[:], key_i[:], 8, None, ALU.logical_shift_right))
                    link(v.tensor_copy(hif[:], dg_i[:]))
                    with v.Fori(0, NT // 4) as it:
                        for b in range(4):
                            t = it * 4 + b
                            v.wait_ge(s["h_mm"], t + 1)
                            v.tensor_scalar(oh[:, b, 0:256], iota_b[:], lof[:, bass.ds(t, 1)], None, ALU.is_equal)
                            v.tensor_scalar(oh[:, b, 256:512], iota_b[:], hif[:, bass.ds(t, 1)], None,
                                            ALU.is_equal).then_inc(s["h_oh"], 1)
                    v.wait_ge(s["h_mm"], NT + 4)
                    link(v.tensor_copy(hist[:], ps[0][:]))
                    for at, base in ((0, base_lo), (256, base_hi)):
                        r = slice(at, at + 256)
                        link(v.tensor_tensor_scan(incl[:, r], onesrow[:, 0:256], hist[:, r], 0.0, ALU.mult, ALU.add))
                        link(v.tensor_tensor(base[:], incl[:, r], hist[:, r], ALU.subtract))
                    for g in range(2):
                        link(v.tensor_copy(cnt[:, g], ps[1 + g][:, 0:256]))
                        link(v.tensor_tensor_scan(cinc[:, g], onesrow[:, 0:256], cnt[:, g], 0.0, ALU.mult, ALU.add))
                        link(v.tensor_copy(col[:, g:g + 1], cinc[:, g, 255:256]))
                    v.sem_inc(s["h_dve"], 1)
                    v.wait_ge(s["h_pe"], 1)
                    link(v.tensor_copy(col[:, 2:4], ps[3][:, 0:2]))
                    link(v.tensor_tensor(col[:, 3:4], col[:, 3:4], ps[3][:, 2:3], ALU.add))
                    for g in range(2):
                        link(v.tensor_scalar(endf[:, g], cinc[:, g], col[:, 2 + g:3 + g], -1.0, ALU.add, ALU.add))
                        link(v.tensor_scalar(endi[:, g], endf[:, g], 0.0, None, ALU.max))
                        link(v.tensor_scalar(hasf[:, g], cnt[:, g], 1.0, None, ALU.min))
                    v.sem_inc(s["h_dve"], 1)

                @block.tensor
                def _(pe):
                    pe.matmul(ps[0][:], ones_b[:], zeros_b[:], start=True, stop=True).then_inc(s["h_mm"], 1)
                    pe.matmul(ps[1][:, 0:256], ones_b[:], zeros_b[:, 0:256], start=True, stop=True).then_inc(s["h_mm"], 2)
                    pe.matmul(ps[2][:, 0:256], ones_b[:], zeros_b[:, 0:256], start=True, stop=True).then_inc(s["h_mm"], 1)
                    with pe.Fori(0, NT // 4) as it:
                        for b in range(4):
                            pe.wait_ge(s["h_oh"], it * 4 + b + 1)
                            more = dict(start=False, stop=True, skip_group_check=True)
                            pe.matmul(ps[0][:], ones_b[:], oh[:, b, :], **more)
                            pe.matmul(ps[1][:, 0:256], oh[:, b, 256:384], oh[:, b, 0:256], **more)
                            pe.matmul(ps[2][:, 0:256], oh[:, b, 384:512], oh[:, b, 0:256], **more).then_inc(s["h_mm"], 1)
                    pe.wait_ge(s["h_dve"], 1)
                    pe.matmul(ps[3][:, 0:2], before[:], col[:, 0:2], start=True, stop=True)
                    pe.matmul(ps[3][:, 2:3], onesf[:], col[:, 0:1], start=True, stop=True).then_inc(s["h_pe"], 1)
            end_phase(nc, s)

        junk2 = [Gf[:, 4608:4864], Gf[:, 9200:9456]]

        def rank_pass(first, high, rows, table_in, table_out, key_col):
            s = phase(nc, ["r_ld0", "r_ld1", "r_oh", "r_mm1", "r_chain", "r_sc0", "r_sc1"],
                      ["r_mm2", "r_idx", "r_used"])
            ld, sc = [s["r_ld0"], s["r_ld1"]], [s["r_sc0"], s["r_sc1"]]
            base = base_hi if high else base_lo
            wide = rows.shape[3]
            n_ld = 16 * (2 if first and wide > 2 else 1)
            with nc.Block() as block:
                @block.sync
                def _(sp):
                    with sp.Fori(0, IT) as it:
                        for b in range(2):
                            at = (it * 2 + b) * CH
                            wait_apart(sp, sc[b], it * (16 * CH) + START)
                            wait_apart(sp, s["r_idx"], it * 2 + b - 1 + START)
                            if first:
                                sp.dma_start(chunk_i[:, b], tiles(a["pairs"])[:, bass.ds(at, CH), :]).then_inc(ld[b], 16)
                                if wide > 2:
                                    sp.dma_start(rows[:, b, :, 2:W1], tiles(a["efeat"])[:, bass.ds(at, CH), :]).then_inc(ld[b], 16)
                            else:
                                sp.dma_start(rows[:, b], table_in.rearrange("(j p) w -> p j w", p=P)[:, bass.ds(at, CH), :]).then_inc(ld[b], 16)

                @block.vector
                def _(v):
                    link = Chain(v, s["r_chain"])
                    link(v.memset(oh[:, 3, 0:256], 0.0))
                    with v.Fori(0, IT) as it:
                        link.restart()
                        for b in range(2):
                            v.wait_ge(ld[b], (it + 1) * n_ld)
                            v.wait_ge(sc[b], it * (16 * CH) + START)
                            if first:
                                link(v.tensor_copy(rows[:, b, :, 0:1], chunk_i[:, b, :, key_col:key_col + 1]))
                                link(v.tensor_copy(rows[:, b, :, 1:2], chunk_i[:, b, :, 1 - key_col:2 - key_col]))
                            link(v.tensor_copy(digi[:, b], rows[:, b, :, 0]))
                            if high:
                                link(v.tensor_scalar(idx[:, b], digi[:, b], 8, None, ALU.logical_shift_right))
                            else:
                                link(v.tensor_scalar(idx[:, b], digi[:, b], 255, None, ALU.bitwise_and))
                            link(v.tensor_copy(digf[:, b], idx[:, b]))
                            def one_hot(t):
                                v.wait_ge(s["r_mm2"], (it * 2 + b) * CH + t - 2 + START)
                                v.tensor_scalar(oh[:, (b * CH + t) % 4, 0:256], iota_b[:], digf[:, b, t:t + 1], None,
                                                ALU.is_equal).then_inc(s["r_oh"], 1)
                            one_hot(0)
                            one_hot(1)
                            for t in range(CH):
                                n = (it * 2 + b) * CH + t
                                if t + 2 < CH:
                                    one_hot(t + 2)
                                v.wait_ge(s["r_mm1"], n + 1)
                                v.tensor_tensor_reduce(out=junk2[t % 2], in0=ps[(b * CH + t) % 2][:, 0:256],
                                                       in1=oh[:, (b * CH + t) % 4, 0:256],
                                                       scale=1.0, scalar=0.0, op0=ALU.mult, op1=ALU.add,
                                                       accum_out=rank[:, b, t:t + 1]).then_inc(s["r_used"], 1)
                            v.wait_ge(s["r_used"], (it * 2 + b + 1) * CH + START)
                            v.tensor_copy(idx[:, b], rank[:, b]).then_inc(s["r_idx"], 1)

                @block.tensor
                def _(pe):
                    pe.matmul(ps[0][:, 0:256], ident[:], base[:], start=True, stop=True)
                    pe.matmul(ps[1][:, 0:256], ident[:], base[:], start=True, stop=True)
                    with pe.Fori(0, IT) as it:
                        for t in range(2 * CH):
                            n = it * (2 * CH) + t
                            more = dict(start=False, stop=True, skip_group_check=True)
                            now, behind = ps[t % 2][:, 0:256], ps[1 - t % 2][:, 0:256]
                            pe.wait_ge(s["r_oh"], n + 1)
                            pe.matmul(now, before_b[:], oh[:, t % 4, 0:256], **more).then_inc(s["r_mm1"], 1)
                            pe.wait_ge(s["r_used"], n + START)
                            pe.matmul(behind, upto_b[:], oh[:, (t - 1) % 4, 0:256], **more)
                            pe.matmul(behind, ones_b[:], oh[:, t % 4, 0:256], **more).then_inc(s["r_mm2"], 1)

                @block.gpsimd
                def _(pool):
                    prime(pool, sc)
                    with pool.Fori(0, IT) as it:
                        for b in range(2):
                            wait_apart(pool, s["r_idx"], it * 2 + b + 1 + START)
                            for t in range(CH):
                                pool.indirect_dma_start(table_out[:, :], bass.IndirectOffsetOnAxis(ap=idx[:, b, t:t + 1], axis=0),
                                                        rows[:, b, t, :], None).then_inc(sc[b], 16)
                    pool.wait_ge(sc[0], IT * 16 * CH + START)
                    pool.wait_ge(sc[1], IT * 16 * CH + START)
            end_phase(nc, s)

        def take_order(table, width):
            s = phase(nc, ["t_ld0", "t_ld1", "t_edge", "t_dve", "t_chain"],
                      ["t_cp"])
            ld = [s["t_ld0"], s["t_ld1"]]
            rows = pay if width == W1 else pay2
            with nc.Block() as block:
                @block.sync
                def _(sp):
                    with sp.Fori(0, IT) as it:
                        for b in range(2):
                            wait_apart(sp, s["t_cp"], it * 2 + b - 1 + START)
                            sp.dma_start(rows[:, b], tiles(table)[:, bass.ds((it * 2 + b) * CH, CH), :]).then_inc(ld[b], 16)
                    sp.wait_ge(s["t_dve"], 1)
                    sp.dma_start(col[1:P, 0:1], keyf[0:P - 1, NT - 1:NT]).then_inc(s["t_edge"], 16)
                    sp.dma_start(col[0:P - 1, 1:2], keyf[1:P, 0:1]).then_inc(s["t_edge"], 16)

                @block.vector
                def _(v):
                    link = Chain(v, s["t_chain"])
                    with v.Fori(0, IT) as it:
                        for b in range(2):
                            at = bass.ds((it * 2 + b) * CH, CH)
                            v.wait_ge(ld[b], it * 16 + 16)
                            v.tensor_copy(keyf[:, at], rows[:, b, :, 0])
                            if width == W1:
                                v.tensor_copy(dist[:, at], rows[:, b, :, 2])
                            v.tensor_copy(farf[:, at], rows[:, b, :, 1]).then_inc(s["t_cp"], 1)
                    v.wait_ge(s["t_cp"], NCH + START)
                    link(v.memset(col[:, 0:2], -1.0))
                    link(v.tensor_copy(seg_idx[:], keyf[:]))
                    link(v.tensor_copy(far_idx[:], farf[:]))
                    v.sem_inc(s["t_dve"], 1)
                    v.wait_ge(s["t_edge"], 32)
                    link(v.tensor_tensor(same_prev[:, 1:NT], keyf[:, 1:NT], keyf[:, 0:NT - 1], ALU.is_equal))
                    link(v.tensor_tensor(same_prev[:, 0:1], keyf[:, 0:1], col[:, 0:1], ALU.is_equal))
                    link(v.tensor_copy(same_next[:, 0:NT - 1], same_prev[:, 1:NT]))
                    link(v.tensor_tensor(same_next[:, NT - 1:NT], keyf[:, NT - 1:NT], col[:, 1:2], ALU.is_equal))
                    link(v.tensor_tensor_scan(lead[:], same_prev[:], same_prev[:], 1.0, ALU.mult, ALU.min))
                    link(v.tensor_tensor_scan(trail[:, ::-1], same_next[:, ::-1], same_next[:, ::-1], 1.0, ALU.mult, ALU.min))
                    link(v.tensor_scalar(cut_prev[:], same_prev[:], -1.0, BIG, ALU.add, ALU.mult))
                    link(v.tensor_scalar(cut_next[:], same_next[:], -1.0, BIG, ALU.add, ALU.mult))
            end_phase(nc, s)

        def segment_scan(width, back=False, store=False):
            s = phase(nc, ["s_scan", "s_dve", "s_pe", "s_chain", "s_fix", "s_st"])
            same, reach = (same_next, trail) if back else (same_prev, lead)
            edge = 0 if back else NT - 1
            turn = slice(None, None, -1) if back else slice(None)
            with nc.Block() as block:
                @block.vector
                def _(v):
                    link = Chain(v, s["s_chain"])
                    if back:
                        for c in range(width):
                            g = G[:, turn, c]
                            v.tensor_tensor_scan(g, same[:, turn], g, 0.0, ALU.mult, ALU.add).then_inc(s["s_scan"], 1)
                    else:
                        with v.Fori(0, width) as c:
                            g = G[:, :, bass.ds(c, 1)].rearrange("p j a -> p (j a)")
                            v.tensor_tensor_scan(g, same[:], g, 0.0, ALU.mult, ALU.add).then_inc(s["s_scan"], 1)
                    v.wait_ge(s["s_scan"], width)
                    link(v.tensor_copy(col[:, 0:width], G[:, edge, 0:width]))
                    link(v.tensor_copy(tmp[:, 0, 0:width], reach[:, edge:edge + 1].to_broadcast([P, width])))
                    v.sem_inc(s["s_dve"], 1)
                    v.wait_ge(s["s_pe"], 1)
                    link(v.tensor_copy(row[0:width, 0, :], ps[0][0:width, 0:P]))
                    link(v.tensor_copy(row[0:width, 1, :], ps[1][0:width, 0:P]))
                    link(v.memset(row[0:width, 2, :], 0.0))
                    into, of = (slice(0, P - 1), slice(1, P)) if back else (slice(1, P), slice(0, P - 1))
                    link(v.tensor_tensor_scan(row[0:width, 2, into][:, turn], row[0:width, 1, of][:, turn],
                                              row[0:width, 0, of][:, turn], 0.0, ALU.mult, ALU.add))
                    v.sem_inc(s["s_dve"], 1)
                    v.wait_ge(s["s_pe"], 2)
                    link(v.tensor_copy(col[:, 0:width], ps[2][:, 0:width]))
                    with v.Fori(0, width) as c:
                        g = G[:, :, bass.ds(c, 1)].rearrange("p j a -> p (j a)")
                        v.scalar_tensor_tensor(g, reach[:], col[:, bass.ds(c, 1)], g, ALU.mult, ALU.add).then_inc(s["s_fix"], 1)

                @block.tensor
                def _(pe):
                    pe.wait_ge(s["s_dve"], 1)
                    pe.transpose(ps[0][0:width, 0:P], col[:, 0:width], ident[:])
                    pe.transpose(ps[1][0:width, 0:P], tmp[:, 0, 0:width], ident[:]).then_inc(s["s_pe"], 1)
                    pe.wait_ge(s["s_dve"], 2)
                    pe.transpose(ps[2][:, 0:width], row[0:width, 2, :], ident[0:width, 0:width]).then_inc(s["s_pe"], 1)

                if store:
                    @block.sync
                    def _(sp):
                        sp.wait_ge(s["s_fix"], width)
                        sp.dma_start(tiles(d_seg), G[:, :, :]).then_inc(s["s_st"], 16)
                        sp.wait_ge(s["s_st"], 16)
            end_phase(nc, s)

        def element_slots():
            s = phase(nc, ["a_ld", "a_chain"])
            with nc.Block() as block:
                @block.sync
                def _(sp):
                    sp.dma_start(G[:, :, 0:GE + 1], tiles(d_slot)[:, :, H:SLW]).then_inc(s["a_ld"], 16)

                @block.vector
                def _(v):
                    link = Chain(v, s["a_chain"])
                    v.wait_ge(s["a_ld"], 16)
                    link(v.tensor_copy(node_i[:].unsqueeze(2), G[:, :, GE:GE + 1]))
                    link(v.tensor_tensor(G[:, :, 0:GE], G[:, :, 0:GE], bc(is_end[:], GE), ALU.mult))
            end_phase(nc, s)

        def softmax_weights():
            s = phase(nc, ["m_dve", "m_pe", "m_act", "m_chain"])
            rev = slice(None, None, -1)
            with nc.Block() as block:
                @block.vector
                def _(v):
                    link = Chain(v, s["m_chain"])
                    link(v.tensor_tensor(score[:], score[:], logm[:], ALU.add))
                    link(v.tensor_tensor_scan(scanf[:], cut_prev[:], score[:], -BIG, ALU.add, ALU.max))
                    link(v.tensor_tensor_scan(scanb[:, rev], cut_next[:, rev], score[:, rev], -BIG, ALU.add, ALU.max))
                    link(v.tensor_copy(col[:, 0:1], scanf[:, NT - 1:NT]))
                    link(v.tensor_copy(col[:, 1:2], scanb[:, 0:1]))
                    link(v.tensor_scalar(col[:, 2:3], lead[:, NT - 1:NT], -1.0, BIG, ALU.add, ALU.mult))
                    link(v.tensor_scalar(col[:, 3:4], trail[:, 0:1], -1.0, BIG, ALU.add, ALU.mult))
                    v.sem_inc(s["m_dve"], 1)
                    v.wait_ge(s["m_pe"], 1)
                    for n in range(4):
                        link(v.tensor_copy(row[0:1, n, :], ps[n][0:1, 0:P]))
                    link(v.memset(rowc[0:1, :, :], -BIG))
                    link(v.tensor_tensor_scan(rowc[0:1, 0, 1:P], row[0:1, 2, 0:P - 1], row[0:1, 0, 0:P - 1], -BIG, ALU.add, ALU.max))
                    link(v.tensor_tensor_scan(rowc[0:1, 1, 0:P - 1][:, rev], row[0:1, 3, 1:P][:, rev], row[0:1, 1, 1:P][:, rev],
                                              -BIG, ALU.add, ALU.max))
                    v.sem_inc(s["m_dve"], 1)
                    v.wait_ge(s["m_pe"], 2)
                    link(v.tensor_copy(col[:, 4:5], ps[0][:, 0:1]))
                    link(v.tensor_copy(col[:, 5:6], ps[1][:, 0:1]))
                    link(v.tensor_tensor_scan(scanf[:], cut_prev[:], score[:], col[:, 4:5], ALU.add, ALU.max))
                    link(v.tensor_tensor_scan(scanb[:, rev], cut_next[:, rev], score[:, rev], col[:, 5:6], ALU.add, ALU.max))
                    link(v.tensor_tensor(scanf[:], scanf[:], scanb[:], ALU.max))
                    link(v.tensor_tensor(score[:], score[:], scanf[:], ALU.subtract))
                    link(v.tensor_scalar(score[:], score[:], 20.0, None, ALU.min))
                    v.sem_inc(s["m_dve"], 1)
                    v.wait_ge(s["m_act"], 1)
                    link(v.tensor_tensor(G[:, :, 0:H], G[:, :, 0:H], bc(scanb[:], H), ALU.mult))
                    link(v.tensor_copy(G[:, :, H:HC], scanb[:].unsqueeze(2)))

                @block.scalar
                def _(act):
                    act.wait_ge(s["m_dve"], 3)
                    act.activation(scanb[:], score[:], ACT.Exp).then_inc(s["m_act"], 1)
                    act.wait_ge(s["m_act"], 1)

                @block.tensor
                def _(pe):
                    pe.wait_ge(s["m_dve"], 1)
                    for n in range(4):
                        last = pe.transpose(ps[n][0:1, 0:P], col[:, n:n + 1], ident[:])
                    last.then_inc(s["m_pe"], 1)
                    pe.wait_ge(s["m_dve"], 2)
                    pe.transpose(ps[0][:, 0:1], rowc[0:1, 0, :], ident[0:1, 0:1])
                    pe.transpose(ps[1][:, 0:1], rowc[0:1, 1, :], ident[0:1, 0:1]).then_inc(s["m_pe"], 1)
            end_phase(nc, s)

        def first_messages():
            s = phase(nc, ["f_ld0", "f_ld1", "f_p0", "f_p1", "f_tr", "f_cp", "f_z", "f_silu", "f_gate", "f_ix", "f_chain", "f_achain", "f_act2", "f_init", "f_g0", "f_g1"],
                      ["f_done", "f_dve"])
            ld, g, pk = [s["f_ld0"], s["f_ld1"]], [s["f_g0"], s["f_g1"]], [s["f_p0"], s["f_p1"]]
            with nc.Block() as block:
                @block.sync
                def _(sp):
                    sp.dma_start(gb[:, 0, :], a["F2b"].partition_broadcast(P)).then_inc(s["f_init"], 16)
                    with sp.Fori(0, IT) as it:
                        for b in range(2):
                            wait_apart(sp, s["f_done"], it * 2 + b - 1 + START)
                            sp.dma_start(bufB[:, b, :, 0:RBF], tiles(d_edges)[:, bass.ds((it * 2 + b) * CH, CH), 3:W1]).then_inc(ld[b], 16)

                @block.gpsimd
                def _(pool):
                    with pool.Fori(0, IT) as it:
                        for b in range(2):
                            at = bass.ds((it * 2 + b) * CH, CH)
                            pool.wait_ge(s["f_done"], it * 2 + b - 1 + START)
                            pool.tensor_copy(chunk_i[:, b, :, 0:1], far_idx[:, at].unsqueeze(2)).then_inc(pk[b], 1)
                            wait_apart(pool, pk[b], it + 1)
                            for t in range(CH):
                                pool.indirect_dma_start(bufA[:, b, t, 0:NTW], None, d_node[:, :],
                                                        bass.IndirectOffsetOnAxis(ap=chunk_i[:, b, t, 0:1], axis=0)).then_inc(g[b], 16)

                @block.tensor
                def _(pe):
                    with pe.Fori(0, IT) as it:
                        for b in range(2):
                            n = it * 2 + b
                            wait_apart(pe, ld[b], it * 16 + 16)
                            for q in range(4):
                                k = min(4, CH - 4 * q)
                                for t in range(4 * q, 4 * q + k):
                                    last = pe.transpose(psw[0:RBF, q, (t % 4) * P:(t % 4 + 1) * P], bufB[:, b, t, 0:RBF], ident[:])
                            last.then_inc(s["f_tr"], 1)
                            wait_apart(pe, s["f_cp"], n + 1)
                            wait_apart(pe, s["f_dve"], n + START)
                            for q in range(4):
                                k = min(4, CH - 4 * q) * P
                                last = pe.matmul(psm[0:H, q, 0:k], f1w[:], xT[0:RBF, q * 512:q * 512 + k], start=True, stop=True)
                            last.then_inc(s["f_z"], 1)
                            wait_apart(pe, s["f_silu"], n + 1)
                            for t in range(CH):
                                last = pe.matmul(psm[:, t // 8, (t % 8) * 64:(t % 8) * 64 + H], sT[0:H, t * P:(t + 1) * P], f2w[:],
                                                 start=True, stop=True)
                            last.then_inc(s["f_gate"], 1)

                @block.scalar
                def _(act):
                    link = Chain(act, s["f_achain"])
                    act.wait_ge(s["f_ix"], 1)
                    act.activation(cw[:], cw[:], ACT.Sin).then_inc(s["f_act2"], 1)
                    with act.Fori(0, IT) as it:
                        link.restart()
                        for b in range(2):
                            n = it * 2 + b
                            act.wait_ge(s["f_tr"], n + 1)
                            for q in range(4):
                                k = min(4, CH - 4 * q) * P
                                link(act.copy(xT[0:RBF, q * 512:q * 512 + k], psw[0:RBF, q, 0:k]))
                            act.sem_inc(s["f_cp"], 1)
                            act.wait_ge(s["f_z"], n + 1)
                            for q in range(4):
                                k = min(4, CH - 4 * q) * P
                                link(act.activation(sT[0:H, q * 512:q * 512 + k], psm[0:H, q, 0:k], ACT.Silu, bias=f1b[:]))
                            act.sem_inc(s["f_silu"], 1)
                    act.wait_ge(s["f_ix"], 2)
                    act.activation(logm[:], logm[:], ACT.Ln).then_inc(s["f_act2"], 1)

                @block.vector
                def _(v):
                    link = Chain(v, s["f_chain"])
                    v.wait_ge(s["f_init"], 16)
                    link(v.tensor_scalar(cw[:], dist[:], CUT, -PI / (2 * CUT), ALU.min, ALU.mult))
                    link(v.tensor_scalar(cw[:], cw[:], PI / 2, None, ALU.add))
                    v.sem_inc(s["f_ix"], 1)
                    v.wait_ge(s["f_act2"], 1)
                    link(v.tensor_tensor(cw[:], cw[:], cw[:], ALU.mult))
                    link(v.tensor_scalar(dist[:], dist[:], CUT, None, ALU.is_lt))
                    link(v.tensor_tensor(cw[:], cw[:], dist[:], ALU.mult))
                    with v.Fori(0, IT) as it:
                        link.restart()
                        for b in range(2):
                            n = it * 2 + b
                            at = bass.ds(n * CH, CH)
                            v.wait_ge(g[b], (it + 1) * (16 * CH))
                            link(v.tensor_tensor(tmp[:, :, 0:GE], bufA[:, b, :, H:H + GE], G[:, at, 0:GE], ALU.mult))
                            link(v.tensor_reduce(col[:, 0:CH], tmp[:, :, 0:GE], AX.X, ALU.add))
                            link(v.tensor_copy(col[:, CH:2 * CH], bufA[:, b, :, NTW - 2]))
                            link(v.tensor_copy(farf[:, at].unsqueeze(2), bufA[:, b, :, NTW - 1:NTW]))
                            link(v.tensor_copy(G[:, at, H:HC], col[:, CH:2 * CH].unsqueeze(2)))
                            link(v.tensor_tensor(col[:, CH:2 * CH], col[:, CH:2 * CH], cw[:, at], ALU.mult))
                            v.wait_ge(s["f_gate"], n + 1)
                            for q, k in ((0, 8), (1, CH - 8)):
                                link(v.tensor_tensor(tmp[:, 8 * q:8 * q + k, 0:H],
                                                     psm[:, q, 0:64 * k].rearrange("p (t c) -> p t c", c=64)[:, :, 0:H],
                                                     bcm(gb[:, 0, :], k), ALU.add))
                            v.sem_inc(s["f_dve"], 1)
                            link(v.tensor_tensor(tmp[:, :, 0:H], tmp[:, :, 0:H], bc(col[:, 0:CH], H), ALU.add))
                            link(v.tensor_tensor(tmp[:, :, 0:H], tmp[:, :, 0:H], bufA[:, b, :, 0:H], ALU.mult))
                            link(v.tensor_tensor(G[:, at, 0:H], tmp[:, :, 0:H], bc(col[:, CH:2 * CH], H), ALU.mult))
                            v.sem_inc(s["f_done"], 1)
                    link(v.tensor_copy(far_idx[:], farf[:]))
                    link(v.tensor_scalar(logm[:].unsqueeze(2), G[:, :, H:HC], 1.0, None, ALU.max))
                    v.sem_inc(s["f_ix"], 1)
                    v.wait_ge(s["f_act2"], 2)

            end_phase(nc, s)

        def layer_norm(v, both, sems, n, gain=None, bias=None, dst=None):
            rows = [slice(0, 8), slice(8, CH)]
            y = [tmp[:, r, 0:H] for r in rows]
            sq = [tmp2[:, r, 0:H] for r in rows]
            size = [8, CH - 8]
            both(lambda q: v.tensor_reduce(col[:, rows[q]], y[q], AX.X, ALU.add))
            both(lambda q: v.scalar_tensor_tensor(y[q], bc(col[:, rows[q]], H), -1.0 / H, y[q], ALU.mult, ALU.add))
            both(lambda q: v.tensor_tensor(sq[q], y[q], y[q], ALU.mult))
            both(lambda q: v.tensor_reduce(col[:, rows[q]], sq[q], AX.X, ALU.add))
            both.join()
            v.sem_inc(sems[0], 1)
            v.wait_ge(sems[1], n + 1)
            root = [col[:, CH:CH + 8], col[:, CH + 8:2 * CH]]
            both(lambda q: v.reciprocal(root[q], root[q]))
            if gain is None:
                both(lambda q: v.tensor_tensor(dst[:, rows[q]], y[q], bc(root[q], H), ALU.mult))
            else:
                both(lambda q: v.tensor_tensor(y[q], y[q], bc(root[q], H), ALU.mult))
                both(lambda q: v.tensor_tensor(y[q], y[q], bcm(gain, size[q]), ALU.mult))
                both(lambda q: v.tensor_tensor(dst[:, rows[q]], y[q], bcm(bias, size[q]), ALU.add))

        PARTS = [(q, min(4, CH - 4 * q)) for q in range(4)]
        HALVES = [(0, 8), (1, CH - 8)]

        def z_part(q, k):
            return psm[:, q, 0:64 * k].rearrange("p (t c) -> p t c", c=64)[:, :, 0:H]

        def node_step(mode, table_in, table_out, table_add=None, gain=None):
            s = phase(nc, ["u_ld0", "u_ld1", "u_ld2", "u_ld3", "u_ix0", "u_ix1", "u_g0", "u_g1", "u_st0", "u_st1", "u_tr", "u_z",
                           "u_leak", "u_var", "u_root", "u_chain", "u_achain"], ["u_hz", "u_done", "u_cp", "u_zread"])
            g, st, ix = [[s[k + "0"], s[k + "1"]] for k in ("u_g", "u_st", "u_ix")]
            ld = [s[f"u_ld{n}"] for n in range(RING)]
            product = mode in ("layer", "conv", "last")
            fetched = mode in ("conv", "last")
            n_ld = 16 * (1 + (table_add is not None))
            n_st = 16 * (CH if mode == "join" else 1)
            y = tmp[:, :, 0:H]
            wcol = col[:, 40:40 + CH]
            with nc.Block() as block:
                @block.sync
                def _(sp):
                    def load(n, b):
                        at = bass.ds(n * CH, CH)
                        sp.dma_start(hz[:, b, :, 0:H], tiles(table_in)[:, at, 0:H]).then_inc(ld[b], 16)
                        if table_add is not None:
                            sp.dma_start(bufD[:, b], tiles(table_add)[:, at, 0:H]).then_inc(ld[b], 16)
                    if mode != "join":
                        prime(sp, st)
                    for n in range(RING):
                        load(n, n)

                    def step(it, last):
                        for b in range(RING):
                            n = it * RING + b
                            if last:
                                sp.wait_ge(s["u_done"], n + 1 + START)
                            else:
                                wait_apart(sp, s["u_done"], n + 1 + START)
                            if mode != "join":
                                sp.dma_start(tiles(table_out)[:, bass.ds(n * CH, CH), :], bufC[:, b % 2]).then_inc(st[b % 2], 16)
                            if not last:
                                load(n + RING, b)
                    steps(sp, step, ST)
                    sp.wait_ge(st[0], IT * n_st + START)
                    sp.wait_ge(st[1], IT * n_st + START)

                @block.gpsimd
                def _(pool):
                    if fetched:
                        with pool.Fori(0, IT) as it:
                            for b in range(2):
                                n = it * 2 + b
                                pool.wait_ge(s["u_hz"], n - 1 + START)
                                pool.tensor_copy(idx[:, b], end_idx[:, bass.ds(n * CH, CH)]).then_inc(ix[b], 1)
                                wait_apart(pool, ix[b], it + 1)
                                for t in range(CH):
                                    pool.indirect_dma_start(bufA[:, b, t, 0:HC], None, d_seg[:, :],
                                                            bass.IndirectOffsetOnAxis(ap=idx[:, b, t:t + 1], axis=0)).then_inc(g[b], 16)
                    if mode == "join":
                        prime(pool, st)
                        with pool.Fori(0, IT) as it:
                            for b in range(2):
                                n = it * 2 + b
                                pool.wait_ge(s["u_done"], n + 1 + START)
                                pool.tensor_copy(idx[:, b], node_i[:, bass.ds(n * CH, CH)]).then_inc(ix[b], 1)
                                wait_apart(pool, ix[b], it + 1)
                                for t in range(CH):
                                    pool.indirect_dma_start(table_out[:, :], bass.IndirectOffsetOnAxis(ap=idx[:, b, t:t + 1], axis=0),
                                                            bufC[:, b, t, :], None).then_inc(st[b], 16)

                @block.vector
                def _(v):
                    both = Halves(v, s["u_chain"])
                    rows = [slice(0, 8), slice(8, CH)]
                    if mode in ("first", "layer"):
                        total = G[:, :, H:HC].rearrange("p t a -> p (t a)")
                        part = [slice(0, NT // 2), slice(NT // 2, NT)]
                        floor, op = (1e-8, ALU.max) if mode == "first" else (1e-10, ALU.add)
                        both(lambda q: v.tensor_tensor(weight[:, part[q]], total[:, part[q]], is_end[:, part[q]], ALU.mult))
                        both(lambda q: v.tensor_scalar(weight[:, part[q]], weight[:, part[q]], floor, None, op))
                        both(lambda q: v.reciprocal(weight[:, part[q]], weight[:, part[q]]))
                        both(lambda q: v.tensor_tensor(weight[:, part[q]], weight[:, part[q]], is_end[:, part[q]], ALU.mult))
                        both.join()

                    def half(n, q):
                        return bass.ds(n * CH + 8 * q, 8 if q == 0 else CH - 8)

                    def head(it, b):
                        n = it * RING + b
                        v.wait_ge(ld[b], (it + 1) * n_ld)
                        if fetched:
                            v.wait_ge(g[b % 2], (it * 2 + (b // 2 + 1)) * (16 * CH))
                            both(lambda q: v.tensor_tensor(hz[:, b, rows[q], H:2 * H], bufA[:, b % 2, rows[q], 0:H],
                                                           bc(has[:, half(n, q)], H), ALU.mult))
                        elif mode != "join":
                            both(lambda q: v.tensor_tensor(hz[:, b, rows[q], H:2 * H], G[:, half(n, q), 0:H],
                                                           bc(weight[:, half(n, q)], H), ALU.mult))
                        if mode != "join":
                            both.join()
                        v.sem_inc(s["u_hz"], 1)

                    def tail(it, b):
                        n = it * RING + b
                        y = [tmp[:, r, 0:H] for r in rows]
                        row = [hz[:, b, r, 0:H] for r in rows]
                        size = [8, CH - 8]
                        if mode == "layer":
                            v.wait_ge(s["u_leak"], n + 1)
                            both(lambda q: v.tensor_tensor(tmp2[:, rows[q], 0:H], z_part(q, size[q]), tmp2[:, rows[q], 0:H], ALU.max))
                            both(lambda q: v.tensor_tensor(y[q], tmp2[:, rows[q], 0:H], row[q], ALU.add))
                            v.sem_inc(s["u_zread"], 1)
                        elif product:
                            v.wait_ge(s["u_z"], n + 1)
                            both(lambda q: v.tensor_tensor(y[q], z_part(q, size[q]), bcm(gb[:, 7, :], size[q]), ALU.add))
                            both.join()
                            v.sem_inc(s["u_zread"], 1)
                            if mode == "last":
                                both(lambda q: v.tensor_tensor(y[q], y[q], bufD[:, b, rows[q]], ALU.add))
                        elif mode == "first":
                            both(lambda q: v.tensor_tensor(y[q], row[q], hz[:, b, rows[q], H:2 * H], ALU.add))
                        else:
                            both(lambda q: v.tensor_tensor(y[q], row[q], bufD[:, b, rows[q]], ALU.add))
                        v.wait_ge(st[b % 2], (it * 2 + b // 2) * n_st + START)
                        if mode == "conv":
                            both(lambda q: v.tensor_scalar(bufC[:, b % 2, rows[q]], y[q], 0.0, None, ALU.max))
                        else:
                            affine = gain is not None
                            layer_norm(v, both, (s["u_var"], s["u_root"]), n,
                                       gb[:, gain, :] if affine else None, gb[:, gain + 1, :] if affine else None, bufC[:, b % 2])
                        both.join()
                        v.sem_inc(s["u_done"], 1)

                    head(0, 0)

                    def step(it, last):
                        both.restart()
                        for b in range(RING):
                            if b + 1 < RING:
                                head(it, b + 1)
                            elif not last:
                                head(it + 1, 0)
                            tail(it, b)
                    steps(v, step, ST)

                @block.scalar
                def _(act):
                    link = Chain(act, s["u_achain"])

                    def copy(n):
                        act.wait_ge(s["u_tr"], n + 1)
                        if not isinstance(n, int) or n > 0:
                            act.wait_ge(s["u_z"], n)
                        for q, k in PARTS:
                            link(act.copy(xT[:, q * 512:q * 512 + k * P], psw[0:2 * H, q, 0:k * P]))
                        act.sem_inc(s["u_cp"], 1)

                    def leak(n):
                        act.wait_ge(s["u_z"], n + 1)
                        for q, k in HALVES:
                            link(act.mul(tmp2[:, 8 * q:8 * q + k, 0:H], z_part(q, k), 0.01))
                        act.sem_inc(s["u_leak"], 1)

                    if product:
                        copy(0)
                    if mode == "layer":
                        leak(0)

                    if mode != "conv":
                        link(act.activation(col[:, 60:61], eps[:], ACT.Sqrt))

                    def step(it, last):
                        link.restart()
                        for b in range(RING):
                            n = it * RING + b
                            more = not (last and b == RING - 1)
                            if product and more:
                                copy(n + 1)
                            if mode != "conv":
                                act.wait_ge(s["u_var"], n + 1)
                                link(act.activation(col[:, CH:2 * CH], col[:, 0:CH], ACT.Sqrt, bias=eps[:], scale=1.0 / H))
                                act.sem_inc(s["u_root"], 1)
                            if mode == "layer" and more:
                                leak(n + 1)
                    steps(act, step, ST)

                if product:
                    @block.tensor
                    def _(pe):
                        with pe.Fori(0, ST) as it:
                            for b in range(RING):
                                n = it * RING + b
                                wait_apart(pe, s["u_hz"], n + 1 + START)
                                wait_apart(pe, s["u_cp"], n + START)
                                for t in range(CH):
                                    last = pe.transpose(psw[0:2 * H, t // 4, (t % 4) * P:(t % 4 + 1) * P], hz[:, b, t, :], ident[:])
                                last.then_inc(s["u_tr"], 1)
                                wait_apart(pe, s["u_cp"], n + 1 + START)
                                wait_apart(pe, s["u_zread"], n + START)
                                for t in range(CH):
                                    last = pe.matmul(psm[:, t // 8, (t % 8) * 64:(t % 8) * 64 + H], xT[:, t * P:(t + 1) * P], wz[:],
                                                     start=True, stop=True)
                                last.then_inc(s["u_z"], 1)
            end_phase(nc, s)

        def qk_step():
            s = phase(nc, ["q_ld0", "q_ld1", "q_ld2", "q_ld3", "q_st0", "q_st1", "q_tr", "q_mm", "q_sq", "q_var", "q_root", "q_chain", "q_achain", "q_halves"],
                      ["q_done", "q_cp", "q_read"])
            ld, st = [s[f"q_ld{n}"] for n in range(RING)], [s["q_st0"], s["q_st1"]]

            def prod(q, k):
                return psm[:, q, 0:P * k].rearrange("p (t c) -> p t c", c=P)[:, :, 0:2 * H]
            with nc.Block() as block:
                @block.sync
                def _(sp):
                    def load(n, b):
                        sp.dma_start(hz[:, b, :, 0:H], tiles(d_h)[:, bass.ds(n * CH, CH), :]).then_inc(ld[b], 16)
                    prime(sp, st)
                    for n in range(RING):
                        load(n, n)

                    def step(it, last):
                        for b in range(RING):
                            n = it * RING + b
                            if last:
                                sp.wait_ge(s["q_done"], n + 1 + START)
                            else:
                                wait_apart(sp, s["q_done"], n + 1 + START)
                            sp.dma_start(tiles(d_kh)[:, bass.ds(n * CH, CH), 0:H], bufC[:, b % 2]).then_inc(st[b % 2], 16)
                            if not last:
                                load(n + RING, b)
                    steps(sp, step, ST)
                    sp.wait_ge(st[0], IT * 16 + START)
                    sp.wait_ge(st[1], IT * 16 + START)

                @block.tensor
                def _(pe):
                    with pe.Fori(0, ST) as it:
                        for b in range(RING):
                            n = it * RING + b
                            wait_apart(pe, ld[b], it * 16 + 16)
                            wait_apart(pe, s["q_cp"], n + START)
                            for t in range(CH):
                                last = pe.transpose(psw[0:H, t // 4, (t % 4) * P:(t % 4 + 1) * P], hz[:, b, t, 0:H], ident[:])
                            last.then_inc(s["q_tr"], 1)
                            wait_apart(pe, s["q_cp"], n + 1 + START)
                            wait_apart(pe, s["q_read"], n + START)
                            for t in range(CH):
                                last = pe.matmul(psm[:, t // 4, (t % 4) * P:(t % 4) * P + 2 * H], xT[0:H, t * P:(t + 1) * P], wqk[:],
                                                 start=True, stop=True)
                            last.then_inc(s["q_mm"], 1)

                @block.scalar
                def _(act):
                    link = Chain(act, s["q_achain"])
                    link(act.activation(col[:, 60:61], eps[:], ACT.Sqrt))
                    with act.Fori(0, IT) as it:
                        link.restart()
                        for b in range(2):
                            n = it * 2 + b
                            act.wait_ge(s["q_tr"], n + 1)
                            for q, k in PARTS:
                                link(act.copy(xT[0:H, q * 512:q * 512 + k * P], psw[0:H, q, 0:k * P]))
                            act.sem_inc(s["q_cp"], 1)
                            act.wait_ge(s["q_mm"], n + 1)
                            for q, k in PARTS:
                                link(act.activation(tmp2[:, 4 * q:4 * q + k, :], prod(q, k), ACT.Square))
                            act.sem_inc(s["q_sq"], 1)
                            act.wait_ge(s["q_var"], n + 1)
                            link(act.activation(col[:, 2 * CH:4 * CH], col[:, 0:2 * CH], ACT.Sqrt, bias=eps[:], scale=1.0 / H))
                            act.sem_inc(s["q_root"], 1)

                @block.vector
                def _(v):
                    link, both = Chain(v, s["q_chain"]), Halves(v, s["q_halves"])
                    rows = [slice(0, 8), slice(8, CH)]
                    size = [8, CH - 8]

                    def variance(n):
                        v.wait_ge(s["q_sq"], n + 1)
                        link(v.tensor_reduce(col[:, 0:2 * CH], tmp2[:, :, :].rearrange("p t (a c) -> p (t a) c", a=2), AX.X, ALU.add))
                        v.sem_inc(s["q_var"], 1)

                    def scaled(n, b):
                        v.wait_ge(s["q_root"], n + 1)
                        link(v.reciprocal(col[:, 0:2 * CH], col[:, 2 * CH:4 * CH]))
                        rstd = col[:, 0:2 * CH].rearrange("p (t a) -> p t a", a=2)
                        for q, k in PARTS:
                            r = slice(4 * q, 4 * q + k)
                            pair = tmps[:, b, r].rearrange("p t (a c) -> p t a c", a=2)
                            last = v.tensor_tensor(pair, prod(q, k).rearrange("p t (a c) -> p t a c", a=2),
                                                   bc(rstd[:, r, :], H), ALU.mult)
                        link(last)
                        v.sem_inc(s["q_read"], 1)

                    def finished(n, b, before):
                        t = tmps[:, b]
                        at = [bass.ds(n * CH, 8), bass.ds(n * CH + 8, CH - 8)]
                        both.restart()
                        both(lambda q: v.tensor_tensor(t[:, rows[q]], t[:, rows[q]], bcm(gains, size[q]), ALU.mult))
                        both(lambda q: v.tensor_tensor(t[:, rows[q]], t[:, rows[q]], bcm(biases, size[q]), ALU.add))

                        def split(q):
                            v.tensor_tensor(G[:, at[q], 0:H], t[:, rows[q], 0:H], bc(is_end[:, at[q]], H), ALU.mult)
                            return v.tensor_copy(bufC[:, b, rows[q]], t[:, rows[q], H:2 * H])
                        v.wait_ge(st[b], before * 16 + START)
                        both(split)
                        both.join()
                        v.sem_inc(s["q_done"], 1)

                    gains = gb[:, 0:2, :].rearrange("p a c -> p (a c)")
                    biases = gb[:, 2:4, :].rearrange("p a c -> p (a c)")
                    variance(0)
                    scaled(0, 0)
                    variance(1)
                    finished(0, 0, 0)
                    scaled(1, 1)
                    with v.Fori(1, IT) as it:
                        link.restart()
                        for b in range(2):
                            n = it * 2 + b
                            variance(n)
                            finished(n - 1, 1 - b, it - 1 + b)
                            scaled(n, b)
                    finished(NCH - 1, 1, IT - 1)
            end_phase(nc, s)

        def edge_step(table=None):
            s = phase(nc, ["e_ld0", "e_ld1", "e_g0", "e_g1", "e_ix0", "e_ix1", "e_chain"], ["e_done", "e_cp"])
            ld, g, ix = [s["e_ld0"], s["e_ld1"]], [s["e_g0"], s["e_g1"]], [s["e_ix0"], s["e_ix1"]]
            scored = table is None
            with nc.Block() as block:
                if scored:
                    @block.sync
                    def _(sp):
                        with sp.Fori(0, IT) as it:
                            for b in range(2):
                                n = it * 2 + b
                                wait_apart(sp, s["e_done"], n - 1 + START)
                                sp.dma_start(bufB[:, b, :, 0:RBF], tiles(d_edges)[:, bass.ds(n * CH, CH), 3:W1]).then_inc(ld[b], 16)

                @block.gpsimd
                def _(pool):
                    with pool.Fori(0, IT) as it:
                        for b in range(2):
                            n = it * 2 + b
                            pool.wait_ge(s["e_cp"], n - 1 + START)
                            pool.tensor_copy(idx[:, b], far_idx[:, bass.ds(n * CH, CH)]).then_inc(ix[b], 1)
                            wait_apart(pool, ix[b], it + 1)
                            for t in range(CH):
                                far = bass.IndirectOffsetOnAxis(ap=idx[:, b, t:t + 1], axis=0)
                                if scored:
                                    pool.indirect_dma_start(bufA[:, b, t, :], None, d_kh[:, :], far).then_inc(g[b], 16)
                                else:
                                    pool.indirect_dma_start(bufC[:, b, t, :], None, table[:, :], far).then_inc(g[b], 16)

                @block.scalar
                def _(act):
                    with act.Fori(0, IT) as it:
                        for b in range(2):
                            n = it * 2 + b
                            act.wait_ge(g[b], (it + 1) * (16 * CH))
                            if scored:
                                act.wait_ge(s["e_done"], n + 1 + START)
                            rows = bufA[:, b, :, H:2 * H] if scored else bufC[:, b]
                            act.copy(G[:, bass.ds(n * CH, CH), 0:H], rows).then_inc(s["e_cp"], 1)

                @block.vector
                def _(v):
                    link = Chain(v, s["e_chain"])
                    if not scored:
                        link(v.memset(G[:, :, H:HC], 0.0))
                        return
                    with v.Fori(0, IT) as it:
                        link.restart()
                        for b in range(2):
                            at = bass.ds((it * 2 + b) * CH, CH)
                            v.wait_ge(g[b], (it + 1) * (16 * CH))
                            v.wait_ge(ld[b], it * 16 + 16)
                            link(v.scalar_tensor_tensor(bufA[:, b, :, 0:RBF], bufB[:, b, :, 0:RBF], 0.1, bufA[:, b, :, 0:RBF], ALU.mult, ALU.add))
                            link(v.tensor_tensor(tmp[:, :, 0:H], bufA[:, b, :, 0:H], G[:, at, 0:H], ALU.mult))
                            link(v.tensor_reduce(score[:, at], tmp[:, :, 0:H], AX.X, ALU.add))
                            v.sem_inc(s["e_done"], 1)
            end_phase(nc, s)

        def load_rows(pairs, zrows=None):
            s = phase(nc, ["w_ld"])
            with nc.Block() as block:
                @block.sync
                def _(sp):
                    for n, src in pairs:
                        sp.dma_start(gb[:, n, :], src.partition_broadcast(P)).then_inc(s["w_ld"], 16)
                    for n, src in enumerate(zrows or []):
                        sp.dma_start(wz[n * H:(n + 1) * H, :], src).then_inc(s["w_ld"], 16)
                    sp.wait_ge(s["w_ld"], 16 * (len(pairs) + len(zrows or [])))
            end_phase(nc, s)

        def layer_weights(i):
            s = phase(nc, ["l_ld", "l_ch", "l_pe", "l_dve", "l_z"])

            def of(name):
                return a[name][bass.ds(i, 1)].rearrange("a k n -> (a k) n")

            def vec(name):
                return a[name][bass.ds(i, 1), :].rearrange("a n -> (a n)")
            with nc.Block() as block:
                @block.sync
                def _(sp):
                    sp.dma_start(wtmp[:, 0, :], of("Wq")).then_inc(s["l_ld"], 16)
                    sp.dma_start(wtmp[:, 1, :], of("Wk")).then_inc(s["l_ld"], 16)
                    sp.dma_start(wtmp[:, 2, :], of("Wm")).then_inc(s["l_ld"], 16)
                    sp.dma_start(wz[0:H, :], of("Wu")[0:H, :]).then_inc(s["l_ld"], 16)
                    sp.dma_start(wtmp[:, 3, :], of("Wu")[H:2 * H, :]).then_inc(s["l_ld"], 16)
                    for n, name in enumerate(("gq", "gk", "bq", "bk", "go", "bo")):
                        sp.dma_start(gb[:, n, :], vec(name).partition_broadcast(P)).then_inc(s["l_ld"], 16)
                    sp.wait_ge(s["l_dve"], 2)
                    sp.dma_start(wz[H:2 * H, :], xT[0:H, H:2 * H]).then_inc(s["l_z"], 16)
                    sp.wait_ge(s["l_z"], 16)

                @block.vector
                def _(v):
                    link = Chain(v, s["l_ch"])
                    v.wait_ge(s["l_ld"], 11 * 16)
                    link(v.tensor_reduce(col[0:H, 0:2], wtmp[:, 0:2, :], AX.X, ALU.add))
                    link(v.tensor_scalar(col[0:H, 0:2], col[0:H, 0:2], -1.0 / H, None, ALU.mult))
                    for n in range(2):
                        link(v.tensor_scalar(wqk[:, n * H:(n + 1) * H], wtmp[:, n, :], col[0:H, n:n + 1], None, ALU.add))
                    v.wait_ge(s["l_pe"], 1)
                    v.tensor_copy(xT[0:H, 0:H], ps[0][0:H, 0:H]).then_inc(s["l_dve"], 1)
                    v.wait_ge(s["l_pe"], 2)
                    v.tensor_copy(xT[0:H, H:2 * H], ps[1][0:H, 0:H]).then_inc(s["l_dve"], 1)

                @block.tensor
                def _(pe):
                    pe.wait_ge(s["l_ld"], 11 * 16)
                    pe.transpose(ps[0][0:H, 0:H], wtmp[:, 2, :], ident[0:H, 0:H]).then_inc(s["l_pe"], 1)
                    pe.wait_ge(s["l_dve"], 1)
                    pe.matmul(ps[1][0:H, 0:H], xT[0:H, 0:H], wtmp[:, 3, :], start=True, stop=True).then_inc(s["l_pe"], 1)
            end_phase(nc, s)

        histogram(a["src"])
        rank_pass(True, False, pay, None, d_half, 0)
        rank_pass(False, True, pay, d_half, d_edges, 0)
        take_order(d_edges, W1)
        make_slots()
        node_rows()
        element_slots()
        segment_scan(GE, back=True)
        first_messages()
        segment_scan(HC)
        load_rows([(0, a["gn"]), (1, a["bn"])])
        node_step("first", d_slot, d_h, gain=0)
        with nc.Fori(0, LAYERS) as layer:
            layer_weights(layer)
            qk_step()
            segment_scan(H, back=True)
            edge_step()
            softmax_weights()
            segment_scan(HC)
            node_step("layer", d_h, d_h, gain=4)
        node_step("join", d_slot, d_x1, table_add=d_h)
        histogram(a["dst"])
        rank_pass(True, False, pay2, None, d_half2, 1)
        rank_pass(False, True, pay2, d_half2, d_pairs, 1)
        take_order(d_pairs, 2)
        edge_step(d_x1)
        segment_scan(HC, store=True)
        load_rows([(7, a["b1"])], [a["w_root1"], a["w_rel1"]])
        node_step("conv", d_x1, d_y1)
        edge_step(d_y1)
        segment_scan(HC, store=True)
        load_rows([(7, a["b2"])], [a["w_root2"], a["w_rel2"]])
        node_step("last", d_y1, out, table_add=d_x1)


def kernel(**inputs):
    import numpy as np
    import concourse.bacc as bacc
    from concourse.bass_utils import run_bass_kernel_spmd

    def arr(name):
        return np.ascontiguousarray(inputs[name])

    def padded(v):
        return np.pad(v, [(0, NP - N)] + [(0, 0)] * (v.ndim - 1))
    ends = np.arange(N, NP, dtype=np.int32)
    src = np.concatenate([arr("src"), ends])
    dst = np.concatenate([arr("dst"), ends])
    arrays = {
        "x": padded(arr("x")), "src": src, "dst": dst, "pairs": np.stack([src, dst], 1),
        "efeat": np.concatenate([padded(arr("edge_weight"))[:, None], padded(arr("edge_attr_40"))], 1),
        "ntype": padded(arr("node_type_119")), "nvec": padded(arr("node_vec")),
    }
    for n in ("Wq", "gq", "bq", "Wk", "gk", "bk", "Wm", "Wu", "go", "bo", "F1W", "F1b", "F2W", "F2b", "gn", "bn", "emb", "adapt"):
        arrays[n] = arr("L0_gnn_" + n)
    for n in ("w_rel1", "w_root1", "b1", "w_rel2", "w_root2", "b2"):
        arrays[n] = arr("L1_gnn_" + n)
    nc = bacc.Bacc("TRN2", target_bir_lowering=False, num_devices=1)
    a = {n: nc.dram_tensor(f"in_{n}", v.shape, mybir.dt.from_np(v.dtype), kind="ExternalInput").ap() for n, v in arrays.items()}
    out = nc.dram_tensor("out", (NP, H), F32, kind="ExternalOutput").ap()
    gnn_kernel(nc, a, out)
    r = run_bass_kernel_spmd(nc, [{f"in_{n}": v for n, v in arrays.items()}], core_ids=[0])
    return r.results[0]["out"][:N]
```

```python
import concourse.bass as bass
from concourse import mybir
from contextlib import ExitStack
from itertools import count

P = 128
N = 50000
H = 48
RBF = 40
GE = 32
NELEM = 119
LAYERS = 4
NT = 392
NP = NT * P
CH = 14
NCH = NT // CH
IT = NCH // 2
RING = 4
ST = NCH // RING
HC = H + 1
W1 = 3 + RBF
NTW = H + GE + 2
SLW = H + GE + 1
CUT = 6.0
PI = 3.141592653589793
BIG = 1e30

F32 = mybir.dt.float32
I32 = mybir.dt.int32
BF16 = mybir.dt.bfloat16
ALU = mybir.AluOpType
ACT = mybir.ActivationFunctionType
AX = mybir.AxisListType


START = 16
PASSED = []
SERIAL = count()


class Chain:

    def __init__(self, eng, sem):
        self.eng, self.sem, self.n = eng, sem, 0

    def __call__(self, ins):
        self.n += 1
        ins.then_inc(self.sem, 1)
        self.eng.wait_ge(self.sem, self.n)

    def restart(self):
        self.eng.sem_clear(self.sem)
        self.n = 0


class Halves:

    def __init__(self, eng, sem):
        self.eng, self.sem, self.n, self.at = eng, sem, 0, [0, 0]

    def __call__(self, op):
        for q in range(2):
            if self.at[q]:
                self.eng.wait_ge(self.sem, self.at[q])
            self.n += 1
            op(q).then_inc(self.sem, 1)
            self.at[q] = self.n

    def join(self):
        self.eng.wait_ge(self.sem, self.n)

    def restart(self):
        self.eng.sem_clear(self.sem)
        self.n, self.at = 0, [0, 0]


def wait_apart(eng, sem, value):
    eng.wait_ge(sem, value)
    eng.sem_inc(PASSED[0], 1)


def phase(nc, names, early=()):
    sems = {n: nc.alloc_semaphore(f"{n}_{next(SERIAL)}") for n in (*names, *early)}
    for n in early:
        nc.sync.sem_inc(sems[n], START)
    if early:
        nc.all_engine_barrier()
    return sems


def end_phase(nc, sems):
    nc.clear_and_free_semaphores(list(sems.values()))
    nc.all_engine_barrier()


def gnn_kernel(nc, a, out):
    ctx = ExitStack()
    with ctx:
        def sb(name, shape, dt=F32):
            return ctx.enter_context(nc.sbuf_tensor(name, shape, dt))

        def dram(name, shape, dt=F32):
            return nc.dram_tensor(name, shape, dt).ap()

        d_half = dram("half_sorted1", [NP, W1])
        d_edges = dram("edges_by_src", [NP, W1])
        d_half2 = dram("half_sorted2", [NP, 2])
        d_pairs = dram("edges_by_dst", [NP, 2])
        d_elem = dram("element_rows", [NELEM, 2 * GE])
        d_node = dram("node_rows", [NP, NTW])
        d_slot = dram("slot_rows", [NP, SLW])
        d_place = dram("slot_places", [2 * NP, 1], I32)
        d_end = dram("last_edge", [65536], I32)
        d_has = dram("has_edges", [65536])
        d_seg = dram("scanned_rows", [NP, HC])
        d_kh = dram("k_h_rows", [NP, 2 * H])
        d_h = d_kh[:, H:2 * H]
        d_x1 = dram("x1_rows", [NP, H])
        d_y1 = dram("y1_rows", [NP, H])

        G = sb("G", [P, NT, HC])
        ident = sb("ident", [P, P])
        before = sb("before", [P, P])
        onesf = sb("onesf", [P, P])
        before_b = sb("before_b", [P, P], BF16)
        upto_b = sb("upto_b", [P, P], BF16)
        ones_b = sb("ones_b", [P, P], BF16)
        zeros_b = sb("zeros_b", [P, 512], BF16)
        iota_i = sb("iota_i", [P, 256], I32)
        iota_b = sb("iota_b", [P, 256], BF16)
        onesrow = sb("onesrow", [P, NT])
        base_lo = sb("base_lo", [P, 256])
        base_hi = sb("base_hi", [P, 256])
        seg_idx = sb("seg_idx", [P, NT], I32)
        far_idx = sb("far_idx", [P, NT], I32)
        end_idx = sb("end_idx", [P, NT], I32)
        has = sb("has", [P, NT])
        keyf = sb("keyf", [P, NT])
        farf = sb("farf", [P, NT])
        same_prev = sb("same_prev", [P, NT])
        same_next = sb("same_next", [P, NT])
        lead = sb("lead", [P, NT])
        trail = sb("trail", [P, NT])
        cut_prev = sb("cut_prev", [P, NT])
        cut_next = sb("cut_next", [P, NT])
        is_end = sb("is_end", [P, NT])
        pos_i = sb("pos_i", [P, NT], I32)
        slot_i = sb("slot_i", [P, NT], I32)
        node_i = sb("node_i", [P, NT], I32)
        dist = sb("dist", [P, NT])
        cw = sb("cw", [P, NT])
        logm = sb("logm", [P, NT])
        score = sb("score", [P, NT])
        scanf = sb("scanf", [P, NT])
        scanb = sb("scanb", [P, NT])
        bufA = sb("bufA", [P, 2, CH, 2 * H])
        hz = sb("hz", [P, RING, CH, 2 * H])
        bufD = sb("bufD", [P, RING, CH, H])
        bufB = bufD[:, 0:2]
        bufC = sb("bufC", [P, 2, CH, H])
        tmps = sb("tmps", [P, 2, CH, 2 * H])
        tmp = tmps[:, 0]
        weight = sb("weight", [P, NT])
        eps = sb("eps", [P, 1])
        tmp2 = sb("tmp2", [P, CH, 2 * H])
        sT = sb("sT", [H, CH * P])
        xT = sb("xT", [2 * H, CH * P])
        col = sb("col", [P, 64])
        row = sb("row", [64, 4, P])
        rowc = sb("rowc", [1, 2, P])
        chunk_i = sb("chunk_i", [P, 2, CH, 2], I32)
        idx = sb("idx", [P, 2, CH], I32)
        digi = sb("digi", [P, 2, CH], I32)
        digf = sb("digf", [P, 2, CH])
        rank = sb("rank", [P, 2, CH])
        primer = sb("primer", [16, 4])
        wqk = sb("wqk", [2 * H, 2, 2 * H])
        wz = sb("wz", [2 * H, H])
        wtmp = sb("wtmp", [2 * H, 4, H])
        gb = sb("gb", [P, 8, H])
        f1w = sb("f1w", [RBF, H])
        f2w = sb("f2w", [H, H])
        f1b = sb("f1b", [H, 1])
        psm = ctx.enter_context(nc.psum_tensor("psm", [P, 4, 512], F32))
        ps = [psm[:, n] for n in range(4)]
        psw = ctx.enter_context(nc.psum_tensor("psw", [P, 4, 512], F32))

        Gf = G[:, :, :].rearrange("p a b -> p (a b)")
        G_b = Gf.bitcast(BF16)
        oh = G_b[:, 0:2048].rearrange("p (b n) -> p b n", b=4)
        hist = Gf[:, 1024:1536]
        incl = Gf[:, 1536:2048]
        cnt = Gf[:, 2048:2560].rearrange("p (g n) -> p g n", g=2)
        cinc = Gf[:, 2560:3072].rearrange("p (g n) -> p g n", g=2)
        endf = Gf[:, 3072:3584].rearrange("p (g n) -> p g n", g=2)
        endi = Gf[:, 3584:4096].bitcast(I32).rearrange("p (g n) -> p g n", g=2)
        hasf = Gf[:, 4096:4608].rearrange("p (g n) -> p g n", g=2)
        key_i = Gf[:, 5000:5000 + NT].bitcast(I32)
        dg_i = Gf[:, 5400:5400 + NT].bitcast(I32)
        lof = Gf[:, 5800:5800 + NT]
        hif = Gf[:, 6200:6200 + NT]
        pay = Gf[:, 7000:7000 + 2 * CH * W1].rearrange("p (b t w) -> p b t w", b=2, w=W1)
        pay2 = Gf[:, 9000:9000 + 2 * CH * 2].rearrange("p (b t w) -> p b t w", b=2, w=2)

        def tiles(table):
            return table.rearrange("(p j) w -> p j w", p=P)

        def flat(v):
            return v.rearrange("(p j) -> p j", p=P)

        def bc(ap, n):
            return ap.unsqueeze(len(ap.shape)).to_broadcast(list(ap.shape) + [n])

        def bcm(ap, n=CH):
            return ap.unsqueeze(1).to_broadcast([ap.shape[0], n, ap.shape[1]])

        def prime(eng, sems):
            for n, sem in enumerate(sems):
                eng.dma_start(primer[:, n:n + 1], a["F1b"][0:16].rearrange("(p a) -> p a", a=1)).then_inc(sem, START)

        def prime2(eng, sems):
            for n, sem in enumerate(sems):
                eng.dma_start(primer[:, 2 + n:3 + n], a["F1b"][0:16].rearrange("(p a) -> p a", a=1)).then_inc(sem, START)

        PASSED[:] = [nc.alloc_semaphore("waits_passed")]
        s = phase(nc, ["c_pool", "c_dve", "c_ld", "c_dma", "c_pe", "c_chain", "c_pchain"])
        with nc.Block() as block:
            @block.gpsimd
            def _(pool):
                link = Chain(pool, s["c_pchain"])
                link(pool.iota(iota_i[:], [[1, 256]], base=0, channel_multiplier=0))
                link(pool.iota(pos_i[:], [[1, NT]], base=0, channel_multiplier=NT))
                link(pool.memset(ones_b[:], 1.0))
                link(pool.memset(onesf[:], 1.0))
                link(pool.memset(onesrow[:], 1.0))
                link(pool.memset(zeros_b[:], 0.0))
                link(pool.memset(eps[:], 1e-5))
                link(pool.memset(ident[:], 0.0))
                link(pool.affine_select(out=ident[:], in_=ident[:], compare_op=ALU.not_equal, fill=1.0,
                                        base=0, pattern=[[-1, P]], channel_multiplier=1))
                link(pool.affine_select(out=before[:], in_=onesf[:], compare_op=ALU.is_gt, fill=0.0,
                                        base=0, pattern=[[1, P]], channel_multiplier=-1))
                pool.sem_inc(s["c_pool"], 1)

            @block.vector
            def _(v):
                link = Chain(v, s["c_chain"])
                v.wait_ge(s["c_pool"], 1)
                link(v.tensor_copy(iota_b[:], iota_i[:]))
                link(v.tensor_copy(before_b[:], before[:]))
                link(v.tensor_scalar(upto_b[:], before[:], -1.0, 1.0, ALU.mult, ALU.add))
                v.sem_inc(s["c_dve"], 1)
                v.wait_ge(s["c_pe"], 1)
                v.tensor_copy(xT[0:GE, 0:NELEM], ps[0][0:GE, 0:NELEM]).then_inc(s["c_dve"], 1)
                v.wait_ge(s["c_pe"], 2)
                v.tensor_copy(bufA[0:NELEM, 0, 2, 0:GE], ps[1][0:NELEM, 0:GE]).then_inc(s["c_dve"], 1)

            @block.tensor
            def _(pe):
                pe.wait_ge(s["c_dve"], 1)
                pe.wait_ge(s["c_ld"], 32)
                pe.transpose(ps[0][0:GE, 0:NELEM], bufA[0:NELEM, 0, 0, 0:GE], ident[0:NELEM, 0:NELEM]).then_inc(s["c_pe"], 1)
                pe.wait_ge(s["c_dve"], 2)
                pe.matmul(ps[1][0:NELEM, 0:GE], xT[0:GE, 0:NELEM], bufA[0:GE, 0, 1, 0:GE],
                          start=True, stop=True).then_inc(s["c_pe"], 1)

            @block.sync
            def _(sp):
                sp.dma_start(bufA[0:NELEM, 0, 0, 0:GE], a["emb"]).then_inc(s["c_ld"], 16)
                sp.dma_start(bufA[0:GE, 0, 1, 0:GE], a["adapt"]).then_inc(s["c_ld"], 16)
                sp.dma_start(d_elem[:, 0:GE], a["emb"]).then_inc(s["c_dma"], 16)
                sp.dma_start(f1w[:], a["F1W"]).then_inc(s["c_dma"], 16)
                sp.dma_start(f2w[:], a["F2W"]).then_inc(s["c_dma"], 16)
                sp.dma_start(f1b[:], a["F1b"].rearrange("(p a) -> p a", a=1)).then_inc(s["c_dma"], 16)
                sp.wait_ge(s["c_dve"], 3)
                sp.dma_start(d_elem[:, GE:2 * GE], bufA[0:NELEM, 0, 2, 0:GE]).then_inc(s["c_dma"], 16)
                sp.wait_ge(s["c_dma"], 80)
        end_phase(nc, s)

        def steps(eng, body, count=IT):
            with eng.Fori(0, count - 1) as it:
                body(it, False)
            body(count - 1, True)

        def make_slots():
            s = phase(nc, ["p_dve", "p_pe", "p_chain"])
            with nc.Block() as block:
                @block.vector
                def _(v):
                    link = Chain(v, s["p_chain"])
                    link(v.tensor_scalar(is_end[:], same_next[:], -1.0, 1.0, ALU.mult, ALU.add))
                    link(v.tensor_scalar(cw[:], has[:], -1.0, 1.0, ALU.mult, ALU.add))
                    link(v.tensor_tensor_scan(scanf[:], onesrow[:], same_next[:], 0.0, ALU.mult, ALU.add))
                    link(v.tensor_tensor_scan(scanb[:], onesrow[:], cw[:], 0.0, ALU.mult, ALU.add))
                    link(v.tensor_copy(col[:, 0:1], scanf[:, NT - 1:NT]))
                    link(v.tensor_copy(col[:, 1:2], scanb[:, NT - 1:NT]))
                    v.sem_inc(s["p_dve"], 1)
                    v.wait_ge(s["p_pe"], 1)
                    link(v.tensor_copy(col[:, 2:4], ps[0][:, 0:2]))
                    for c, (scan, own) in enumerate(((scanf, same_next), (scanb, cw))):
                        link(v.scalar_tensor_tensor(scan[:], scan[:], col[:, 2 + c:3 + c], own[:], ALU.add, ALU.subtract))
                        link(v.tensor_tensor(scan[:], scan[:], own[:], ALU.mult))
                    link(v.tensor_copy(logm[:], pos_i[:]))
                    link(v.scalar_tensor_tensor(logm[:], logm[:], float(NP), is_end[:], ALU.add, ALU.mult))
                    link(v.tensor_tensor(seg_idx[:], scanf[:], logm[:], ALU.add))
                    link(v.tensor_copy(logm[:], end_idx[:]))
                    link(v.scalar_tensor_tensor(logm[:], logm[:], float(NP), has[:], ALU.add, ALU.mult))
                    link(v.tensor_tensor(node_i[:], scanb[:], logm[:], ALU.add))

                @block.tensor
                def _(pe):
                    pe.wait_ge(s["p_dve"], 1)
                    pe.matmul(ps[0][:, 0:2], before[:], col[:, 0:2], start=True, stop=True).then_inc(s["p_pe"], 1)
            end_phase(nc, s)

            s = phase(nc, ["p_sc0", "p_sc1", "p_g0", "p_g1", "p_ix", *HISTOGRAM], ["p_cp"])
            sc, g = [s["p_sc0"], s["p_sc1"]], [s["p_g0"], s["p_g1"]]
            with nc.Block() as block:
                @block.gpsimd
                def _(pool):
                    prime(pool, sc)
                    with pool.Fori(0, IT) as it:
                        for b in range(2):
                            at = bass.ds((it * 2 + b) * CH, CH)
                            pool.wait_ge(sc[b], it * (16 * CH) + START)
                            pool.tensor_copy(chunk_i[:, b, :, 0:1], pos_i[:, at].unsqueeze(2)).then_inc(s["p_ix"], 1)
                            pool.tensor_copy(idx[:, b], seg_idx[:, at]).then_inc(s["p_ix"], 1)
                            wait_apart(pool, s["p_ix"], it * 4 + 2 * b + 2)
                            for t in range(CH):
                                pool.indirect_dma_start(d_place[:, :], bass.IndirectOffsetOnAxis(ap=idx[:, b, t:t + 1], axis=0),
                                                        chunk_i[:, b, t, 0:1], None).then_inc(sc[b], 16)
                    pool.wait_ge(sc[0], IT * 16 * CH + START)
                    pool.wait_ge(sc[1], IT * 16 * CH + START)
                    with pool.Fori(0, IT) as it:
                        for b in range(2):
                            at = bass.ds((it * 2 + b) * CH, CH)
                            pool.wait_ge(s["p_cp"], it * 2 + b - 1 + START)
                            pool.tensor_copy(idx[:, b], node_i[:, at]).then_inc(s["p_ix"], 1)
                            wait_apart(pool, s["p_ix"], it * 2 + b + (4 * IT + 1))
                            for t in range(CH):
                                pool.indirect_dma_start(chunk_i[:, b, t, 1:2], None, d_place[:, :],
                                                        bass.IndirectOffsetOnAxis(ap=idx[:, b, t:t + 1], axis=0)).then_inc(g[b], 16)

                @block.sync
                def _(sp):
                    histogram_loads(sp, s, a["dst"])

                @block.tensor
                def _(pe):
                    histogram_products(pe, s)

                @block.vector
                def _(v):
                    histogram_counts(v, s)
                    with v.Fori(0, IT) as it:
                        for b in range(2):
                            v.wait_ge(g[b], (it + 1) * (16 * CH))
                            v.tensor_copy(slot_i[:, bass.ds((it * 2 + b) * CH, CH)].unsqueeze(2),
                                          chunk_i[:, b, :, 1:2]).then_inc(s["p_cp"], 1)
            end_phase(nc, s)

        def node_rows():
            s = phase(nc, ["n_ld", "n_oh", "n_tr", "n_ot", "n_z", "n_achain", "n_st0", "n_st1", "n_sc0", "n_sc1", "n_ix", "n_x0", "n_x1", "n_chain"], ["n_cp"])
            st, sc, xs = [[s[k + "0"], s[k + "1"]] for k in ("n_st", "n_sc", "n_x")]
            with nc.Block() as block:
                @block.sync
                def _(sp):
                    sp.dma_start(seg_idx[:], flat(a["ntype"])).then_inc(s["n_ld"], 16)
                    sp.dma_start(score[:], flat(a["nvec"])).then_inc(s["n_ld"], 16)
                    sp.dma_start(elem[:], d_elem[:, :]).then_inc(s["n_ld"], 16)
                    prime(sp, st)
                    with sp.Fori(0, IT) as it:
                        for b in range(2):
                            at = (it * 2 + b) * CH
                            wait_apart(sp, s["n_cp"], it * 2 + b - 1 + START)
                            sp.dma_start(bufB[:, b], tiles(a["x"])[:, bass.ds(at, CH), :]).then_inc(xs[b], 16)
                            sp.wait_ge(s["n_cp"], it * 2 + b + 1 + START)
                            sp.dma_start(tiles(d_node)[:, bass.ds(at, CH), :], node_row[b]).then_inc(st[b], 16)
                    sp.wait_ge(st[0], IT * 16 + START)
                    sp.wait_ge(st[1], IT * 16 + START)

                @block.gpsimd
                def _(pool):
                    prime2(pool, sc)
                    with pool.Fori(0, IT) as it:
                        for b in range(2):
                            n = it * 2 + b
                            pool.wait_ge(s["n_cp"], n + 1 + START)
                            pool.tensor_copy(chunk_i[:, b, :, 0:1], slot_i[:, bass.ds(n * CH, CH)].unsqueeze(2)).then_inc(s["n_ix"], 1)
                            wait_apart(pool, s["n_ix"], n + 1)
                            for t in range(CH):
                                pool.indirect_dma_start(d_slot[:, :], bass.IndirectOffsetOnAxis(ap=chunk_i[:, b, t, 0:1], axis=0),
                                                        slot_row[b][:, t, :], None).then_inc(sc[b], 16)
                    pool.wait_ge(sc[0], IT * 16 * CH + START)
                    pool.wait_ge(sc[1], IT * 16 * CH + START)

                @block.tensor
                def _(pe):
                    pe.wait_ge(s["n_ld"], 48)
                    with pe.Fori(0, IT) as it:
                        for b in range(2):
                            n = it * 2 + b
                            wait_apart(pe, s["n_oh"], n + 1)
                            for t in range(CH):
                                last = pe.transpose(psw[0:NELEM, t // 4, (t % 4) * P:(t % 4 + 1) * P], type_oh[:, t, :], ident[:])
                            last.then_inc(s["n_tr"], 1)
                            wait_apart(pe, s["n_ot"], n + 1)
                            wait_apart(pe, s["n_cp"], n + START)
                            for t in range(CH):
                                last = pe.matmul(psm[:, t // 8, (t % 8) * 2 * GE:(t % 8 + 1) * 2 * GE], type_ohT[:, t * P:(t + 1) * P], elem[:],
                                                 start=True, stop=True)
                            last.then_inc(s["n_z"], 1)

                @block.scalar
                def _(act):
                    link = Chain(act, s["n_achain"])
                    with act.Fori(0, IT) as it:
                        link.restart()
                        for b in range(2):
                            act.wait_ge(s["n_tr"], it * 2 + b + 1)
                            for q in range(4):
                                k = min(4, CH - 4 * q) * P
                                link(act.copy(type_ohT[:, q * 512:q * 512 + k], psw[0:NELEM, q, 0:k]))
                            act.sem_inc(s["n_ot"], 1)

                @block.vector
                def _(v):
                    link = Chain(v, s["n_chain"])
                    v.wait_ge(s["n_ld"], 48)
                    link(v.tensor_copy(typef, seg_idx[:]))
                    link(v.tensor_copy(iotaf, iota_i[:, 0:NELEM]))

                    def one_hot(n):
                        v.tensor_tensor(type_oh, bcm(iotaf), bc(typef[:, bass.ds(n * CH, CH)], NELEM), ALU.is_equal).then_inc(s["n_oh"], 1)

                    def step(it, last):
                        for b in range(2):
                            n = it * 2 + b
                            at = bass.ds(n * CH, CH)
                            v.wait_ge(s["n_tr"], n + 1)
                            if not (last and b):
                                one_hot(n + 1)
                            v.wait_ge(st[b], it * 16 + START)
                            v.wait_ge(sc[b], it * (16 * CH) + START)
                            v.tensor_copy(node_row[b][:, :, H + GE:H + GE + 1], score[:, at].unsqueeze(2))
                            v.tensor_copy(node_row[b][:, :, H + GE + 1:NTW], slot_i[:, at].unsqueeze(2))
                            v.tensor_copy(slot_row[b][:, :, H + GE:SLW], pos_i[:, at].unsqueeze(2))
                            v.wait_ge(xs[b], it * 16 + 16)
                            v.tensor_copy(node_row[b][:, :, 0:H], bufB[:, b])
                            v.tensor_copy(slot_row[b][:, :, 0:H], bufB[:, b])
                            v.wait_ge(s["n_z"], n + 1)
                            for q, k in ((0, 8), (1, CH - 8)):
                                both = psm[:, q, 0:2 * GE * k].rearrange("p (t c) -> p t c", c=2 * GE)
                                v.tensor_copy(slot_row[b][:, 8 * q:8 * q + k, H:H + GE], both[:, :, 0:GE])
                                done = v.tensor_copy(node_row[b][:, 8 * q:8 * q + k, H:H + GE], both[:, :, GE:2 * GE])
                            done.then_inc(s["n_cp"], 1)
                    one_hot(0)
                    steps(v, step)
            end_phase(nc, s)

        node_row = [Gf[:, 10000 + n * CH * NTW:10000 + (n + 1) * CH * NTW].rearrange("p (t w) -> p t w", w=NTW) for n in range(2)]
        type_oh = Gf[:, 0:CH * NELEM].rearrange("p (t e) -> p t e", e=NELEM)
        type_ohT = Gf[0:NELEM, 2000:2000 + CH * P]
        elem = Gf[0:NELEM, 4000:4000 + 2 * GE]
        iotaf = Gf[:, 4100:4100 + NELEM]
        typef = Gf[:, 4300:4300 + NT]
        slot_row = [Gf[:, 13000 + n * CH * SLW:13000 + (n + 1) * CH * SLW].rearrange("p (t w) -> p t w", w=SLW) for n in range(2)]

        HISTOGRAM = ["h_ld", "h_oh", "h_mm", "h_chain", "h_pe", "h_dve", "h_st"]

        def histogram_loads(sp, s, key):
            sp.dma_start(key_i[:], flat(key)).then_inc(s["h_ld"], 16)
            sp.wait_ge(s["h_dve"], 2)
            for g in range(2):
                at = slice(g * 32768, (g + 1) * 32768)
                sp.dma_start(d_end[at].rearrange("(p c) -> p c", p=P), endi[:, g]).then_inc(s["h_st"], 16)
                sp.dma_start(d_has[at].rearrange("(p c) -> p c", p=P), hasf[:, g]).then_inc(s["h_st"], 16)
            sp.wait_ge(s["h_st"], 64)
            sp.dma_start(end_idx[:], flat(d_end[0:NP])).then_inc(s["h_st"], 16)
            sp.dma_start(has[:], flat(d_has[0:NP])).then_inc(s["h_st"], 16)
            sp.wait_ge(s["h_st"], 96)

        def histogram_counts(v, s):
            link = Chain(v, s["h_chain"])
            v.wait_ge(s["h_ld"], 16)
            link(v.tensor_scalar(dg_i[:], key_i[:], 255, None, ALU.bitwise_and))
            link(v.tensor_copy(lof[:], dg_i[:]))
            link(v.tensor_scalar(dg_i[:], key_i[:], 8, None, ALU.logical_shift_right))
            link(v.tensor_copy(hif[:], dg_i[:]))
            with v.Fori(0, NT // 4) as it:
                for b in range(4):
                    t = it * 4 + b
                    v.wait_ge(s["h_mm"], t + 1)
                    v.tensor_scalar(oh[:, b, 0:256], iota_b[:], lof[:, bass.ds(t, 1)], None, ALU.is_equal)
                    v.tensor_scalar(oh[:, b, 256:512], iota_b[:], hif[:, bass.ds(t, 1)], None,
                                    ALU.is_equal).then_inc(s["h_oh"], 1)
            v.wait_ge(s["h_mm"], NT + 4)
            link(v.tensor_copy(hist[:], ps[0][:]))
            for at, base in ((0, base_lo), (256, base_hi)):
                r = slice(at, at + 256)
                link(v.tensor_tensor_scan(incl[:, r], onesrow[:, 0:256], hist[:, r], 0.0, ALU.mult, ALU.add))
                link(v.tensor_tensor(base[:], incl[:, r], hist[:, r], ALU.subtract))
            for g in range(2):
                link(v.tensor_copy(cnt[:, g], ps[1 + g][:, 0:256]))
                link(v.tensor_tensor_scan(cinc[:, g], onesrow[:, 0:256], cnt[:, g], 0.0, ALU.mult, ALU.add))
                link(v.tensor_copy(col[:, g:g + 1], cinc[:, g, 255:256]))
            v.sem_inc(s["h_dve"], 1)
            v.wait_ge(s["h_pe"], 1)
            link(v.tensor_copy(col[:, 2:4], ps[3][:, 0:2]))
            link(v.tensor_tensor(col[:, 3:4], col[:, 3:4], ps[3][:, 2:3], ALU.add))
            for g in range(2):
                link(v.tensor_scalar(endf[:, g], cinc[:, g], col[:, 2 + g:3 + g], -1.0, ALU.add, ALU.add))
                link(v.tensor_scalar(endi[:, g], endf[:, g], 0.0, None, ALU.max))
                link(v.tensor_scalar(hasf[:, g], cnt[:, g], 1.0, None, ALU.min))
            v.sem_inc(s["h_dve"], 1)

        def histogram_products(pe, s):
            pe.matmul(ps[0][:], ones_b[:], zeros_b[:], start=True, stop=True).then_inc(s["h_mm"], 1)
            pe.matmul(ps[1][:, 0:256], ones_b[:], zeros_b[:, 0:256], start=True, stop=True).then_inc(s["h_mm"], 2)
            pe.matmul(ps[2][:, 0:256], ones_b[:], zeros_b[:, 0:256], start=True, stop=True).then_inc(s["h_mm"], 1)
            with pe.Fori(0, NT // 4) as it:
                for b in range(4):
                    pe.wait_ge(s["h_oh"], it * 4 + b + 1)
                    more = dict(start=False, stop=True, skip_group_check=True)
                    pe.matmul(ps[0][:], ones_b[:], oh[:, b, :], **more)
                    pe.matmul(ps[1][:, 0:256], oh[:, b, 256:384], oh[:, b, 0:256], **more)
                    pe.matmul(ps[2][:, 0:256], oh[:, b, 384:512], oh[:, b, 0:256], **more).then_inc(s["h_mm"], 1)
            pe.wait_ge(s["h_dve"], 1)
            pe.matmul(ps[3][:, 0:2], before[:], col[:, 0:2], start=True, stop=True)
            pe.matmul(ps[3][:, 2:3], onesf[:], col[:, 0:1], start=True, stop=True).then_inc(s["h_pe"], 1)

        def histogram(key):
            s = phase(nc, HISTOGRAM)
            with nc.Block() as block:
                @block.sync
                def _(sp):
                    histogram_loads(sp, s, key)

                @block.vector
                def _(v):
                    histogram_counts(v, s)

                @block.tensor
                def _(pe):
                    histogram_products(pe, s)
            end_phase(nc, s)

        junk2 = [Gf[:, 4608:4864], Gf[:, 9200:9456]]

        def rank_pass(first, high, rows, table_in, table_out, key_col):
            s = phase(nc, ["r_ld0", "r_ld1", "r_oh", "r_mm1", "r_chain", "r_sc0", "r_sc1"],
                      ["r_mm2", "r_idx", "r_used"])
            ld, sc = [s["r_ld0"], s["r_ld1"]], [s["r_sc0"], s["r_sc1"]]
            base = base_hi if high else base_lo
            wide = rows.shape[3]
            n_ld = 16 * (2 if first and wide > 2 else 1)
            with nc.Block() as block:
                @block.sync
                def _(sp):
                    with sp.Fori(0, IT) as it:
                        for b in range(2):
                            at = (it * 2 + b) * CH
                            wait_apart(sp, sc[b], it * (16 * CH) + START)
                            wait_apart(sp, s["r_idx"], it * 2 + b - 1 + START)
                            if first:
                                sp.dma_start(chunk_i[:, b], tiles(a["pairs"])[:, bass.ds(at, CH), :]).then_inc(ld[b], 16)
                                if wide > 2:
                                    sp.dma_start(rows[:, b, :, 2:W1], tiles(a["efeat"])[:, bass.ds(at, CH), :]).then_inc(ld[b], 16)
                            else:
                                sp.dma_start(rows[:, b], table_in.rearrange("(j p) w -> p j w", p=P)[:, bass.ds(at, CH), :]).then_inc(ld[b], 16)

                @block.vector
                def _(v):
                    link = Chain(v, s["r_chain"])
                    link(v.memset(oh[:, 3, 0:256], 0.0))
                    with v.Fori(0, IT) as it:
                        link.restart()
                        for b in range(2):
                            v.wait_ge(ld[b], (it + 1) * n_ld)
                            v.wait_ge(sc[b], it * (16 * CH) + START)
                            if first:
                                link(v.tensor_copy(rows[:, b, :, 0:1], chunk_i[:, b, :, key_col:key_col + 1]))
                                link(v.tensor_copy(rows[:, b, :, 1:2], chunk_i[:, b, :, 1 - key_col:2 - key_col]))
                            link(v.tensor_copy(digi[:, b], rows[:, b, :, 0]))
                            if high:
                                link(v.tensor_scalar(idx[:, b], digi[:, b], 8, None, ALU.logical_shift_right))
                            else:
                                link(v.tensor_scalar(idx[:, b], digi[:, b], 255, None, ALU.bitwise_and))
                            link(v.tensor_copy(digf[:, b], idx[:, b]))
                            def one_hot(t):
                                v.wait_ge(s["r_mm2"], (it * 2 + b) * CH + t - 2 + START)
                                v.tensor_scalar(oh[:, (b * CH + t) % 4, 0:256], iota_b[:], digf[:, b, t:t + 1], None,
                                                ALU.is_equal).then_inc(s["r_oh"], 1)
                            one_hot(0)
                            one_hot(1)
                            for t in range(CH):
                                n = (it * 2 + b) * CH + t
                                if t + 2 < CH:
                                    one_hot(t + 2)
                                v.wait_ge(s["r_mm1"], n + 1)
                                v.tensor_tensor_reduce(out=junk2[t % 2], in0=ps[(b * CH + t) % 2][:, 0:256],
                                                       in1=oh[:, (b * CH + t) % 4, 0:256],
                                                       scale=1.0, scalar=0.0, op0=ALU.mult, op1=ALU.add,
                                                       accum_out=rank[:, b, t:t + 1]).then_inc(s["r_used"], 1)
                            v.wait_ge(s["r_used"], (it * 2 + b + 1) * CH + START)
                            v.tensor_copy(idx[:, b], rank[:, b]).then_inc(s["r_idx"], 1)

                @block.tensor
                def _(pe):
                    pe.matmul(ps[0][:, 0:256], ident[:], base[:], start=True, stop=True)
                    pe.matmul(ps[1][:, 0:256], ident[:], base[:], start=True, stop=True)
                    with pe.Fori(0, IT) as it:
                        for t in range(2 * CH):
                            n = it * (2 * CH) + t
                            more = dict(start=False, stop=True, skip_group_check=True)
                            now, behind = ps[t % 2][:, 0:256], ps[1 - t % 2][:, 0:256]
                            pe.wait_ge(s["r_oh"], n + 1)
                            pe.matmul(now, before_b[:], oh[:, t % 4, 0:256], **more).then_inc(s["r_mm1"], 1)
                            pe.wait_ge(s["r_used"], n + START)
                            pe.matmul(behind, upto_b[:], oh[:, (t - 1) % 4, 0:256], **more)
                            pe.matmul(behind, ones_b[:], oh[:, t % 4, 0:256], **more).then_inc(s["r_mm2"], 1)

                @block.gpsimd
                def _(pool):
                    prime(pool, sc)
                    with pool.Fori(0, IT) as it:
                        for b in range(2):
                            wait_apart(pool, s["r_idx"], it * 2 + b + 1 + START)
                            for t in range(CH):
                                pool.indirect_dma_start(table_out[:, :], bass.IndirectOffsetOnAxis(ap=idx[:, b, t:t + 1], axis=0),
                                                        rows[:, b, t, :], None).then_inc(sc[b], 16)
                    pool.wait_ge(sc[0], IT * 16 * CH + START)
                    pool.wait_ge(sc[1], IT * 16 * CH + START)
            end_phase(nc, s)

        def take_order(table, width):
            s = phase(nc, ["t_ld0", "t_ld1", "t_edge", "t_dve", "t_chain"],
                      ["t_cp"])
            ld = [s["t_ld0"], s["t_ld1"]]
            rows = pay if width == W1 else pay2
            with nc.Block() as block:
                @block.sync
                def _(sp):
                    with sp.Fori(0, IT) as it:
                        for b in range(2):
                            wait_apart(sp, s["t_cp"], it * 2 + b - 1 + START)
                            sp.dma_start(rows[:, b], tiles(table)[:, bass.ds((it * 2 + b) * CH, CH), :]).then_inc(ld[b], 16)
                    sp.wait_ge(s["t_dve"], 1)
                    sp.dma_start(col[1:P, 0:1], keyf[0:P - 1, NT - 1:NT]).then_inc(s["t_edge"], 16)
                    sp.dma_start(col[0:P - 1, 1:2], keyf[1:P, 0:1]).then_inc(s["t_edge"], 16)

                @block.vector
                def _(v):
                    link = Chain(v, s["t_chain"])
                    with v.Fori(0, IT) as it:
                        for b in range(2):
                            at = bass.ds((it * 2 + b) * CH, CH)
                            v.wait_ge(ld[b], it * 16 + 16)
                            v.tensor_copy(keyf[:, at], rows[:, b, :, 0])
                            if width == W1:
                                v.tensor_copy(dist[:, at], rows[:, b, :, 2])
                            v.tensor_copy(farf[:, at], rows[:, b, :, 1]).then_inc(s["t_cp"], 1)
                    v.wait_ge(s["t_cp"], NCH + START)
                    link(v.memset(col[:, 0:2], -1.0))
                    link(v.tensor_copy(seg_idx[:], keyf[:]))
                    link(v.tensor_copy(far_idx[:], farf[:]))
                    v.sem_inc(s["t_dve"], 1)
                    v.wait_ge(s["t_edge"], 32)
                    link(v.tensor_tensor(same_prev[:, 1:NT], keyf[:, 1:NT], keyf[:, 0:NT - 1], ALU.is_equal))
                    link(v.tensor_tensor(same_prev[:, 0:1], keyf[:, 0:1], col[:, 0:1], ALU.is_equal))
                    link(v.tensor_copy(same_next[:, 0:NT - 1], same_prev[:, 1:NT]))
                    link(v.tensor_tensor(same_next[:, NT - 1:NT], keyf[:, NT - 1:NT], col[:, 1:2], ALU.is_equal))
                    link(v.tensor_tensor_scan(lead[:], same_prev[:], same_prev[:], 1.0, ALU.mult, ALU.min))
                    link(v.tensor_tensor_scan(trail[:, ::-1], same_next[:, ::-1], same_next[:, ::-1], 1.0, ALU.mult, ALU.min))
                    link(v.tensor_scalar(cut_prev[:], same_prev[:], -1.0, BIG, ALU.add, ALU.mult))
                    link(v.tensor_scalar(cut_next[:], same_next[:], -1.0, BIG, ALU.add, ALU.mult))
            end_phase(nc, s)

        def segment_scan(width, back=False, store=False):
            s = phase(nc, ["s_scan", "s_dve", "s_pe", "s_chain", "s_fix", "s_st"])
            same, reach = (same_next, trail) if back else (same_prev, lead)
            edge = 0 if back else NT - 1
            some = 8 if width % 8 == 0 else 7
            turn = slice(None, None, -1) if back else slice(None)
            with nc.Block() as block:
                @block.vector
                def _(v):
                    link = Chain(v, s["s_chain"])
                    if back:
                        for c in range(width):
                            g = G[:, turn, c]
                            v.tensor_tensor_scan(g, same[:, turn], g, 0.0, ALU.mult, ALU.add).then_inc(s["s_scan"], 1)
                    else:
                        with v.Fori(0, width // some) as it:
                            for n in range(some):
                                g = G[:, :, bass.ds(it * some + n, 1)].rearrange("p j a -> p (j a)")
                                v.tensor_tensor_scan(g, same[:], g, 0.0, ALU.mult, ALU.add).then_inc(s["s_scan"], 1)
                    v.wait_ge(s["s_scan"], width)
                    link(v.tensor_copy(col[:, 0:width], G[:, edge, 0:width]))
                    link(v.tensor_copy(tmp[:, 0, 0:width], reach[:, edge:edge + 1].to_broadcast([P, width])))
                    v.sem_inc(s["s_dve"], 1)
                    v.wait_ge(s["s_pe"], 1)
                    link(v.tensor_copy(row[0:width, 0, :], ps[0][0:width, 0:P]))
                    link(v.tensor_copy(row[0:width, 1, :], ps[1][0:width, 0:P]))
                    link(v.memset(row[0:width, 2, :], 0.0))
                    into, of = (slice(0, P - 1), slice(1, P)) if back else (slice(1, P), slice(0, P - 1))
                    link(v.tensor_tensor_scan(row[0:width, 2, into][:, turn], row[0:width, 1, of][:, turn],
                                              row[0:width, 0, of][:, turn], 0.0, ALU.mult, ALU.add))
                    v.sem_inc(s["s_dve"], 1)
                    v.wait_ge(s["s_pe"], 2)
                    link(v.tensor_copy(col[:, 0:width], ps[2][:, 0:width]))
                    with v.Fori(0, width // some) as it:
                        for n in range(some):
                            g = G[:, :, bass.ds(it * some + n, 1)].rearrange("p j a -> p (j a)")
                            v.scalar_tensor_tensor(g, reach[:], col[:, bass.ds(it * some + n, 1)], g, ALU.mult, ALU.add).then_inc(s["s_fix"], 1)

                @block.tensor
                def _(pe):
                    pe.wait_ge(s["s_dve"], 1)
                    pe.transpose(ps[0][0:width, 0:P], col[:, 0:width], ident[:])
                    pe.transpose(ps[1][0:width, 0:P], tmp[:, 0, 0:width], ident[:]).then_inc(s["s_pe"], 1)
                    pe.wait_ge(s["s_dve"], 2)
                    pe.transpose(ps[2][:, 0:width], row[0:width, 2, :], ident[0:width, 0:width]).then_inc(s["s_pe"], 1)

                if store:
                    @block.sync
                    def _(sp):
                        sp.wait_ge(s["s_fix"], width)
                        sp.dma_start(tiles(d_seg), G[:, :, :]).then_inc(s["s_st"], 16)
                        sp.wait_ge(s["s_st"], 16)
            end_phase(nc, s)

        def element_slots():
            s = phase(nc, ["a_ld", "a_chain"])
            with nc.Block() as block:
                @block.sync
                def _(sp):
                    sp.dma_start(G[:, :, 0:GE + 1], tiles(d_slot)[:, :, H:SLW]).then_inc(s["a_ld"], 16)

                @block.vector
                def _(v):
                    link = Chain(v, s["a_chain"])
                    v.wait_ge(s["a_ld"], 16)
                    link(v.tensor_copy(node_i[:].unsqueeze(2), G[:, :, GE:GE + 1]))
                    link(v.tensor_tensor(G[:, :, 0:GE], G[:, :, 0:GE], bc(is_end[:], GE), ALU.mult))
            end_phase(nc, s)

        def softmax_weights():
            s = phase(nc, ["m_dve", "m_pe", "m_act", "m_chain"])
            rev = slice(None, None, -1)
            with nc.Block() as block:
                @block.vector
                def _(v):
                    link = Chain(v, s["m_chain"])
                    link(v.tensor_tensor(score[:], score[:], logm[:], ALU.add))
                    link(v.tensor_tensor_scan(scanf[:], cut_prev[:], score[:], -BIG, ALU.add, ALU.max))
                    link(v.tensor_tensor_scan(scanb[:, rev], cut_next[:, rev], score[:, rev], -BIG, ALU.add, ALU.max))
                    link(v.tensor_copy(col[:, 0:1], scanf[:, NT - 1:NT]))
                    link(v.tensor_copy(col[:, 1:2], scanb[:, 0:1]))
                    link(v.tensor_scalar(col[:, 2:3], lead[:, NT - 1:NT], -1.0, BIG, ALU.add, ALU.mult))
                    link(v.tensor_scalar(col[:, 3:4], trail[:, 0:1], -1.0, BIG, ALU.add, ALU.mult))
                    v.sem_inc(s["m_dve"], 1)
                    v.wait_ge(s["m_pe"], 1)
                    for n in range(4):
                        link(v.tensor_copy(row[0:1, n, :], ps[n][0:1, 0:P]))
                    link(v.memset(rowc[0:1, :, :], -BIG))
                    link(v.tensor_tensor_scan(rowc[0:1, 0, 1:P], row[0:1, 2, 0:P - 1], row[0:1, 0, 0:P - 1], -BIG, ALU.add, ALU.max))
                    link(v.tensor_tensor_scan(rowc[0:1, 1, 0:P - 1][:, rev], row[0:1, 3, 1:P][:, rev], row[0:1, 1, 1:P][:, rev],
                                              -BIG, ALU.add, ALU.max))
                    v.sem_inc(s["m_dve"], 1)
                    v.wait_ge(s["m_pe"], 2)
                    link(v.tensor_copy(col[:, 4:5], ps[0][:, 0:1]))
                    link(v.tensor_copy(col[:, 5:6], ps[1][:, 0:1]))
                    link(v.tensor_tensor_scan(scanf[:], cut_prev[:], score[:], col[:, 4:5], ALU.add, ALU.max))
                    link(v.tensor_tensor_scan(scanb[:, rev], cut_next[:, rev], score[:, rev], col[:, 5:6], ALU.add, ALU.max))
                    link(v.tensor_tensor(scanf[:], scanf[:], scanb[:], ALU.max))
                    link(v.tensor_tensor(score[:], score[:], scanf[:], ALU.subtract))
                    link(v.tensor_scalar(score[:], score[:], 20.0, None, ALU.min))
                    v.sem_inc(s["m_dve"], 1)
                    v.wait_ge(s["m_act"], 1)
                    link(v.tensor_tensor(G[:, :, 0:H], G[:, :, 0:H], bc(scanb[:], H), ALU.mult))
                    link(v.tensor_copy(G[:, :, H:HC], scanb[:].unsqueeze(2)))

                @block.scalar
                def _(act):
                    act.wait_ge(s["m_dve"], 3)
                    act.activation(scanb[:], score[:], ACT.Exp).then_inc(s["m_act"], 1)
                    act.wait_ge(s["m_act"], 1)

                @block.tensor
                def _(pe):
                    pe.wait_ge(s["m_dve"], 1)
                    for n in range(4):
                        last = pe.transpose(ps[n][0:1, 0:P], col[:, n:n + 1], ident[:])
                    last.then_inc(s["m_pe"], 1)
                    pe.wait_ge(s["m_dve"], 2)
                    pe.transpose(ps[0][:, 0:1], rowc[0:1, 0, :], ident[0:1, 0:1])
                    pe.transpose(ps[1][:, 0:1], rowc[0:1, 1, :], ident[0:1, 0:1]).then_inc(s["m_pe"], 1)
            end_phase(nc, s)

        def first_messages():
            s = phase(nc, ["f_ld0", "f_ld1", "f_p0", "f_p1", "f_cp", "f_z", "f_silu", "f_gate", "f_ix", "f_chain", "f_achain", "f_act2", "f_init", "f_g0", "f_g1"],
                      ["f_done", "f_dve", "f_tr"])
            ATTRS = [(q, min(4, CH - 4 * q) * P) for q in range(4)]
            ld, g, pk = [s["f_ld0"], s["f_ld1"]], [s["f_g0"], s["f_g1"]], [s["f_p0"], s["f_p1"]]
            with nc.Block() as block:
                @block.sync
                def _(sp):
                    sp.dma_start(gb[:, 0, :], a["F2b"].partition_broadcast(P)).then_inc(s["f_init"], 16)
                    with sp.Fori(0, IT) as it:
                        for b in range(2):
                            wait_apart(sp, s["f_tr"], it * 2 + b - 1 + START)
                            sp.dma_start(bufB[:, b, :, 0:RBF], tiles(d_edges)[:, bass.ds((it * 2 + b) * CH, CH), 3:W1]).then_inc(ld[b], 16)

                @block.gpsimd
                def _(pool):
                    with pool.Fori(0, IT) as it:
                        for b in range(2):
                            at = bass.ds((it * 2 + b) * CH, CH)
                            pool.wait_ge(s["f_done"], it * 2 + b - 1 + START)
                            pool.tensor_copy(chunk_i[:, b, :, 0:1], far_idx[:, at].unsqueeze(2)).then_inc(pk[b], 1)
                            wait_apart(pool, pk[b], it + 1)
                            for t in range(CH):
                                pool.indirect_dma_start(bufA[:, b, t, 0:NTW], None, d_node[:, :],
                                                        bass.IndirectOffsetOnAxis(ap=chunk_i[:, b, t, 0:1], axis=0)).then_inc(g[b], 16)

                @block.tensor
                def _(pe):
                    def turn(b, rounds):
                        wait_apart(pe, ld[b], rounds)
                        for t in range(CH):
                            last = pe.transpose(psw[0:RBF, t // 4, (t % 4) * P:(t % 4 + 1) * P], bufB[:, b, t, 0:RBF], ident[:])
                        last.then_inc(s["f_tr"], 1)

                    def step(it, last):
                        for b in range(2):
                            n = it * 2 + b
                            wait_apart(pe, s["f_cp"], n + 1)
                            wait_apart(pe, s["f_dve"], n + START)
                            for q, k in ATTRS:
                                done = pe.matmul(psm[0:H, q, 0:k], f1w[:], xT[0:RBF, q * 512:q * 512 + k], start=True, stop=True)
                            done.then_inc(s["f_z"], 1)
                            if not (last and b):
                                turn(1 - b, (it + b) * 16 + 16)
                            wait_apart(pe, s["f_silu"], n + 1)
                            for t in range(CH):
                                done = pe.matmul(psm[:, t // 8, (t % 8) * 64:(t % 8) * 64 + H], sT[0:H, t * P:(t + 1) * P], f2w[:],
                                                 start=True, stop=True)
                            done.then_inc(s["f_gate"], 1)
                    turn(0, 16)
                    steps(pe, step)

                @block.scalar
                def _(act):
                    link = Chain(act, s["f_achain"])
                    act.wait_ge(s["f_ix"], 1)
                    act.activation(cw[:], cw[:], ACT.Sin).then_inc(s["f_act2"], 1)

                    def copy(n):
                        act.wait_ge(s["f_tr"], n + 1 + START)
                        for q, k in ATTRS:
                            link(act.copy(xT[0:RBF, q * 512:q * 512 + k], psw[0:RBF, q, 0:k]))
                        act.sem_inc(s["f_cp"], 1)

                    def step(it, last):
                        link.restart()
                        for b in range(2):
                            n = it * 2 + b
                            act.wait_ge(s["f_z"], n + 1)
                            for q, k in ATTRS:
                                link(act.activation(sT[0:H, q * 512:q * 512 + k], psm[0:H, q, 0:k], ACT.Silu, bias=f1b[:]))
                            act.sem_inc(s["f_silu"], 1)
                            if not (last and b):
                                copy(n + 1)
                    copy(0)
                    steps(act, step)
                    act.wait_ge(s["f_ix"], 2)
                    act.activation(logm[:], logm[:], ACT.Ln).then_inc(s["f_act2"], 1)

                @block.vector
                def _(v):
                    link = Chain(v, s["f_chain"])
                    v.wait_ge(s["f_init"], 16)
                    link(v.tensor_scalar(cw[:], dist[:], CUT, -PI / (2 * CUT), ALU.min, ALU.mult))
                    link(v.tensor_scalar(cw[:], cw[:], PI / 2, None, ALU.add))
                    v.sem_inc(s["f_ix"], 1)
                    v.wait_ge(s["f_act2"], 1)
                    link(v.tensor_tensor(cw[:], cw[:], cw[:], ALU.mult))
                    link(v.tensor_scalar(dist[:], dist[:], CUT, None, ALU.is_lt))
                    link(v.tensor_tensor(cw[:], cw[:], dist[:], ALU.mult))
                    with v.Fori(0, IT) as it:
                        link.restart()
                        for b in range(2):
                            n = it * 2 + b
                            at = bass.ds(n * CH, CH)
                            v.wait_ge(g[b], (it + 1) * (16 * CH))
                            link(v.tensor_tensor(tmp[:, :, 0:GE], bufA[:, b, :, H:H + GE], G[:, at, 0:GE], ALU.mult))
                            link(v.tensor_reduce(col[:, 0:CH], tmp[:, :, 0:GE], AX.X, ALU.add))
                            link(v.tensor_copy(col[:, CH:2 * CH], bufA[:, b, :, NTW - 2]))
                            link(v.tensor_copy(farf[:, at].unsqueeze(2), bufA[:, b, :, NTW - 1:NTW]))
                            link(v.tensor_copy(G[:, at, H:HC], col[:, CH:2 * CH].unsqueeze(2)))
                            link(v.tensor_tensor(col[:, CH:2 * CH], col[:, CH:2 * CH], cw[:, at], ALU.mult))
                            v.wait_ge(s["f_gate"], n + 1)
                            for q, k in ((0, 8), (1, CH - 8)):
                                link(v.tensor_tensor(tmp[:, 8 * q:8 * q + k, 0:H],
                                                     psm[:, q, 0:64 * k].rearrange("p (t c) -> p t c", c=64)[:, :, 0:H],
                                                     bcm(gb[:, 0, :], k), ALU.add))
                            v.sem_inc(s["f_dve"], 1)
                            link(v.tensor_tensor(tmp[:, :, 0:H], tmp[:, :, 0:H], bc(col[:, 0:CH], H), ALU.add))
                            link(v.tensor_tensor(tmp[:, :, 0:H], tmp[:, :, 0:H], bufA[:, b, :, 0:H], ALU.mult))
                            link(v.tensor_tensor(G[:, at, 0:H], tmp[:, :, 0:H], bc(col[:, CH:2 * CH], H), ALU.mult))
                            v.sem_inc(s["f_done"], 1)
                    link(v.tensor_copy(far_idx[:], farf[:]))
                    link(v.tensor_scalar(logm[:].unsqueeze(2), G[:, :, H:HC], 1.0, None, ALU.max))
                    v.sem_inc(s["f_ix"], 1)
                    v.wait_ge(s["f_act2"], 2)

            end_phase(nc, s)

        PARTS = [(q, min(4, CH - 4 * q)) for q in range(4)]
        HALVES = [(0, 8), (1, CH - 8)]

        def z_part(b, q, k):
            return psm[:, 2 * (b % 2) + q, 0:64 * k].rearrange("p (t c) -> p t c", c=64)[:, :, 0:H]

        def node_step(mode, table_in, table_out, table_add=None, gain=None):
            s = phase(nc, ["u_ld0", "u_ld1", "u_ld2", "u_ld3", "u_ix0", "u_ix1", "u_g0", "u_g1", "u_st0", "u_st1", "u_tr", "u_z",
                           "u_leak", "u_centred", "u_sq", "u_var", "u_root", "u_chain", "u_achain"], ["u_hz", "u_done", "u_cp", "u_zread"])
            g, st, ix = [[s[k + "0"], s[k + "1"]] for k in ("u_g", "u_st", "u_ix")]
            ld = [s[f"u_ld{n}"] for n in range(RING)]
            product = mode in ("layer", "conv", "last")
            fetched = mode in ("conv", "last")
            n_ld = 16 * (1 + (table_add is not None))
            n_st = 16 * (CH if mode == "join" else 1)
            norm = mode != "conv"
            with nc.Block() as block:
                @block.sync
                def _(sp):
                    def load(n, b):
                        at = bass.ds(n * CH, CH)
                        sp.dma_start(hz[:, b, :, 0:H], tiles(table_in)[:, at, 0:H]).then_inc(ld[b], 16)
                        if table_add is not None:
                            sp.dma_start(bufD[:, b], tiles(table_add)[:, at, 0:H]).then_inc(ld[b], 16)
                    if mode != "join":
                        prime(sp, st)
                    for n in range(RING):
                        load(n, n)

                    def step(it, last):
                        for b in range(RING):
                            n = it * RING + b
                            if last:
                                sp.wait_ge(s["u_done"], n + 1 + START)
                            else:
                                wait_apart(sp, s["u_done"], n + 1 + START)
                                load(n + RING, b)
                            if mode != "join":
                                sp.dma_start(tiles(table_out)[:, bass.ds(n * CH, CH), :], bufC[:, b % 2]).then_inc(st[b % 2], 16)
                    steps(sp, step, ST)
                    sp.wait_ge(st[0], IT * n_st + START)
                    sp.wait_ge(st[1], IT * n_st + START)

                @block.gpsimd
                def _(pool):
                    if fetched:
                        with pool.Fori(0, IT) as it:
                            for b in range(2):
                                n = it * 2 + b
                                pool.wait_ge(s["u_hz"], n - 1 + START)
                                pool.tensor_copy(idx[:, b], end_idx[:, bass.ds(n * CH, CH)]).then_inc(ix[b], 1)
                                wait_apart(pool, ix[b], it + 1)
                                for t in range(CH):
                                    pool.indirect_dma_start(bufA[:, b, t, 0:HC], None, d_seg[:, :],
                                                            bass.IndirectOffsetOnAxis(ap=idx[:, b, t:t + 1], axis=0)).then_inc(g[b], 16)
                    if mode == "join":
                        prime(pool, st)
                        with pool.Fori(0, IT) as it:
                            for b in range(2):
                                n = it * 2 + b
                                pool.wait_ge(s["u_done"], n + 1 + START)
                                pool.tensor_copy(idx[:, b], node_i[:, bass.ds(n * CH, CH)]).then_inc(ix[b], 1)
                                wait_apart(pool, ix[b], it + 1)
                                for t in range(CH):
                                    pool.indirect_dma_start(table_out[:, :], bass.IndirectOffsetOnAxis(ap=idx[:, b, t:t + 1], axis=0),
                                                            bufC[:, b, t, :], None).then_inc(st[b], 16)

                @block.vector
                def _(v):
                    both = Halves(v, s["u_chain"])
                    rows = [slice(0, 8), slice(8, CH)]
                    if mode in ("first", "layer"):
                        total = G[:, :, H:HC].rearrange("p t a -> p (t a)")
                        part = [slice(0, NT // 2), slice(NT // 2, NT)]
                        floor, op = (1e-8, ALU.max) if mode == "first" else (1e-10, ALU.add)
                        both(lambda q: v.tensor_tensor(weight[:, part[q]], total[:, part[q]], is_end[:, part[q]], ALU.mult))
                        both(lambda q: v.tensor_scalar(weight[:, part[q]], weight[:, part[q]], floor, None, op))
                        both(lambda q: v.reciprocal(weight[:, part[q]], weight[:, part[q]]))
                        both(lambda q: v.tensor_tensor(weight[:, part[q]], weight[:, part[q]], is_end[:, part[q]], ALU.mult))
                        both.join()

                    def half(n, q):
                        return bass.ds(n * CH + 8 * q, 8 if q == 0 else CH - 8)

                    def head(it, b):
                        n = it * RING + b
                        v.wait_ge(ld[b], (it + 1) * n_ld)
                        if fetched:
                            v.wait_ge(g[b % 2], (it * 2 + (b // 2 + 1)) * (16 * CH))
                            both(lambda q: v.tensor_tensor(hz[:, b, rows[q], H:2 * H], bufA[:, b % 2, rows[q], 0:H],
                                                           bc(has[:, half(n, q)], H), ALU.mult))
                        elif mode != "join":
                            both(lambda q: v.tensor_tensor(hz[:, b, rows[q], H:2 * H], G[:, half(n, q), 0:H],
                                                           bc(weight[:, half(n, q)], H), ALU.mult))
                        if mode != "join":
                            both.join()
                        v.sem_inc(s["u_hz"], 1)

                    size = [8, CH - 8]
                    total_of, var_of = col[:, 3 * CH:4 * CH], col[:, 0:CH]

                    def root_of(b):
                        return col[:, (1 + b % 2) * CH:(2 + b % 2) * CH]

                    def y_of(b):
                        return [tmps[:, b % 2, r, 0:H] for r in rows]

                    def begin(it, b):
                        n = it * RING + b
                        y = y_of(b)
                        row = [hz[:, b, r, 0:H] for r in rows]
                        if mode == "layer":
                            v.wait_ge(s["u_leak"], n + 1)
                            both(lambda q: v.tensor_tensor(tmp2[:, rows[q], 0:H], z_part(b, q, size[q]), tmp2[:, rows[q], 0:H], ALU.max))
                            both(lambda q: v.tensor_tensor(y[q], tmp2[:, rows[q], 0:H], row[q], ALU.add))
                            v.sem_inc(s["u_zread"], 1)
                        elif product:
                            v.wait_ge(s["u_z"], n + 1)
                            both(lambda q: v.tensor_tensor(y[q], z_part(b, q, size[q]), bcm(gb[:, 7, :], size[q]), ALU.add))
                            both.join()
                            v.sem_inc(s["u_zread"], 1)
                            if mode == "last":
                                both(lambda q: v.tensor_tensor(y[q], y[q], bufD[:, b, rows[q]], ALU.add))
                        elif mode == "first":
                            both(lambda q: v.tensor_tensor(y[q], row[q], hz[:, b, rows[q], H:2 * H], ALU.add))
                        else:
                            both(lambda q: v.tensor_tensor(y[q], row[q], bufD[:, b, rows[q]], ALU.add))
                        if norm:
                            both(lambda q: v.tensor_reduce(total_of[:, rows[q]], y[q], AX.X, ALU.add))
                            both(lambda q: v.scalar_tensor_tensor(y[q], bc(total_of[:, rows[q]], H), -1.0 / H, y[q], ALU.mult, ALU.add))
                            both.join()
                            v.sem_inc(s["u_centred"], 1)

                    def variance(it, b):
                        v.wait_ge(s["u_sq"], it * RING + b + 1)
                        both(lambda q: v.tensor_reduce(var_of[:, rows[q]], tmp2[:, rows[q], H:2 * H], AX.X, ALU.add))
                        both.join()
                        v.sem_inc(s["u_var"], 1)

                    def finish(it, b):
                        n = it * RING + b
                        y, root, to = y_of(b), root_of(b), bufC[:, b % 2]
                        if norm:
                            v.wait_ge(s["u_root"], n + 1)
                            both(lambda q: v.reciprocal(root[:, rows[q]], root[:, rows[q]]))
                        v.wait_ge(st[b % 2], (it * 2 + b // 2) * n_st + START)
                        if not norm:
                            both(lambda q: v.tensor_scalar(to[:, rows[q]], y[q], 0.0, None, ALU.max))
                        elif gain is None:
                            both(lambda q: v.tensor_tensor(to[:, rows[q]], y[q], bc(root[:, rows[q]], H), ALU.mult))
                        else:
                            both(lambda q: v.tensor_tensor(y[q], y[q], bc(root[:, rows[q]], H), ALU.mult))
                            both(lambda q: v.tensor_tensor(y[q], y[q], bcm(gb[:, gain, :], size[q]), ALU.mult))
                            both(lambda q: v.tensor_tensor(to[:, rows[q]], y[q], bcm(gb[:, gain + 1, :], size[q]), ALU.add))
                        both.join()
                        v.sem_inc(s["u_done"], 1)

                    def later(part, it, b, last):
                        if b < RING:
                            part(it, b)
                        elif not last:
                            part(it + 1, b - RING)

                    head(0, 0)
                    head(0, 1)
                    if not fetched:
                        head(0, 2)
                    begin(0, 0)
                    if norm:
                        variance(0, 0)

                    def step(it, last):
                        both.restart()
                        for b in range(RING):
                            if fetched:
                                later(head, it, b + 2, last)
                            later(begin, it, b + 1, last)
                            if not fetched:
                                later(head, it, b + 3, last)
                            if norm:
                                later(variance, it, b + 1, last)
                            finish(it, b)
                    steps(v, step, ST)

                @block.scalar
                def _(act):
                    link = Chain(act, s["u_achain"])

                    def copy(n):
                        for q, k in PARTS:
                            act.wait_ge(s["u_tr"], n * 4 + q + 1)
                            act.copy(xT[:, q * 512:q * 512 + k * P], psw[0:2 * H, q, 0:k * P]).then_inc(s["u_cp"], 1)

                    def leak(n, b):
                        act.wait_ge(s["u_z"], n + 1)
                        for q, k in HALVES:
                            link(act.mul(tmp2[:, 8 * q:8 * q + k, 0:H], z_part(b, q, k), 0.01))
                        act.sem_inc(s["u_leak"], 1)

                    if product:
                        copy(0)
                    if mode == "layer":
                        leak(0, 0)
                    if product:
                        copy(1)
                    if norm:
                        link(act.activation(col[:, 60:61], eps[:], ACT.Sqrt))

                    def step(it, last):
                        link.restart()
                        for b in range(RING):
                            n = it * RING + b
                            if norm:
                                act.wait_ge(s["u_centred"], n + 1)
                                link(act.activation(tmp2[:, :, H:2 * H], tmps[:, b % 2, :, 0:H], ACT.Square))
                                act.sem_inc(s["u_sq"], 1)
                                act.wait_ge(s["u_var"], n + 1)
                                link(act.activation(col[:, (1 + b % 2) * CH:(2 + b % 2) * CH], col[:, 0:CH], ACT.Sqrt,
                                                    bias=eps[:], scale=1.0 / H))
                                act.sem_inc(s["u_root"], 1)
                            if mode == "layer" and not (last and b + 1 == RING):
                                leak(n + 1, b + 1)
                            if product and not (last and b + 2 >= RING):
                                copy(n + 2)
                    steps(act, step, ST)

                if product:
                    @block.tensor
                    def _(pe):
                        def turn(b, q, k):
                            for t in range(4 * q, 4 * q + k):
                                last = pe.transpose(psw[0:2 * H, q, (t % 4) * P:(t % 4 + 1) * P], hz[:, b, t, :], ident[:])
                            last.then_inc(s["u_tr"], 1)

                        with pe.Fori(0, ST) as it:
                            for b in range(RING):
                                n = it * RING + b
                                wait_apart(pe, s["u_hz"], n + 1 + START)
                                for q, k in PARTS:
                                    turn(b, q, k)
                                wait_apart(pe, s["u_zread"], n - 1 + START)
                                for q, k in PARTS:
                                    wait_apart(pe, s["u_cp"], n * 4 + q + 1 + START)
                                    for t in range(4 * q, 4 * q + k):
                                        done = pe.matmul(psm[:, 2 * (b % 2) + t // 8, (t % 8) * 64:(t % 8) * 64 + H],
                                                         xT[:, t * P:(t + 1) * P], wz[:], start=True, stop=True)
                                done.then_inc(s["u_z"], 1)
            end_phase(nc, s)

        def qk_step():
            s = phase(nc, ["q_ld0", "q_ld1", "q_ld2", "q_ld3", "q_st0", "q_st1", "q_tr", "q_mm", "q_sq", "q_var", "q_root", "q_chain", "q_achain"],
                      ["q_done", "q_cp", "q_read"])
            ld, st = [s[f"q_ld{n}"] for n in range(RING)], [s["q_st0"], s["q_st1"]]

            products = [psm, psw]
            turned = [psm[0:2 * H, 3], psw[0:2 * H, 3]]
            FIVES = [(0, 5), (5, 5), (10, CH - 10)]
            PAIRS = [(0, 4), (4, CH // 2 - 4)]

            def prod(b, q):
                return products[b][:, q, 0:2 * H * FIVES[q][1]].rearrange("p (t c) -> p t c", c=2 * H)

            def h_rows(b):
                return hz[:, b].rearrange("p t c -> p (t c)")[:, 0:CH * H]

            def rows_T(b):
                return xT[:, b % 2 * (CH // 2 * P):(b % 2 + 1) * (CH // 2 * P)]
            with nc.Block() as block:
                @block.sync
                def _(sp):
                    def load(n, b):
                        sp.dma_start(h_rows(b).rearrange("p (t c) -> p t c", c=H), tiles(d_h)[:, bass.ds(n * CH, CH), :]).then_inc(ld[b], 16)
                    prime(sp, st)
                    for n in range(RING):
                        load(n, n)

                    def step(it, last):
                        for b in range(RING):
                            n = it * RING + b
                            if last:
                                sp.wait_ge(s["q_done"], n + 1 + START)
                            else:
                                wait_apart(sp, s["q_done"], n + 1 + START)
                            sp.dma_start(tiles(d_kh)[:, bass.ds(n * CH, CH), 0:H], bufC[:, b % 2]).then_inc(st[b % 2], 16)
                            if not last:
                                load(n + RING, b)
                    steps(sp, step, ST)
                    sp.wait_ge(st[0], IT * 16 + START)
                    sp.wait_ge(st[1], IT * 16 + START)

                @block.tensor
                def _(pe):
                    groups = [(t, 2) for t in range(0, CH, 2) if t // 5 == (t + 1) // 5]
                    groups += [(t, 1) for t in range(CH) if t // 5 != (t + 1 - t % 2 * 2) // 5]

                    def turn(b, rounds):
                        wait_apart(pe, ld[b], rounds)
                        for u in range(CH // 2):
                            last = pe.transpose(turned[u // 4][:, (u % 4) * P:(u % 4 + 1) * P], h_rows(b)[:, 2 * H * u:2 * H * (u + 1)], ident[:])
                        last.then_inc(s["q_tr"], 1)

                    def step(it, last):
                        for b in range(RING):
                            n = it * RING + b
                            wait_apart(pe, s["q_cp"], n + 1 + START)
                            if not last or b < RING - 1:
                                turn((b + 1) % RING, (it + (b + 1) // RING) * 16 + 16)
                            wait_apart(pe, s["q_read"], n - 1 + START)
                            for t, k in groups:
                                w = wqk[:, :, :].rearrange("p a c -> p (a c)") if k == 2 else wqk[:, t % 2, :]
                                done = pe.matmul(products[b % 2][:, t // 5, (t % 5) * 2 * H:(t % 5 + k) * 2 * H],
                                                 rows_T(b)[:, t // 2 * P:(t // 2 + 1) * P], w, start=True, stop=True)
                            done.then_inc(s["q_mm"], 1)
                    turn(0, 16)
                    steps(pe, step, ST)

                @block.scalar
                def _(act):
                    link = Chain(act, s["q_achain"])

                    def copy(n, b):
                        act.wait_ge(s["q_tr"], n + 1)
                        for q, (u, k) in enumerate(PAIRS):
                            link(act.copy(rows_T(b)[:, u * P:(u + k) * P], turned[q][:, 0:k * P]))
                        act.sem_inc(s["q_cp"], 1)

                    def step(it, last):
                        link.restart()
                        for b in range(2):
                            n = it * 2 + b
                            if not last or b == 0:
                                copy(n + 1, b + 1)
                            act.wait_ge(s["q_mm"], n + 1)
                            for q, (t, k) in enumerate(FIVES):
                                link(act.activation(tmp2[:, t:t + k, :], prod(b, q), ACT.Square))
                            act.sem_inc(s["q_sq"], 1)
                            act.wait_ge(s["q_var"], n + 1)
                            link(act.activation(col[:, 2 * CH:4 * CH], col[:, 0:2 * CH], ACT.Sqrt, bias=eps[:], scale=1.0 / H))
                            act.sem_inc(s["q_root"], 1)
                    link(act.activation(col[:, 60:61], eps[:], ACT.Sqrt))
                    copy(0, 0)
                    steps(act, step)

                @block.vector
                def _(v):
                    link = Chain(v, s["q_chain"])
                    root = col[:, 0:2 * CH].rearrange("p (t a) -> p t a", a=2)

                    def step(it, last):
                        link.restart()
                        for b in range(2):
                            n = it * 2 + b
                            v.wait_ge(s["q_sq"], n + 1)
                            link(v.tensor_reduce(col[:, 0:2 * CH], tmp2[:, :, :].rearrange("p t (a c) -> p (t a) c", a=2), AX.X, ALU.add))
                            v.sem_inc(s["q_var"], 1)
                            v.wait_ge(s["q_root"], n + 1)
                            link(v.reciprocal(col[:, 0:2 * CH], col[:, 2 * CH:4 * CH]))
                            link(v.tensor_tensor(root[:, :, 0], root[:, :, 0], is_end[:, bass.ds(n * CH, CH)], ALU.mult))
                            v.wait_ge(st[b], it * 16 + START)
                            for q, (t, k) in enumerate(FIVES):
                                v.tensor_tensor(G[:, bass.ds(n * CH + t, k), 0:H], prod(b, q)[:, :, 0:H], bc(root[:, t:t + k, 0], H), ALU.mult)
                                done = v.tensor_tensor(bufC[:, b, t:t + k], prod(b, q)[:, :, H:2 * H], bc(root[:, t:t + k, 1], H), ALU.mult)
                            link(done)
                            v.sem_inc(s["q_read"], 1)
                            v.sem_inc(s["q_done"], 1)
                    steps(v, step)
            end_phase(nc, s)

        def edge_step(table=None):
            s = phase(nc, ["e_ld0", "e_ld1", "e_g0", "e_g1", "e_ix0", "e_ix1", "e_chain"], ["e_done", "e_cp"])
            ld, g, ix = [s["e_ld0"], s["e_ld1"]], [s["e_g0"], s["e_g1"]], [s["e_ix0"], s["e_ix1"]]
            scored = table is None
            with nc.Block() as block:
                if scored:
                    @block.sync
                    def _(sp):
                        with sp.Fori(0, IT) as it:
                            for b in range(2):
                                n = it * 2 + b
                                wait_apart(sp, s["e_done"], n - 1 + START)
                                sp.dma_start(bufB[:, b, :, 0:RBF], tiles(d_edges)[:, bass.ds(n * CH, CH), 3:W1]).then_inc(ld[b], 16)

                @block.gpsimd
                def _(pool):
                    with pool.Fori(0, IT) as it:
                        for b in range(2):
                            n = it * 2 + b
                            pool.wait_ge(s["e_cp"], n - 1 + START)
                            pool.tensor_copy(idx[:, b], far_idx[:, bass.ds(n * CH, CH)]).then_inc(ix[b], 1)
                            wait_apart(pool, ix[b], it + 1)
                            for t in range(CH):
                                far = bass.IndirectOffsetOnAxis(ap=idx[:, b, t:t + 1], axis=0)
                                if scored:
                                    pool.indirect_dma_start(bufA[:, b, t, :], None, d_kh[:, :], far).then_inc(g[b], 16)
                                else:
                                    pool.indirect_dma_start(bufC[:, b, t, :], None, table[:, :], far).then_inc(g[b], 16)

                @block.scalar
                def _(act):
                    with act.Fori(0, IT) as it:
                        for b in range(2):
                            n = it * 2 + b
                            act.wait_ge(g[b], (it + 1) * (16 * CH))
                            if scored:
                                act.wait_ge(s["e_done"], n + 1 + START)
                            rows = bufA[:, b, :, H:2 * H] if scored else bufC[:, b]
                            act.copy(G[:, bass.ds(n * CH, CH), 0:H], rows).then_inc(s["e_cp"], 1)

                @block.vector
                def _(v):
                    link = Chain(v, s["e_chain"])
                    if not scored:
                        link(v.memset(G[:, :, H:HC], 0.0))
                        return
                    with v.Fori(0, IT) as it:
                        link.restart()
                        for b in range(2):
                            at = bass.ds((it * 2 + b) * CH, CH)
                            q_row, k_row = tmp[:, :, H:2 * H], bufA[:, b, :, 0:H]
                            link(v.tensor_tensor(q_row, G[:, at, 0:H], bcm(gb[:, 0, :]), ALU.mult))
                            link(v.tensor_tensor(q_row, q_row, bcm(gb[:, 2, :]), ALU.add))
                            v.wait_ge(g[b], (it + 1) * (16 * CH))
                            link(v.tensor_tensor(k_row, k_row, bcm(gb[:, 1, :]), ALU.mult))
                            link(v.tensor_tensor(k_row, k_row, bcm(gb[:, 3, :]), ALU.add))
                            v.wait_ge(ld[b], it * 16 + 16)
                            link(v.scalar_tensor_tensor(bufA[:, b, :, 0:RBF], bufB[:, b, :, 0:RBF], 0.1, bufA[:, b, :, 0:RBF], ALU.mult, ALU.add))
                            link(v.tensor_tensor(tmp[:, :, 0:H], k_row, q_row, ALU.mult))
                            link(v.tensor_reduce(score[:, at], tmp[:, :, 0:H], AX.X, ALU.add))
                            v.sem_inc(s["e_done"], 1)
            end_phase(nc, s)

        def load_rows(pairs, zrows=None):
            s = phase(nc, ["w_ld"])
            with nc.Block() as block:
                @block.sync
                def _(sp):
                    for n, src in pairs:
                        sp.dma_start(gb[:, n, :], src.partition_broadcast(P)).then_inc(s["w_ld"], 16)
                    for n, src in enumerate(zrows or []):
                        sp.dma_start(wz[n * H:(n + 1) * H, :], src).then_inc(s["w_ld"], 16)
                    sp.wait_ge(s["w_ld"], 16 * (len(pairs) + len(zrows or [])))
            end_phase(nc, s)

        def layer_weights(i):
            s = phase(nc, ["l_ld", "l_ch", "l_pe", "l_dve", "l_z"])

            def of(name):
                return a[name][bass.ds(i, 1)].rearrange("a k n -> (a k) n")

            def vec(name):
                return a[name][bass.ds(i, 1), :].rearrange("a n -> (a n)")
            with nc.Block() as block:
                @block.sync
                def _(sp):
                    for half in (slice(0, H), slice(H, 2 * H)):
                        sp.dma_start(wtmp[half, 0, :], of("Wq")).then_inc(s["l_ld"], 16)
                        sp.dma_start(wtmp[half, 1, :], of("Wk")).then_inc(s["l_ld"], 16)
                    sp.dma_start(wtmp[0:H, 2, :], of("Wm")).then_inc(s["l_ld"], 16)
                    sp.dma_start(wz[0:H, :], of("Wu")[0:H, :]).then_inc(s["l_ld"], 16)
                    sp.dma_start(wtmp[0:H, 3, :], of("Wu")[H:2 * H, :]).then_inc(s["l_ld"], 16)
                    for n, name in enumerate(("gq", "gk", "bq", "bk", "go", "bo")):
                        sp.dma_start(gb[:, n, :], vec(name).partition_broadcast(P)).then_inc(s["l_ld"], 16)
                    sp.wait_ge(s["l_dve"], 2)
                    sp.dma_start(wz[H:2 * H, :], xT[0:H, H:2 * H]).then_inc(s["l_z"], 16)
                    sp.wait_ge(s["l_z"], 16)

                @block.vector
                def _(v):
                    link = Chain(v, s["l_ch"])
                    v.wait_ge(s["l_ld"], 13 * 16)
                    link(v.tensor_reduce(col[0:2 * H, 0:2], wtmp[:, 0:2, :], AX.X, ALU.add))
                    link(v.tensor_scalar(col[0:2 * H, 0:2], col[0:2 * H, 0:2], -1.0 / H, None, ALU.mult))
                    link(v.tensor_copy(col[0:2 * H, 2:3], before[0:2 * H, H:H + 1]))
                    link(v.tensor_scalar(col[0:2 * H, 3:4], before[0:2 * H, H:H + 1], -1.0, 1.0, ALU.mult, ALU.add))
                    for tile in range(2):
                        for n in range(2):
                            link(v.tensor_scalar(wqk[:, tile, n * H:(n + 1) * H], wtmp[:, n, :], col[0:2 * H, n:n + 1],
                                                 col[0:2 * H, 2 + tile:3 + tile], ALU.add, ALU.mult))
                    v.wait_ge(s["l_pe"], 1)
                    v.tensor_copy(xT[0:H, 0:H], ps[0][0:H, 0:H]).then_inc(s["l_dve"], 1)
                    v.wait_ge(s["l_pe"], 2)
                    v.tensor_copy(xT[0:H, H:2 * H], ps[1][0:H, 0:H]).then_inc(s["l_dve"], 1)

                @block.tensor
                def _(pe):
                    pe.wait_ge(s["l_ld"], 13 * 16)
                    pe.transpose(ps[0][0:H, 0:H], wtmp[0:H, 2, :], ident[0:H, 0:H]).then_inc(s["l_pe"], 1)
                    pe.wait_ge(s["l_dve"], 1)
                    pe.matmul(ps[1][0:H, 0:H], xT[0:H, 0:H], wtmp[0:H, 3, :], start=True, stop=True).then_inc(s["l_pe"], 1)
            end_phase(nc, s)

        histogram(a["src"])
        rank_pass(True, False, pay, None, d_half, 0)
        rank_pass(False, True, pay, d_half, d_edges, 0)
        take_order(d_edges, W1)
        make_slots()
        node_rows()
        element_slots()
        segment_scan(GE, back=True)
        first_messages()
        segment_scan(HC)
        load_rows([(0, a["gn"]), (1, a["bn"])])
        node_step("first", d_slot, d_h, gain=0)
        with nc.Fori(0, LAYERS) as layer:
            layer_weights(layer)
            qk_step()
            segment_scan(H, back=True)
            edge_step()
            softmax_weights()
            segment_scan(HC)
            node_step("layer", d_h, d_h, gain=4)
        node_step("join", d_slot, d_x1, table_add=d_h)
        rank_pass(True, False, pay2, None, d_half2, 1)
        rank_pass(False, True, pay2, d_half2, d_pairs, 1)
        take_order(d_pairs, 2)
        edge_step(d_x1)
        segment_scan(HC, store=True)
        load_rows([(7, a["b1"])], [a["w_root1"], a["w_rel1"]])
        node_step("conv", d_x1, d_y1)
        edge_step(d_y1)
        segment_scan(HC, store=True)
        load_rows([(7, a["b2"])], [a["w_root2"], a["w_rel2"]])
        node_step("last", d_y1, out, table_add=d_x1)


def kernel(**inputs):
    import numpy as np
    import concourse.bacc as bacc
    from concourse.bass_utils import run_bass_kernel_spmd

    def arr(name):
        return np.ascontiguousarray(inputs[name])

    def padded(v):
        return np.pad(v, [(0, NP - N)] + [(0, 0)] * (v.ndim - 1))
    ends = np.arange(N, NP, dtype=np.int32)
    src = np.concatenate([arr("src"), ends])
    dst = np.concatenate([arr("dst"), ends])
    arrays = {
        "x": padded(arr("x")), "src": src, "dst": dst, "pairs": np.stack([src, dst], 1),
        "efeat": np.concatenate([padded(arr("edge_weight"))[:, None], padded(arr("edge_attr_40"))], 1),
        "ntype": padded(arr("node_type_119")), "nvec": padded(arr("node_vec")),
    }
    for n in ("Wq", "gq", "bq", "Wk", "gk", "bk", "Wm", "Wu", "go", "bo", "F1W", "F1b", "F2W", "F2b", "gn", "bn", "emb", "adapt"):
        arrays[n] = arr("L0_gnn_" + n)
    for n in ("w_rel1", "w_root1", "b1", "w_rel2", "w_root2", "b2"):
        arrays[n] = arr("L1_gnn_" + n)
    nc = bacc.Bacc("TRN2", target_bir_lowering=False, num_devices=1)
    a = {n: nc.dram_tensor(f"in_{n}", v.shape, mybir.dt.from_np(v.dtype), kind="ExternalInput").ap() for n, v in arrays.items()}
    out = nc.dram_tensor("out", (NP, H), F32, kind="ExternalOutput").ap()
    gnn_kernel(nc, a, out)
    r = run_bass_kernel_spmd(nc, [{f"in_{n}": v for n, v in arrays.items()}], core_ids=[0])
    return r.results[0]["out"][:N]
```
